# Optimizing a Trainium2 kernel written in Bass

```python
import numpy as np
import jax
import jax.numpy as jnp

def _softmax(x, axis=-1):
    return jax.nn.softmax(x, axis=axis)

def _gelu(x):
    return jax.nn.gelu(x, approximate=True)

def _silu(x):
    return jax.nn.silu(x)

def _sigmoid(x):
    return jax.nn.sigmoid(x)

def _layernorm(x, axis=-1, eps=1e-05):
    m = jnp.mean(x, axis=axis, keepdims=True)
    v = jnp.var(x, axis=axis, keepdims=True)
    return (x - m) / jnp.sqrt(v + eps)

def _scatter_add(tgt, idx, src, axis=0):
    return tgt.at[idx].add(src)

def _segment_sum(src, seg, n):
    return jax.ops.segment_sum(src, seg, n)
kernel_name = 'mk_audio_tower_d2_tok_audfeat768_r4_dc8526'

def setup_inputs(seed: int=0):
    np.random.seed(seed)
    _w = jnp.asarray

    def _rec_inputs():
        import jax
        import jax.numpy as jnp
        _rk = jax.random.key(seed)
        x = -0.000183583 + 0.999963 * jax.random.normal(jax.random.fold_in(_rk, 1), (16, 750, 192), jnp.float32)
        return x
    x = _rec_inputs()

    def _L0_tok_setup():
        import jax, jax.numpy as jnp
        import numpy as np
        KEEP_RATIO = 0.7
        LN_EPS = 1e-05
        key = jax.random.key(seed)
        k1, k2 = jax.random.split(key)
        B, N, D = (16, 2048, 192)
        x = jax.random.normal(k1, (B, N, D), dtype=jnp.float32)
        gamma = jnp.ones((D,), dtype=jnp.float32)
        beta = jnp.zeros((D,), dtype=jnp.float32)
        w = jax.random.normal(k2, (D,), dtype=jnp.float32) * (1.0 / np.sqrt(D))
        b = jnp.zeros((1,), dtype=jnp.float32)
        return {'x': x, 'gamma': gamma, 'beta': beta, 'w': w, 'b': b}
    _L0_tok_all = _L0_tok_setup()
    _L0_tok_in = {k: v for k, v in _L0_tok_all.items() if k in ('gamma', 'beta', 'w', 'b')}
    del _L0_tok_all

    def _L0_attn_setup():
        import jax, jax.numpy as jnp
        import numpy as np
        D_MODEL = 192
        D_STATE = 16
        BATCH = 2
        SEQLEN = 512
        key = jax.random.key(seed)
        ks = jax.random.split(key, 8)
        s = 0.02
        return {'x': jax.random.normal(ks[0], (BATCH, SEQLEN, D_MODEL), dtype=jnp.float32), 'log_lambda': jax.random.uniform(ks[1], (D_MODEL, D_STATE), dtype=jnp.float32), 'Wd': jax.random.normal(ks[2], (D_MODEL, D_MODEL), dtype=jnp.float32) * s, 'bd': jax.random.normal(ks[3], (D_MODEL,), dtype=jnp.float32) * s, 'WB': jax.random.normal(ks[4], (D_STATE, D_MODEL), dtype=jnp.float32) * s, 'WC': jax.random.normal(ks[5], (D_STATE, D_MODEL), dtype=jnp.float32) * s, 'Wout': jax.random.normal(ks[6], (D_MODEL, D_MODEL * D_STATE), dtype=jnp.float32) * s, 'bout': jax.random.normal(ks[7], (D_MODEL,), dtype=jnp.float32) * s}
    _L0_attn_all = _L0_attn_setup()
    _L0_attn_in = {k: v for k, v in _L0_attn_all.items() if k in ('log_lambda', 'Wd', 'bd', 'WB', 'WC', 'Wout', 'bout')}
    del _L0_attn_all

    def _L0_ffn_setup():
        import jax, jax.numpy as jnp
        import numpy as np
        DIM = 192
        HID = 128
        E = 16
        G = 8
        TOPK_G = 4
        TOPK_E = 4
        SCALE = 2.5
        B, S = (2, 512)
        key = jax.random.key(seed)
        ks = jax.random.split(key, 9)
        init = lambda k, shape: jax.random.normal(k, shape, dtype=jnp.float32) * 0.02
        z = lambda shape: jnp.zeros(shape, jnp.float32)
        return {'x': jax.random.normal(ks[0], (B, S, DIM), dtype=jnp.float32), 'gate_w': init(ks[1], (DIM, E)), 'gate_b': z((E,)), 'bias': z((E,)), 'Wu': init(ks[2], (E, DIM, HID)), 'bu': z((E, HID)), 'Wg': init(ks[3], (E, DIM, HID)), 'bg': z((E, HID)), 'Wd': init(ks[4], (E, HID, DIM)), 'bd': z((E, DIM)), 'sWu': init(ks[5], (DIM, HID)), 'sbu': z((HID,)), 'sWg': init(ks[6], (DIM, HID)), 'sbg': z((HID,)), 'sWd': init(ks[7], (HID, DIM)), 'sbd': z((DIM,))}
    _L0_ffn_all = _L0_ffn_setup()
    _L0_ffn_in = {k: v for k, v in _L0_ffn_all.items() if k in ('gate_w', 'gate_b', 'bias', 'Wu', 'bu', 'Wg', 'bg', 'Wd', 'bd', 'sWu', 'sbu', 'sWg', 'sbg', 'sWd', 'sbd')}
    del _L0_ffn_all

    def _L1_attn_setup():
        import jax, jax.numpy as jnp
        import numpy as np
        NUM_HEADS = 12
        N_BITS = 8

        def fake_quant(x, n_bits=N_BITS):
            qmax = 2 ** (n_bits - 1) - 1
            scale = jnp.maximum(jnp.max(jnp.abs(x)) / qmax, 1e-08)
            q = jnp.clip(jnp.round(x / scale), -qmax - 1, qmax) * scale
            return x + jax.lax.stop_gradient(q - x)
        key = jax.random.key(seed)
        ks = jax.random.split(key, 5)
        B, N, C = (8, 256, 192)
        return {'x': jax.random.normal(ks[0], (B, N, C), dtype=jnp.float32), 'w_qkv': jax.random.normal(ks[1], (3 * C, C), dtype=jnp.float32) * 0.02, 'b_qkv': jax.random.normal(ks[2], (3 * C,), dtype=jnp.float32) * 0.02, 'w_proj': jax.random.normal(ks[3], (C, C), dtype=jnp.float32) * 0.02, 'b_proj': jax.random.normal(ks[4], (C,), dtype=jnp.float32) * 0.02}
    _L1_attn_all = _L1_attn_setup()
    _L1_attn_in = {k: v for k, v in _L1_attn_all.items() if k in ('w_qkv', 'b_qkv', 'w_proj', 'b_proj')}
    del _L1_attn_all

    def _L1_ffn_setup():
        import jax, jax.numpy as jnp
        import numpy as np
        B, S, D, F, E = (8, 512, 192, 768, 16)
        CAP = 64
        EPS = 1e-06

        def _switch_moe_block(x, ln_w, w_router, wi, wo):
            var = jnp.mean(jnp.square(x.astype(jnp.float32)), axis=-1, keepdims=True)
            normed = (x * jax.lax.rsqrt(var + EPS)).astype(x.dtype) * ln_w
            logits = jnp.einsum('bsd,de->bse', normed.astype(jnp.float32), w_router.astype(jnp.float32))
            probs = jax.nn.softmax(logits, axis=-1)
            expert_idx = jnp.argmax(probs, axis=-1)
            onehot = jax.nn.one_hot(expert_idx, E, dtype=jnp.float32)
            priority = jnp.cumsum(onehot, axis=1)
            keep = onehot * (priority <= CAP)
            pos = (priority - 1.0).astype(jnp.int32)
            dispatch = keep[..., None] * jax.nn.one_hot(pos, CAP, dtype=jnp.float32)
            expert_in = jnp.einsum('bsec,bsd->becd', dispatch, normed)
            h = jax.nn.relu(jnp.einsum('becd,edf->becf', expert_in, wi))
            expert_out = jnp.einsum('becf,efd->becd', h, wo)
            combined = jnp.einsum('bsec,becd->bsd', dispatch, expert_out)
            routed = jnp.sum(dispatch, axis=(2, 3)) > 0
            next_states = jnp.where(routed[..., None], combined.astype(x.dtype), normed)
            router_prob = jnp.max(probs, axis=-1, keepdims=True).astype(x.dtype)
            return x + router_prob * next_states
        key = jax.random.key(seed)
        k_x, k_r, k_wi, k_wo = jax.random.split(key, 4)
        x = jax.random.normal(k_x, (B, S, D), dtype=jnp.float32)
        ln_w = jnp.ones((D,), dtype=jnp.float32)
        w_router = jax.random.normal(k_r, (D, E), dtype=jnp.float32) * 0.02
        wi = jax.random.normal(k_wi, (E, D, F), dtype=jnp.float32) * D ** (-0.5)
        wo = jax.random.normal(k_wo, (E, F, D), dtype=jnp.float32) * F ** (-0.5)
        return {'x': x, 'ln_w': ln_w, 'w_router': w_router, 'wi': wi, 'wo': wo}
    _L1_ffn_all = _L1_ffn_setup()
    _L1_ffn_in = {k: v for k, v in _L1_ffn_all.items() if k in ('ln_w', 'w_router', 'wi', 'wo')}
    del _L1_ffn_all
    return {'x': x, 'L0_tok_gamma': _L0_tok_in['gamma'], 'L0_tok_beta': _L0_tok_in['beta'], 'L0_tok_w': _L0_tok_in['w'], 'L0_tok_b': _L0_tok_in['b'], 'L0_attn_log_lambda': _L0_attn_in['log_lambda'], 'L0_attn_Wd': _L0_attn_in['Wd'], 'L0_attn_bd': _L0_attn_in['bd'], 'L0_attn_WB': _L0_attn_in['WB'], 'L0_attn_WC': _L0_attn_in['WC'], 'L0_attn_Wout': _L0_attn_in['Wout'], 'L0_attn_bout': _L0_attn_in['bout'], 'L0_ffn_gate_w': _L0_ffn_in['gate_w'], 'L0_ffn_gate_b': _L0_ffn_in['gate_b'], 'L0_ffn_bias': _L0_ffn_in['bias'], 'L0_ffn_Wu': _L0_ffn_in['Wu'], 'L0_ffn_bu': _L0_ffn_in['bu'], 'L0_ffn_Wg': _L0_ffn_in['Wg'], 'L0_ffn_bg': _L0_ffn_in['bg'], 'L0_ffn_Wd': _L0_ffn_in['Wd'], 'L0_ffn_bd': _L0_ffn_in['bd'], 'L0_ffn_sWu': _L0_ffn_in['sWu'], 'L0_ffn_sbu': _L0_ffn_in['sbu'], 'L0_ffn_sWg': _L0_ffn_in['sWg'], 'L0_ffn_sbg': _L0_ffn_in['sbg'], 'L0_ffn_sWd': _L0_ffn_in['sWd'], 'L0_ffn_sbd': _L0_ffn_in['sbd'], 'L1_attn_w_qkv': _L1_attn_in['w_qkv'], 'L1_attn_b_qkv': _L1_attn_in['b_qkv'], 'L1_attn_w_proj': _L1_attn_in['w_proj'], 'L1_attn_b_proj': _L1_attn_in['b_proj'], 'L1_ffn_ln_w': _L1_ffn_in['ln_w'], 'L1_ffn_w_router': _L1_ffn_in['w_router'], 'L1_ffn_wi': _L1_ffn_in['wi'], 'L1_ffn_wo': _L1_ffn_in['wo']}

def reference(x, L0_tok_gamma, L0_tok_beta, L0_tok_w, L0_tok_b, L0_attn_log_lambda, L0_attn_Wd, L0_attn_bd, L0_attn_WB, L0_attn_WC, L0_attn_Wout, L0_attn_bout, L0_ffn_gate_w, L0_ffn_gate_b, L0_ffn_bias, L0_ffn_Wu, L0_ffn_bu, L0_ffn_Wg, L0_ffn_bg, L0_ffn_Wd, L0_ffn_bd, L0_ffn_sWu, L0_ffn_sbu, L0_ffn_sWg, L0_ffn_sbg, L0_ffn_sWd, L0_ffn_sbd, L1_attn_w_qkv, L1_attn_b_qkv, L1_attn_w_proj, L1_attn_b_proj, L1_ffn_ln_w, L1_ffn_w_router, L1_ffn_wi, L1_ffn_wo):
    import jax
    import jax.numpy as jnp

    def _L0_tok_ref(x, gamma, beta, w, b):
        import jax, jax.numpy as jnp
        import numpy as np
        KEEP_RATIO = 0.7
        LN_EPS = 1e-05
        B, N, D = x.shape
        mu = jnp.mean(x, axis=-1, keepdims=True)
        var = jnp.mean(jnp.square(x - mu), axis=-1, keepdims=True)
        xn = (x - mu) * jax.lax.rsqrt(var + LN_EPS) * gamma + beta
        scores = jnp.einsum('bnd,d->bn', xn, w) + b[0]
        k = int(N * KEEP_RATIO)
        _, idx = jax.lax.top_k(scores, k)
        x_kept = jnp.take_along_axis(x, idx[..., None], axis=1)
        return x_kept

    def _L0_attn_ref(x, log_lambda, Wd, bd, WB, WC, Wout, bout):
        import jax, jax.numpy as jnp
        import numpy as np
        D_MODEL = 192
        D_STATE = 16
        BATCH = 2
        SEQLEN = 512
        B, L, D = x.shape
        N = log_lambda.shape[1]
        lam = jax.nn.softplus(log_lambda)
        delta = jax.nn.softplus(jnp.einsum('bld,ed->ble', x, Wd) + bd)
        Bt = jnp.einsum('bld,nd->bln', x, WB)
        Ct = jnp.einsum('bld,nd->bln', x, WC)
        A_d = jnp.exp(-delta[..., None] * lam)
        B_d = delta[..., None] * Bt[:, :, None, :]

        def step(h, inp):
            a, b, c = inp
            h = a * h + b
            y = h * c[:, None, :]
            return (h, y)
        h0 = jnp.zeros((B, D, N), dtype=x.dtype)
        xs = (jnp.swapaxes(A_d, 0, 1), jnp.swapaxes(B_d, 0, 1), jnp.swapaxes(Ct, 0, 1))
        _, ys = jax.lax.scan(step, h0, xs)
        flat = jnp.swapaxes(ys, 0, 1).reshape(B, L, D * N)
        out = jnp.einsum('blk,dk->bld', flat, Wout) + bout
        return out

    def _L0_ffn_ref(x, gate_w, gate_b, bias, Wu, bu, Wg, bg, Wd, bd, sWu, sbu, sWg, sbg, sWd, sbd):
        import jax, jax.numpy as jnp
        import numpy as np
        DIM = 192
        HID = 128
        E = 16
        G = 8
        TOPK_G = 4
        TOPK_E = 4
        SCALE = 2.5
        B, S = (2, 512)
        orig_shape = x.shape
        xt = x.reshape(-1, DIM)
        T = xt.shape[0]
        scores = jax.nn.softmax(xt @ gate_w + gate_b, axis=-1)
        orig_scores = jax.lax.stop_gradient(scores)
        s = scores + bias[None, :]
        s3 = s.reshape(T, G, E // G)
        group_scores = jax.lax.top_k(s3, 2)[0].sum(-1)
        gidx = jax.lax.top_k(group_scores, TOPK_G)[1]
        gmask = jnp.any(jnp.arange(G)[None, None, :] == gidx[:, :, None], axis=1)
        s_masked = jnp.where(gmask[:, :, None], s3, -jnp.inf).reshape(T, E)
        _, idx = jax.lax.top_k(s_masked, TOPK_E)
        w = jnp.take_along_axis(orig_scores, idx, axis=1) * SCALE
        w_full = jnp.zeros((T, E), xt.dtype).at[jnp.arange(T)[:, None], idx].add(w)
        up = jax.nn.silu(jnp.einsum('td,edh->teh', xt, Wu) + bu)
        gt = jnp.einsum('td,edh->teh', xt, Wg) + bg
        act = up * gt * w_full[:, :, None]
        y = jnp.einsum('teh,ehd->td', act, Wd) + w_full @ bd
        sh = jax.nn.silu(xt @ sWu + sbu) * (xt @ sWg + sbg)
        y = y + sh @ sWd + sbd
        return y.reshape(orig_shape)

    def _L1_attn_ref(x, w_qkv, b_qkv, w_proj, b_proj):
        import jax, jax.numpy as jnp
        import numpy as np
        NUM_HEADS = 12
        N_BITS = 8

        def fake_quant(x, n_bits=N_BITS):
            qmax = 2 ** (n_bits - 1) - 1
            scale = jnp.maximum(jnp.max(jnp.abs(x)) / qmax, 1e-08)
            q = jnp.clip(jnp.round(x / scale), -qmax - 1, qmax) * scale
            return x + jax.lax.stop_gradient(q - x)
        B, N, C = x.shape
        H = NUM_HEADS
        hd = C // H
        scale = hd ** (-0.5)
        qkv = jnp.einsum('bnc,oc->bno', fake_quant(x), fake_quant(w_qkv)) + b_qkv
        qkv = qkv.reshape(B, N, 3, H, hd).transpose(2, 0, 3, 1, 4)
        q, k, v = (qkv[0], qkv[1], qkv[2])
        attn = jnp.einsum('bhnd,bhmd->bhnm', fake_quant(q), fake_quant(k)) * scale
        attn = jax.nn.softmax(attn, axis=-1)
        out = jnp.einsum('bhnm,bhmd->bhnd', fake_quant(attn), fake_quant(v))
        out = out.transpose(0, 2, 1, 3).reshape(B, N, C)
        out = jnp.einsum('bnc,oc->bno', fake_quant(out), fake_quant(w_proj)) + b_proj
        return out

    def _L1_ffn_ref(x, ln_w, w_router, wi, wo):
        import jax, jax.numpy as jnp
        import numpy as np
        B, S, D, F, E = (8, 512, 192, 768, 16)
        CAP = 64
        EPS = 1e-06

        def _switch_moe_block(x, ln_w, w_router, wi, wo):
            var = jnp.mean(jnp.square(x.astype(jnp.float32)), axis=-1, keepdims=True)
            normed = (x * jax.lax.rsqrt(var + EPS)).astype(x.dtype) * ln_w
            logits = jnp.einsum('bsd,de->bse', normed.astype(jnp.float32), w_router.astype(jnp.float32))
            probs = jax.nn.softmax(logits, axis=-1)
            expert_idx = jnp.argmax(probs, axis=-1)
            onehot = jax.nn.one_hot(expert_idx, E, dtype=jnp.float32)
            priority = jnp.cumsum(onehot, axis=1)
            keep = onehot * (priority <= CAP)
            pos = (priority - 1.0).astype(jnp.int32)
            dispatch = keep[..., None] * jax.nn.one_hot(pos, CAP, dtype=jnp.float32)
            expert_in = jnp.einsum('bsec,bsd->becd', dispatch, normed)
            h = jax.nn.relu(jnp.einsum('becd,edf->becf', expert_in, wi))
            expert_out = jnp.einsum('becf,efd->becd', h, wo)
            combined = jnp.einsum('bsec,becd->bsd', dispatch, expert_out)
            routed = jnp.sum(dispatch, axis=(2, 3)) > 0
            next_states = jnp.where(routed[..., None], combined.astype(x.dtype), normed)
            router_prob = jnp.max(probs, axis=-1, keepdims=True).astype(x.dtype)
            return x + router_prob * next_states
        return _switch_moe_block(x, ln_w, w_router, wi, wo)
    h = _L0_tok_ref(x, L0_tok_gamma, L0_tok_beta, L0_tok_w, L0_tok_b)
    h = h + _L0_attn_ref(_layernorm(h, axis=-1), L0_attn_log_lambda, L0_attn_Wd, L0_attn_bd, L0_attn_WB, L0_attn_WC, L0_attn_Wout, L0_attn_bout)
    h = h + _L0_ffn_ref(_layernorm(h, axis=-1), L0_ffn_gate_w, L0_ffn_gate_b, L0_ffn_bias, L0_ffn_Wu, L0_ffn_bu, L0_ffn_Wg, L0_ffn_bg, L0_ffn_Wd, L0_ffn_bd, L0_ffn_sWu, L0_ffn_sbu, L0_ffn_sWg, L0_ffn_sbg, L0_ffn_sWd, L0_ffn_sbd)
    h = h + _L1_attn_ref(_layernorm(h, axis=-1), L1_attn_w_qkv, L1_attn_b_qkv, L1_attn_w_proj, L1_attn_b_proj)
    h = h + _L1_ffn_ref(_layernorm(h, axis=-1), L1_ffn_ln_w, L1_ffn_w_router, L1_ffn_wi, L1_ffn_wo)
    return h

_drawn_inputs = setup_inputs


def setup_inputs(seed=0):
    import zlib

    import numpy as np

    out = dict(_drawn_inputs(seed))
    spreads = {'L0_tok_gamma': (1.0, 0.2),
     'L0_tok_beta': (0.0, 0.1),
     'L0_ffn_gate_b': (0.0, 0.539),
     'L0_ffn_bias': (0.0, 0.1),
     'L0_ffn_bu': (0.0, 0.8),
     'L0_ffn_bg': (0.0, 0.8),
     'L0_ffn_bd': (0.0, 0.507),
     'L0_ffn_sbu': (0.0, 0.8),
     'L0_ffn_sbg': (0.0, 0.8),
     'L0_ffn_sbd': (0.0, 0.4),
     'L1_ffn_ln_w': (1.0, 0.6)}
    factors = {'L0_attn_log_lambda': 7.447,
     'L0_attn_Wd': 3.608,
     'L0_attn_bd': 8.0,
     'L0_ffn_gate_w': 2.948,
     'L0_ffn_Wu': 8.0,
     'L0_ffn_Wg': 8.0,
     'L0_ffn_Wd': 8.0,
     'L0_ffn_sWu': 5.676,
     'L0_ffn_sWg': 5.637,
     'L0_ffn_sWd': 5.281,
     'L1_attn_w_qkv': 5.118,
     'L1_attn_b_qkv': 8.0,
     'L1_attn_w_proj': 4.527,
     'L1_attn_b_proj': 16.203,
     'L1_ffn_w_router': 3.406,
     'L1_ffn_wi': 4.107,
     'L1_ffn_wo': 3.433}
    for name, (base, spread) in spreads.items():
        noise = np.random.default_rng([zlib.crc32(name.encode()), seed]).standard_normal(out[name].shape)
        drawn = base * np.exp(spread * noise) if base else spread * noise
        out[name] = jnp.asarray(drawn.astype(out[name].dtype))
    for name, factor in factors.items():
        out[name] = (out[name] * factor).astype(out[name].dtype)
    return out
```

```python
from contextlib import ExitStack

import concourse.bass as bass
from concourse import mybir

F32 = mybir.dt.float32
BF16 = mybir.dt.bfloat16
I32 = mybir.dt.int32
U32 = mybir.dt.uint32
ALU = mybir.AluOpType
ACT = mybir.ActivationFunctionType
AX = mybir.AxisListType.X

NB, N_IN, D = 16, 750, 192
S = 525
T = NB * S
TP, TT = 105, 5
KC, KT = 96, 2


def semaphores(nc, ctx, prefix):
    mine = []

    def sem(name):
        mine.append(nc.alloc_semaphore(prefix + name))
        return mine[-1]

    def clear():
        nc.clear_and_free_semaphores(mine)
        nc.all_engine_barrier()

    ctx.callback(clear)
    return sem


class Steps:

    def __init__(self, eng, sem, per=0, turn=0):
        self.eng, self.sem, self.base, self.n, self.per = eng, sem, turn * per, 0, per

    def after(self, ins):
        ins.then_inc(self.sem, 1)
        self.n += 1
        self.eng.wait_ge(self.sem, self.base + self.n)

    def counted(self, ins):
        ins.then_inc(self.sem, 1)
        self.n += 1

    def wait(self, back=0):
        if self.n > back:
            self.eng.wait_ge(self.sem, self.base + (self.n - back))

    def end(self):
        assert self.n == self.per, (self.n, self.per)


RSQRT_STEPS = 11


def rsqrt(nc, st, y, v, h):
    st.after(nc.vector.tensor_scalar(h.bitcast(I32), v.bitcast(I32), 1, None, ALU.logical_shift_right))
    st.after(nc.vector.tensor_scalar(y.bitcast(I32), h.bitcast(I32), -1.0, float(0x5F3759DF), ALU.mult, ALU.add))
    for _ in range(3):
        st.after(nc.vector.tensor_tensor(h, y, y, ALU.mult))
        st.after(nc.vector.scalar_tensor_tensor(h, h, -0.5, v, ALU.mult, ALU.mult))
        st.after(nc.vector.scalar_tensor_tensor(y, h, 1.5, y, ALU.add, ALU.mult))


def token_selection(nc, x, gamma, beta, w, b0, score_d, h0):
    P, G = 125, N_IN // 125
    PER = 2 + 1 + RSQRT_STEPS + 3 + (2 * G - 1) + 3
    with ExitStack() as ctx:
        sb = lambda name, shape, dt=F32: ctx.enter_context(nc.sbuf_tensor("a_" + name, shape, dt))
        sem = semaphores(nc, ctx, "a_")
        xt = sb("xt", [P, 2, G * D])
        prod = sb("prod", [P, G * D])
        gam, bet, wr, bb = sb("gam", [P, D]), sb("bet", [P, D]), sb("wr", [P, D]), sb("bb", [P, 1])
        gw, bw, sgw, cst = sb("gw", [P, D]), sb("bw", [P, D]), sb("sgw", [P, 1]), sb("cst", [P, 1])
        stats, mv = sb("stats", [P, G, 6]), sb("mv", [P, G, 2])
        dot, ve, rs, hh, sc = (sb(n, [P, G]) for n in ("dot", "ve", "rs", "hh", "sc"))
        srow = sb("srow", [P, 2, N_IN])
        earlier = sb("earlier", [P, G, N_IN], BF16)
        junk = sb("junk", [P, 4, N_IN], BF16)
        above, ties = sb("above", [P, G]), sb("ties", [P, G])
        rank, over, base = sb("rank", [P, G]), sb("over", [P, G]), sb("base", [P, 1])
        dest = sb("dest", [P, 2, G], U32)

        s_const = sem("s_const")
        s_mask0, s_mask = sem("s_mask0"), sem("s_mask")
        s_x = [sem(f"s_x{k}") for k in range(2)]
        s_score, s_scored = sem("s_score"), sem("s_scored")
        s_row = [sem(f"s_row{k}") for k in range(2)]
        s_ranked = sem("s_ranked")
        s_dest = sem("s_dest")
        s_kept = [sem(f"s_kept{k}") for k in range(2)]
        s_v = sem("s_v")
        s_go = sem("s_go")
        s_pre = sem("s_pre")

        block = ctx.enter_context(nc.Block())

        @block.sync
        def _(sp):
            for dst, src in ((gam, gamma), (bet, beta), (wr, w)):
                sp.dma_start(dst[:, :], src.rearrange("(a d) -> a d", a=1).broadcast_to([P, D])).then_inc(s_const, 16)
            sp.dma_start(bb[:, :], b0.rearrange("(a d) -> a d", a=1).broadcast_to([P, 1])).then_inc(s_const, 16)
            with sp.Fori(0, NB // 2) as i:
                for k in range(2):
                    sp.wait_ge(s_kept[k], i * (16 * G))
                    sp.dma_start(xt[:, k, :], x[i * 2 + k].rearrange("(p g) d -> p (g d)", p=P)).then_inc(s_x[k], 16)

        @block.scalar
        def _(act):
            with act.Fori(0, NB // 2) as i:
                for k in range(2):
                    act.wait_ge(s_score, i * 2 + (k + 1))
                    act.dma_start(score_d[i * 2 + k].rearrange("(p g) -> p g", p=P), sc[:, :]).then_inc(s_scored, 16)
                    act.wait_ge(s_scored, i * 32 + 16 * (k + 1))
                    act.wait_ge(s_ranked, i * 2)
                    act.dma_start(srow[:, k, :],
                                  score_d[i * 2 + k].rearrange("(a n) -> a n", a=1).broadcast_to([P, N_IN])).then_inc(s_row[k], 16)

        @block.gpsimd
        def _(pool):
            pool.memset(earlier[:, :, :], 1.0).then_inc(s_mask0, 1)
            pool.wait_ge(s_mask0, 1)
            pool.affine_select(out=earlier[:, :, :], in_=earlier[:, :, :], compare_op=ALU.is_gt, fill=0.0,
                               base=0, pattern=[[1, G], [-1, N_IN]], channel_multiplier=G).then_inc(s_mask, 1)
            last_row = pool.to_reg(T - 1)
            with pool.Fori(0, NB // 2) as i:
                for k in range(2):
                    pool.wait_ge(s_dest, i * 2 + (k + 1))
                    pool.sem_inc(s_go, 1)
                    for g in range(G):
                        pool.indirect_dma_start(h0, bass.IndirectOffsetOnAxis(ap=dest[:, k, g:g + 1], axis=0),
                                                xt[:, k, g * D:(g + 1) * D], None,
                                                bounds_check=last_row, oob_is_err=False).then_inc(s_kept[k], 16)
            for k in range(2):
                pool.wait_ge(s_kept[k], 16 * G * (NB // 2))

        @block.vector
        def _(dve):
            v = nc.vector
            dve.wait_ge(s_const, 64)
            dve.wait_ge(s_mask, 1)
            pre = Steps(dve, s_pre)
            pre.after(v.tensor_tensor(gw[:, :], gam[:, :], wr[:, :], ALU.mult))
            pre.after(v.tensor_tensor(bw[:, :], bet[:, :], wr[:, :], ALU.mult))
            pre.after(v.tensor_reduce(sgw[:, :], gw[:, :], AX, ALU.add))
            pre.after(v.tensor_reduce(cst[:, :], bw[:, :], AX, ALU.add))
            pre.after(v.tensor_tensor(cst[:, :], cst[:, :], bb[:, :], ALU.add))
            pre.after(v.memset(base[:, :], 0.0))
            with dve.Fori(0, NB // 2) as i:
                for k in range(2):
                    st = Steps(dve, s_v, PER, i * 2 + k)
                    dve.wait_ge(s_x[k], i * 16 + 16)
                    x3 = xt[:, k, :].rearrange("p (g d) -> p g d", g=G)
                    v.tensor_tensor(prod[:, :].rearrange("p (g d) -> p g d", g=G), x3,
                                    gw[:, :].rearrange("p (a d) -> p a d", a=1).broadcast_to([P, G, D]), ALU.mult)
                    for g in range(G):
                        ins = v.bn_stats(stats[:, g, :], x3[:, g, :])
                    st.after(ins)
                    v.tensor_reduce(dot[:, :], prod[:, :].rearrange("p (g d) -> p g d", g=G), AX, ALU.add)
                    for g in range(G):
                        ins = v.bn_aggr(mv[:, g, :], stats[:, g, :])
                    st.after(ins)
                    st.after(v.tensor_scalar(ve[:, :], mv[:, :, 1], 1e-5, None, ALU.add))
                    rsqrt(nc, st, rs[:, :], ve[:, :], hh[:, :])
                    st.after(v.tensor_scalar(hh[:, :], mv[:, :, 0], sgw[:, 0:1], None, ALU.mult))
                    st.after(v.tensor_tensor(hh[:, :], dot[:, :], hh[:, :], ALU.subtract))
                    st.after(v.tensor_tensor(hh[:, :], hh[:, :], rs[:, :], ALU.mult))
                    dve.wait_ge(s_scored, i * 32 + 16 * k)
                    v.tensor_scalar(sc[:, :], hh[:, :], cst[:, 0:1], None, ALU.add).then_inc(s_score, 1)
                    dve.wait_ge(s_score, i * 2 + (k + 1))
                    dve.wait_ge(s_row[k], i * 16 + 16)
                    for g in range(G):
                        st.wait(3)
                        st.counted(v.tensor_scalar(junk[:, 2 * (g % 2), :], srow[:, k, :], sc[:, g:g + 1], 0.0,
                                                  ALU.is_gt, ALU.add, accum_out=above[:, g:g + 1]))
                        st.wait(3)
                        ins = v.scalar_tensor_tensor(junk[:, 2 * (g % 2) + 1, :], srow[:, k, :], sc[:, g:g + 1],
                                                     earlier[:, g, :], ALU.is_equal, ALU.mult,
                                                     accum_out=ties[:, g:g + 1])
                        if g < G - 1:
                            st.counted(ins)
                    ins.then_inc(s_ranked, 1)
                    dve.wait_ge(s_ranked, i * 2 + (k + 1))
                    st.after(v.tensor_tensor(rank[:, :], above[:, :], ties[:, :], ALU.add))
                    st.after(v.tensor_scalar(over[:, :], rank[:, :], float(S), 1.0e6, ALU.is_ge, ALU.mult))
                    dve.wait_ge(s_kept[k], i * (16 * G))
                    v.scalar_tensor_tensor(dest[:, k, :], rank[:, :], base[:, 0:1], over[:, :],
                                           ALU.add, ALU.add).then_inc(s_dest, 1)
                    dve.wait_ge(s_dest, i * 2 + (k + 1))
                    st.after(v.tensor_scalar(base[:, :], base[:, :], float(S), None, ALU.add))
                    st.end()


def at(turn, per, n):
    return turn * per + (CREDIT + n)


def two_a_turn(eng, n, body):
    with eng.Fori(0, n // 2 - 1) as i:
        for k in range(2):
            body(i * 2 + k, i, k, 0)
    for k in range(2):
        body(n - 2 + k, n // 2 - 1, k, 1 + k)


CREDIT = 64


def ssm(nc, h0, loglam, wd, bd, wb, wc, wout, bout, ct_d, h1):
    NS, NU, NA = 16, 24, 128
    NH = D - NA
    H0W, H1W = 263, S - 263
    HALF = [(0, H0W), (H0W, S)]
    LAG, RING = 3, 4
    FS = 9
    GU, NG = 4, NU // 4
    FRONT_AT = {2 * s + 4: s for s in range(FS)}
    VP = 1 + 1 + RSQRT_STEPS + 1
    with ExitStack() as ctx:
        sb = lambda name, shape, dt=F32: ctx.enter_context(nc.sbuf_tensor("b_" + name, shape, dt))
        ps = lambda name, shape: ctx.enter_context(nc.psum_tensor("b_" + name, shape, F32))
        sem = semaphores(nc, ctx, "b_")
        ident = sb("ident", [128, 128])
        wd_n, wout_n = sb("wd_n", [KC, 2, D]), sb("wout_n", [KC, 2, D * NS])
        wb_n, wc_n = sb("wb_n", [NS, D]), sb("wc_n", [NS, D])
        w_hi = sb("w_hi", [KC, 2, NS // 2, 128])
        wdT = sb("wdT", [KC, KT, 256])
        wbcT = sb("wbcT", [KC, KT, 128])
        woutT = sb("woutT", [128, NU, D])
        ll, la, nlam = sb("ll", [128, NU]), sb("la", [128, NU]), sb("nlam", [128, NU])
        bdc = sb("bdc", [128, 2])
        bo = sb("bo", [TP, D])
        sel = sb("sel", [96, NU, 128], BF16)
        h = sb("h", [TP, 2, TT, D])
        hb = sb("hb", [TP, 2, TT, D])
        ho = sb("ho", [TP, 2, TT, D])
        xn = sb("xn", [TP, TT, D])
        stats, mv = sb("stats", [TP, TT, 6]), sb("mv", [TP, TT, 2])
        ve, rs, hh, nb_ = (sb(n, [TP, TT]) for n in ("ve", "rs", "hh", "nb"))
        xT = sb("xT", [KC, KT, S])
        za, zr, zl = sb("za", [128, 2, H0W]), sb("zr", [128, 2, H0W]), sb("zl", [128, 2, H0W])
        delta = sb("delta", [128, 2, 2, S])
        bs = sb("bs", [96, 2, S], BF16)
        br, b2 = sb("br", [96, H0W]), sb("b2", [96, H0W], BF16)
        cs = sb("cs", [128, 2, S])
        cb = sb("cb", [128, 3, GU, S])
        ae, bm, hs, ys = (sb(n, [128, RING, S]) for n in ("ae", "bm", "hs", "ys"))
        pB = ps("pB", [128, 2, 1024])
        pF = ps("pF", [128, 512])
        pA = ps("pA", [TP, 3, 512])

        s_w, s_id0, s_id, s_wT, s_wTc, s_lam, s_pre = (sem(n) for n in (
            "s_w", "s_id0", "s_id", "s_wT", "s_wTc", "s_lam", "s_pre"))
        s_h = [sem(f"s_h{k}") for k in range(2)]
        s_cb = [sem(f"s_cb{k}") for k in range(3)]
        s_ct = [sem(f"s_ct{k}") for k in range(2)]
        s_out = [sem(f"s_out{k}") for k in range(2)]
        names = ("stat", "xn", "front", "faR", "b1", "bR", "b2", "bs", "ln", "delta", "B", "bm", "ae", "hs", "ys",
                 "wo", "fin", "hb")
        s = {n: sem("q_" + n) for n in names}
        s_va, s_aa, s_go = sem("s_va"), sem("s_aa"), sem("s_go")
        block = ctx.enter_context(nc.Block())
        v, a = nc.vector, nc.scalar

        def batches(eng, body):
            for k in range(2):
                body(k, 0, k, k == 0, False)
            with eng.Fori(1, NB // 2 - 1) as i:
                for k in range(2):
                    body(i * 2 + k, i, k, False, False)
            for k in range(2):
                body(NB - 2 + k, NB // 2 - 1, k, False, k == 1)

        @block.sync
        def _(sp):
            sp.dma_start(wd_n[:, :, :], wd.rearrange("(c p) d -> p c d", p=KC)).then_inc(s_w, 16)
            sp.dma_start(wout_n[:, :, :], wout.rearrange("(c p) d -> p c d", p=KC)).then_inc(s_w, 16)
            sp.dma_start(wb_n[:, :], wb).then_inc(s_w, 16)
            sp.dma_start(wc_n[:, :], wc).then_inc(s_w, 16)
            sp.dma_start(ll[:, 0:NS], loglam[0:NA, :]).then_inc(s_w, 16)
            two = loglam[NA:D, :].rearrange("e (j t) -> t e j", t=2)
            for t in range(2):
                sp.dma_start(ll[64 * t:64 * t + 64, NS:NU], two[t], allow_slow_non_contiguous=True).then_inc(s_w, 16)
                sp.dma_start(bdc[64 * t:64 * t + 64, 1:2], bd[NA:D].rearrange("(e a) -> e a", a=1)).then_inc(s_w, 16)
            sp.dma_start(bdc[:, 0:1], bd[0:NA].rearrange("(e a) -> e a", a=1)).then_inc(s_w, 16)
            sp.dma_start(bo[:, :], bout.rearrange("(a d) -> a d", a=1).broadcast_to([TP, D])).then_inc(s_w, 16)
            rows = lambda x, b: x[bass.ds(b * S, S), :].rearrange("(t p) d -> p t d", p=TP)
            sp.dma_start(h[:, 0, :, :], rows(h0, 0)).then_inc(s_h[0], 16)

            def body(b, i, k, first, last):
                if not last:
                    sp.wait_ge(s["xn"], at(b, 1, 0))
                    sp.wait_ge(s["hb"], at(b, 1, 0))
                    sp.dma_start(h[:, 1 - k, :, :], rows(h0, b + 1)).then_inc(s_h[1 - k], 16)
                sp.wait_ge(s_ct[k], i * 32 + 32)
                for g in range(NG):
                    n_dma = 16 if g * GU < NS else 32
                    sp.wait_ge(s["ys"], at(b, NU, (g - 2) * GU))
                    if g * GU < NS:
                        src = ct_d[b, g * GU:(g + 1) * GU, :].rearrange("(a n) l -> a (n l)", a=1)
                        sp.dma_start(cb[:, g % 3, :, :].rearrange("p n l -> p (n l)"),
                                     src.broadcast_to([128, GU * S])).then_inc(s_cb[g % 3], 16)
                    else:
                        j = g * GU - NS
                        for t in range(2):
                            src = ct_d[b, 2 * j:2 * j + 2 * GU, :].rearrange("(n t) l -> t n l", t=2)
                            sp.dma_start(cb[64 * t:64 * t + 64, g % 3, :, :],
                                         src[t:t + 1].broadcast_to([64, GU, S])).then_inc(s_cb[g % 3], 16)
                    if g == 3 and not first:
                        store(b - 1, 1 - k)

            def store(b, k):
                sp.wait_ge(s["fin"], at(b, 1, 1))
                sp.dma_start(rows(h1, b), ho[:, k, :, :]).then_inc(s_out[k], 16)

            batches(sp, body)
            store(NB - 1, 1)
            for k in range(2):
                sp.wait_ge(s_out[k], 16 * (NB // 2))

        def cb_count(g):
            return sum(16 if q * GU < NS else 32 for q in range(g % 3, g + 1, 3))
        CB_ALL = [cb_count(3 + q) for q in range(3)]

        @block.gpsimd
        def _(pool):
            for n in ("ys", "hb"):
                pool.sem_inc(s[n], CREDIT)
            pool.memset(ident[:, :], 0.0).then_inc(s_id0, 1)
            pool.memset(sel[:, :, :], 0.0).then_inc(s_id0, 1)
            pool.memset(wbcT[:, :, :], 0.0).then_inc(s_id0, 1)
            pool.wait_ge(s_id0, 3)
            pool.affine_select(out=ident[:, :], in_=ident[:, :], compare_op=ALU.not_equal, fill=1.0, base=0,
                               pattern=[[-1, 128]], channel_multiplier=1).then_inc(s_id, 1)
            for g in range(3):
                pool.wait_ge(s_id, 1 + 2 * g)
                m = sel[32 * g:32 * g + 32, 0:NS, :]
                pool.affine_select(out=m, in_=m, compare_op=ALU.not_equal, fill=1.0, base=0,
                                   pattern=[[-1, NS], [0, 128]], channel_multiplier=1).then_inc(s_id, 1)
                pool.wait_ge(s_id, 2 + 2 * g)
                m = sel[32 * g:32 * g + 32, NS:NU, :].rearrange("p j (t e) -> p j t e", t=2)
                pool.affine_select(out=m, in_=m, compare_op=ALU.not_equal, fill=1.0, base=0,
                                   pattern=[[-2, NS // 2], [-1, 2], [0, NH]], channel_multiplier=1).then_inc(s_id, 1)

            def body(b, i, k, first, last):
                pool.wait_ge(s_h[k], i * 16 + 16)
                pool.wait_ge(s["fin"], at(b, 1, -1))
                pool.tensor_tensor(hb[:, k, :, :], h[:, k, :, :],
                                   bo[:, :].rearrange("p (a d) -> p a d", a=1).broadcast_to([TP, TT, D]),
                                   ALU.add).then_inc(s["hb"], 1)
                for u in range(NU):
                    g = u // GU
                    if u % GU == 0:
                        pool.wait_ge(s_cb[g % 3], b * CB_ALL[g % 3] + cb_count(g))
                    pool.wait_ge(s["hs"], at(b, NU, u + 1))
                    pool.wait_ge(s["wo"], at(b, NU, u + 1 - RING))
                    pool.tensor_tensor(ys[:, u % RING, :], hs[:, u % RING, :], cb[:, g % 3, u % GU, :],
                                       ALU.mult).then_inc(s["ys"], 1)

            pool.wait_ge(s_w, 16 * 11)
            for r in range(2):
                pool.wait_ge(s_id, 7 + r)
                pool.tensor_copy(w_hi[:, r, :, :].rearrange("p j (t e) -> p (j t) e", t=2),
                                 wout_n[:, r, :].rearrange("p (d n) -> p n d", n=NS)[:, :, NA:D]).then_inc(s_id, 1)
            batches(pool, body)

        def front_act(b, i, k, step, ln_ready=None):
            n = b * 1
            a_eng = nc.scalar
            a_eng.wait_ge(s["front"], at(b, FS, step + 1))
            if step < 3:
                if step == 1:
                    dst = xT[:, :, 4 * TP:S]
                    src = pF[0:KC, 0:2 * TP].rearrange("p (c l) -> p c l", c=2)
                else:
                    dst, src = xT[:, step // 2, 0:4 * TP], pF[0:KC, 0:4 * TP]
                a_eng.activation(dst, src, ACT.Copy).then_inc(s["faR"], 1)
            elif step < 7:
                q, half = (step - 3) // 2, (step - 3) % 2
                w = HALF[half][1] - HALF[half][0]
                if step == 3:
                    a_eng.wait_ge(s["delta"], at(b, 4, 0))
                else:
                    a_eng.wait_ge(s["delta"], at(b, 4, step - 4))
                a_eng.activation(za[:, half, 0:w], pF[:, 0:w], ACT.Abs, bias=bdc[:, q:q + 1]).then_inc(s_aa, 1)
                a_eng.activation(zr[:, half, 0:w], pF[:, 0:w], ACT.Relu, bias=bdc[:, q:q + 1]).then_inc(s["faR"], 1)
                base = b * 8 + 2 * (step - 3)
                a_eng.wait_ge(s_aa, base + 1)
                a_eng.activation(za[:, half, 0:w], za[:, half, 0:w], ACT.Exp, scale=-1.0).then_inc(s_aa, 1)
                a_eng.wait_ge(s_aa, base + 2)
                a_eng.activation(zl[:, half, 0:w], za[:, half, 0:w], ACT.Ln, bias=1.0).then_inc(s["ln"], 1)
            else:
                half = step - 7
                lo, hi = HALF[half]
                if half == 0:
                    a_eng.wait_ge(s["B"], at(b, NU, -NU))
                a_eng.activation(bs[:, k, lo:hi], pF[0:96, 0:hi - lo], ACT.Copy).then_inc(s["b1"], 1)
                if half == 0:
                    a_eng.wait_ge(s_ct[k], i * 32)
                a_eng.activation(cs[96:96 + NS, k, lo:hi], pF[96:96 + NS, 0:hi - lo], ACT.Copy)\
                    .then_inc(s["faR"], 1)

        def front_act_late(b, i, k, step):
            if step >= 7:
                half = step - 7
                lo, hi = HALF[half]
                a_eng = nc.scalar
                a_eng.wait_ge(s["bR"], at(b, 2, half + 1))
                a_eng.activation(bs[32:64, k, lo:hi], br[32:64, 0:hi - lo], ACT.Copy)
                a_eng.activation(b2[64:96, 0:hi - lo], br[64:96, 0:hi - lo], ACT.Copy).then_inc(s["b2"], 1)
                a_eng.wait_ge(s["faR"], at(b, FS, step + 1))
                a_eng.dma_start(ct_d[b, :, lo:hi], cs[96:96 + NS, k, lo:hi]).then_inc(s_ct[k], 16)

        def front_ln_act(b, i, k):
            nc.scalar.wait_ge(s["stat"], at(b, 1, 1))
            nc.scalar.wait_ge(s["front"], at(b, FS, 0))
            for t in range(TT):
                ins = nc.scalar.activation(xn[:, t, :], h[:, k, t, :], ACT.Identity, bias=nb_[:, t:t + 1],
                                           scale=rs[:, t:t + 1])
            ins.then_inc(s["xn"], 1)

        @block.scalar
        def _(act):
            for n in ("faR", "b1", "b2", "ln", "ae", "xn"):
                act.sem_inc(s[n], CREDIT)
            act.wait_ge(s_w, 16 * 11)
            chain = Steps(act, s_lam)
            chain.after(act.activation(la[:, :], ll[:, :], ACT.Abs))
            chain.after(act.activation(la[:, :], la[:, :], ACT.Exp, scale=-1.0))
            chain.after(act.activation(la[:, :], la[:, :], ACT.Ln, bias=1.0))
            chain.after(act.activation(ll[:, :], ll[:, :], ACT.Relu))
            front_ln_act(0, 0, 0)
            for step in range(FS):
                front_act(0, 0, 0, step)
                front_act_late(0, 0, 0, step)
            act.wait_ge(s_pre, 1)

            def body(b, i, k, first, last):
                for u in range(NU):
                    q = 0 if u < NS else 1
                    if u == 0:
                        act.wait_ge(s["delta"], at(b, 4, 4))
                    act.wait_ge(s["hs"], at(b, NU, u + 1 - RING))
                    act.activation(ae[:, u % RING, :], delta[:, k, q, :], ACT.Exp, scale=nlam[:, u:u + 1])\
                        .then_inc(s["ae"], 1)
                    if not last:
                        ii = i + k
                        if u == 2:
                            front_ln_act(b + 1, ii, 1 - k)
                        if u in FRONT_AT:
                            front_act(b + 1, ii, 1 - k, FRONT_AT[u])
                        if u - 1 in FRONT_AT:
                            front_act_late(b + 1, ii, 1 - k, FRONT_AT[u - 1])

            batches(act, body)

        def front_pe(b, i, k, step):
            pe = nc.tensor
            if step == 0:
                pe.wait_ge(s["xn"], at(b, 1, 1))
            pe.wait_ge(s["faR"], at(b, FS, step))
            if step < 3:
                if step == 1:
                    tiles = [(c, 4, c * TP) for c in range(KT)]
                else:
                    tiles = [(step // 2, t, t * TP) for t in range(4)]
                for c, t, col in tiles:
                    ins = pe.transpose(pF[0:KC, col:col + TP], xn[:, t, c * KC:(c + 1) * KC], ident[0:TP, 0:TP])
            else:
                if step == 8:
                    pe.wait_ge(s["bR"], at(b, 2, 1))
                half = (step - 3) % 2
                lo, hi = HALF[half]
                for c in range(KT):
                    lhs = wdT[:, c, 128 * ((step - 3) // 2):][:, 0:128] if step < 7 else wbcT[:, c, :]
                    ins = pe.matmul(pF[:, 0:hi - lo], lhs, xT[:, c, lo:hi], start=(c == 0), stop=(c == KT - 1))
            ins.then_inc(s["front"], 1)

        @block.tensor
        def _(pe):
            for n in ("front", "B", "wo"):
                pe.sem_inc(s[n], CREDIT)
            pe.wait_ge(s_w, 16 * 11)
            pe.wait_ge(s_id, 9)
            w4 = wout_n[:, :, :].rearrange("p c (d n) -> p c n d", n=NS)
            n = 0
            for c in range(KT):
                for r in range(2):
                    ins = pe.transpose(pF[0:KC, (2 * c + r) * KC:(2 * c + r + 1) * KC], wd_n[:, r, c * KC:(c + 1) * KC],
                                       ident[0:KC, 0:KC])
            ins.then_inc(s_wT, 1)
            pe.wait_ge(s_wTc, 1)
            for c in range(KT):
                pe.transpose(pF[0:KC, c * NS:(c + 1) * NS], wb_n[:, c * KC:(c + 1) * KC], ident[0:NS, 0:NS])
                ins = pe.transpose(pF[0:KC, (2 + c) * NS:(3 + c) * NS], wc_n[:, c * KC:(c + 1) * KC], ident[0:NS, 0:NS])
            ins.then_inc(s_wT, 1)
            for u in range(NU):
                pe.wait_ge(s_wTc, u + 1 if u >= 2 else 2)
                bank = pB[:, u % 2, 0:D]
                for r in range(2):
                    if u < NS:
                        src = w4[:, r, u, 0:NA]
                    else:
                        src = w_hi[:, r, u - NS, :]
                    ins = pe.transpose(bank[:, r * KC:(r + 1) * KC], src, ident[0:KC, 0:KC])
                ins.then_inc(s_wT, 1)
            pe.wait_ge(s_wTc, 2 + NU)
            for step in range(FS):
                front_pe(0, 0, 0, step)

            def spread(b, k, u):
                if u == 0:
                    pe.wait_ge(s["bs"], at(b, 2, 2))
                pe.wait_ge(s["bm"], at(b, NU, u + 1 - 2))
                for lo, hi in ((0, 512), (512, S)):
                    ins = pe.matmul(pB[:, u % 2, lo:hi], sel[:, u, :], bs[:, k, lo:hi], start=True, stop=True)
                ins.then_inc(s["B"], 1)

            def project(b, k, u):
                pe.wait_ge(s["ys"], at(b, NU, u + 1))
                if u == 0:
                    pe.wait_ge(s["fin"], at(b, 1, 0))
                for t in range(TT):
                    ins = pe.matmul(pA[:, t // 2, (t % 2) * D:(t % 2 + 1) * D], ys[:, u % RING, t * TP:(t + 1) * TP],
                                    woutT[:, u, :], start=(u == 0 and t % 2 == 0), stop=(u == NU - 1),
                                    skip_group_check=True)
                ins.then_inc(s["wo"], 1)

            for u in range(2):
                spread(0, 0, u)

            def body(b, i, k, first, last):
                for u in range(NU + LAG):
                    if u < NU - 2:
                        spread(b, k, u + 2)
                    elif u < NU and not last:
                        spread(b + 1, 1 - k, u + 2 - NU)
                    if u >= LAG:
                        project(b, k, u - LAG)
                    if u in FRONT_AT and not last:
                        front_pe(b + 1, i + k, 1 - k, FRONT_AT[u])

            batches(pe, body)

        def front_stat(b, i, k):
            dve = nc.vector
            st = Steps(dve, s_va, VP, b)
            dve.wait_ge(s_h[k], i * 16 + 16)
            dve.wait_ge(s["xn"], at(b, 1, 0))
            for t in range(TT):
                ins = v.bn_stats(stats[:, t, :], h[:, k, t, :])
            st.after(ins)
            dve.sem_inc(s_go, 1)
            for t in range(TT):
                ins = v.bn_aggr(mv[:, t, :], stats[:, t, :])
            st.after(ins)
            st.after(v.tensor_scalar(ve[:, :], mv[:, :, 1], 1e-5, None, ALU.add))
            rsqrt(nc, st, rs[:, :], ve[:, :], hh[:, :])
            st.end()
            v.scalar_tensor_tensor(nb_[:, :], mv[:, :, 0], -1.0, rs[:, :], ALU.mult, ALU.mult).then_inc(s["stat"], 1)

        def front_dve(b, i, k, step):
            dve = nc.vector
            if 3 <= step < 7:
                q, half = (step - 3) // 2, (step - 3) % 2
                lo, hi = HALF[half]
                dve.wait_ge(s["ln"], at(b, 4, step - 2))
                v.tensor_tensor(delta[:, k, q, lo:hi], zr[:, half, 0:hi - lo], zl[:, half, 0:hi - lo], ALU.add)\
                    .then_inc(s["delta"], 1)
            if step >= 7:
                half = step - 7
                lo, hi = HALF[half]
                dve.wait_ge(s["b1"], at(b, 2, half + 1))
                v.tensor_tensor(br[:, 0:hi - lo], pF[0:96, 0:hi - lo], bs[:, k, lo:hi], ALU.subtract)\
                    .then_inc(s["bR"], 1)

        def front_dve_late(b, i, k, step):
            dve = nc.vector
            if step >= 7:
                half = step - 7
                lo, hi = HALF[half]
                dve.wait_ge(s["b2"], at(b, 2, half + 1))
                v.tensor_tensor(bs[64:96, k, lo:hi], br[64:96, 0:hi - lo], b2[64:96, 0:hi - lo],
                                ALU.subtract)\
                    .then_inc(s["bs"], 1)
                dve.wait_ge(s["bs"], at(b, 2, half + 1))

        @block.vector
        def _(dve):
            for n in ("stat", "bR", "bs", "delta", "bm", "hs", "fin"):
                dve.sem_inc(s[n], CREDIT)
            front_stat(0, 0, 0)
            dve.wait_ge(s_wT, 1)
            for c in range(KT):
                ins = v.tensor_copy(wdT[:, c, 0:D], pF[0:KC, 2 * c * KC:(2 * c + 2) * KC])
            for c in range(KT):
                ins = v.tensor_copy(wdT[:, c, D:256], pF[0:KC, 2 * c * KC + NA:(2 * c + 2) * KC])
            ins.then_inc(s_wTc, 1)
            dve.wait_ge(s_wT, 2)
            dve.wait_ge(s_id0, 3)
            for c in range(KT):
                for g in range(3):
                    v.tensor_copy(wbcT[:, c, 32 * g:32 * g + NS], pF[0:KC, c * NS:(c + 1) * NS])
                ins = v.tensor_copy(wbcT[:, c, 96:96 + NS], pF[0:KC, (2 + c) * NS:(3 + c) * NS])
            ins.then_inc(s_wTc, 1)
            for u in range(NU):
                dve.wait_ge(s_wT, u + 3)
                v.tensor_copy(woutT[:, u, :], pB[:, u % 2, 0:D]).then_inc(s_wTc, 1)
            dve.wait_ge(s_lam, 4)
            v.scalar_tensor_tensor(nlam[:, :], ll[:, :], -1.0, la[:, :], ALU.mult, ALU.subtract).then_inc(s_pre, 1)
            for step in range(FS):
                front_dve(0, 0, 0, step)
                front_dve_late(0, 0, 0, step)

            def weigh(b, k, u):
                if u == 0:
                    dve.wait_ge(s["delta"], at(b, 4, 4))
                dve.wait_ge(s["B"], at(b, NU, u + 1))
                dve.wait_ge(s["hs"], at(b, NU, u + 1 - RING))
                v.tensor_tensor(bm[:, u % RING, :], delta[:, k, 0 if u < NS else 1, :], pB[:, u % 2, 0:S], ALU.mult)\
                    .then_inc(s["bm"], 1)

            def finish(b, i, k):
                dve.wait_ge(s["wo"], at(b, NU, NU))
                dve.wait_ge(s["hb"], at(b, 1, 1))
                dve.wait_ge(s_out[k], i * 16)
                for c in range(3):
                    n = 2 if c < 2 else 1
                    ins = v.tensor_tensor(ho[:, k, 2 * c:2 * c + n, :],
                                          pA[:, c, 0:n * D].rearrange("p (t d) -> p t d", t=n),
                                          hb[:, k, 2 * c:2 * c + n, :], ALU.add)
                ins.then_inc(s["fin"], 1)

            weigh(0, 0, 0)

            def body(b, i, k, first, last):
                for u in range(NU):
                    if u < NU - 1:
                        weigh(b, k, u + 1)
                    elif not last:
                        weigh(b + 1, 1 - k, 0)
                    dve.wait_ge(s["ae"], at(b, NU, u + 1))
                    dve.wait_ge(s["bm"], at(b, NU, u + 1))
                    dve.wait_ge(s["ys"], at(b, NU, u + 1 - RING))
                    v.tensor_tensor_scan(hs[:, u % RING, :], ae[:, u % RING, :], bm[:, u % RING, :], 0.0,
                                         ALU.mult, ALU.add).then_inc(s["hs"], 1)
                    if u == LAG and not first:
                        finish(b - 1, i - 1 + k, 1 - k)
                    if not last:
                        if u == 0:
                            front_stat(b + 1, i + k, 1 - k)
                        if u in FRONT_AT:
                            front_dve(b + 1, i + k, 1 - k, FRONT_AT[u])
                        if u - 1 in FRONT_AT:
                            front_dve_late(b + 1, i + k, 1 - k, FRONT_AT[u - 1])

            batches(dve, body)
            finish(NB - 1, NB // 2 - 1, 1)


def dense_experts(nc, h1, gate_w, gate_b, bias, wu, bu, wg, bg, wd, bd, swu, sbu, swg, sbg, swd, sbd, h2):
    E, HID, G = 16, 128, 8
    EA = E + 1
    CT, NC = 4, T // (4 * TP)
    N = CT * TP
    STAT_AT, FRONT_AT, ROUTE_AT = 0, {2: 0, 4: 1, 6: 2, 13: 3, 15: 4}, {7: 0, 9: 1, 10: 2, 11: 3, 12: 4}
    FS = 5
    VP = 1 + 1 + RSQRT_STEPS + 1
    RP = 20
    with ExitStack() as ctx:
        sb = lambda name, shape, dt=F32: ctx.enter_context(nc.sbuf_tensor("c_" + name, shape, dt))
        ps = lambda name, shape: ctx.enter_context(nc.psum_tensor("c_" + name, shape, F32))
        sem = semaphores(nc, ctx, "c_")
        ident = sb("ident", [128, 128])
        wu_s, wg_s = sb("wu_s", [KC, KT, EA, HID]), sb("wg_s", [KC, KT, EA, HID])
        wd_s = sb("wd_s", [HID, EA, D])
        bn = sb("bn", [EA, 2, HID])
        bc = sb("bc", [HID, 2, EA])
        bd_s = sb("bd_s", [EA, D])
        gw_s = sb("gw_s", [KC, KT, E])
        gb_s, bi_s = sb("gb_s", [TP, E]), sb("bi_s", [TP, E])
        tri = sb("tri", [TP, E, E])
        h, y = sb("h", [TP, 2, CT, D]), sb("y", [TP, 2, CT, D])
        xn = sb("xn", [TP, CT, D])
        stats, mv = sb("stats", [TP, CT, 6]), sb("mv", [TP, CT, 2])
        ve, rs, hh, nb_ = (sb(n, [TP, CT]) for n in ("ve", "rs", "hh", "nb"))
        xT = sb("xT", [KC, 2, KT, N])
        lg, sc, sm = sb("lg", [TP, CT, E]), sb("sc", [TP, CT, E]), sb("sm", [TP, CT, E])
        mx, sums = sb("mx", [TP, CT]), sb("sums", [TP, CT])
        gs, gm = sb("gs", [TP, CT, G]), sb("gm", [TP, CT, G])
        c1, c2 = sb("c1", [TP, CT, E, E]), sb("c2", [TP, CT, E, E])
        rk = sb("rk", [TP, CT, E])
        w = sb("w", [TP, 2, CT, EA])
        wT = sb("wT", [EA, N])
        su, ac = sb("su", [HID, 2, N]), sb("ac", [HID, 2, N])
        pU, pG = ps("pU", [HID, 2, 512]), ps("pG", [HID, 2, 512])
        pD, pF = ps("pD", [TP, 2, 512]), ps("pF", [128, 2, 512])

        s_w, s_id0, s_id, s_bn, s_bc, s_va, s_ro, s_go = (sem(n) for n in (
            "s_w", "s_id0", "s_id", "s_bn", "s_bc", "s_va", "s_ro", "s_go"))
        s_h = [sem(f"s_h{k}") for k in range(2)]
        s_out = [sem(f"s_out{k}") for k in range(2)]
        s = {n: sem("q_" + n) for n in ("stat", "xn", "front", "xT", "lg", "lg0", "exp", "w", "wT", "y0", "ug", "su",
                                        "ac", "dn", "acc", "accv")}
        N_W = 16 * 17
        block = ctx.enter_context(nc.Block())
        v = nc.vector
        tiles = lambda x, c: x[bass.ds(c * N, N), :].rearrange("(t p) d -> p t d", p=TP)

        @block.sync
        def _(sp):
            row = lambda x: x.rearrange("(a d) -> a d", a=1)
            for c in range(2):
                sp.dma_start(h[:, c, :, :], tiles(h1, c)).then_inc(s_h[c], 16)
            sp.dma_start(gw_s[:, :, :], gate_w.rearrange("(c p) e -> p c e", p=KC)).then_inc(s_w, 16)
            sp.dma_start(gb_s[:, :], row(gate_b).broadcast_to([TP, E])).then_inc(s_w, 16)
            sp.dma_start(bi_s[:, :], row(bias).broadcast_to([TP, E])).then_inc(s_w, 16)
            for n, (be, bsh) in enumerate(((bu, sbu), (bg, sbg))):
                sp.dma_start(bn[0:E, n, :], be).then_inc(s_w, 16)
                sp.dma_start(bn[E:EA, n, :], row(bsh)).then_inc(s_w, 16)
            sp.dma_start(bd_s[0:E, :], bd).then_inc(s_w, 16)
            sp.dma_start(bd_s[E:EA, :], row(sbd)).then_inc(s_w, 16)
            for dst, we, ws in ((wu_s, wu, swu), (wg_s, wg, swg)):
                for c in range(KT):
                    sp.dma_start(dst[:, c, 0:E, :], we[:, c * KC:(c + 1) * KC, :].rearrange("e p n -> p e n"))\
                        .then_inc(s_w, 16)
                sp.dma_start(dst[:, :, E, :], ws.rearrange("(c p) n -> p c n", p=KC)).then_inc(s_w, 16)
            sp.dma_start(wd_s[:, 0:E, :], wd.rearrange("e p n -> p e n")).then_inc(s_w, 16)
            sp.dma_start(wd_s[:, E, :], swd).then_inc(s_w, 16)

            def body(c, i, k, last):
                if not last:
                    sp.wait_ge(s["y0"], at(c, 1, 1))
                    sp.dma_start(h[:, k, :, :], tiles(h1, c + 2)).then_inc(s_h[k], 16)
                sp.wait_ge(s["acc"], at(c, EA, EA))
                sp.dma_start(tiles(h2, c), y[:, k, :, :]).then_inc(s_out[k], 16)

            two_a_turn(sp, NC, body)
            for k in range(2):
                sp.wait_ge(s_out[k], 16 * (NC // 2))

        @block.gpsimd
        def _(pool):
            pool.memset(ident[:, :], 0.0).then_inc(s_id0, 1)
            pool.memset(tri[:, :, :], 0.0).then_inc(s_id0, 1)
            pool.memset(w[:, :, :, :], 1.0).then_inc(s_id0, 1)
            pool.wait_ge(s_id0, 3)
            pool.affine_select(out=ident[:, :], in_=ident[:, :], compare_op=ALU.not_equal, fill=1.0, base=0,
                               pattern=[[-1, 128]], channel_multiplier=1).then_inc(s_id, 1)
            pool.wait_ge(s_id, 1)
            pool.affine_select(out=tri[:, :, :], in_=tri[:, :, :], compare_op=ALU.is_ge, fill=1.0, base=0,
                               pattern=[[-1, E], [1, E]], channel_multiplier=0).then_inc(s_id, 1)

        def front_pe(c, i, k, step):
            pe = nc.tensor
            if step < 2:
                if step == 0:
                    pe.wait_ge(s["xn"], at(c, 1, 1))
                    pe.wait_ge(s["y0"], at(c, 1, 0))
                else:
                    pe.wait_ge(s["xT"], at(c, 2, 1))
                for t in range(CT):
                    ins = pe.transpose(pF[0:KC, 0, t * TP:(t + 1) * TP], xn[:, t, step * KC:(step + 1) * KC],
                                       ident[0:TP, 0:TP])
            elif step == 2:
                pe.wait_ge(s["xT"], at(c, 2, 2))
                for t in range(CT):
                    for cc in range(KT):
                        ins = pe.matmul(pF[0:TP, 0, t * E:(t + 1) * E], xT[:, k, cc, t * TP:(t + 1) * TP],
                                        gw_s[:, cc, :], start=(cc == 0), stop=(cc == KT - 1))
            elif step == 3:
                pe.wait_ge(s["w"], at(c, 1, 1))
                for t in range(CT):
                    ins = pe.transpose(pF[0:EA, 0, t * TP:(t + 1) * TP], w[:, k, t, :], ident[0:TP, 0:TP])
            else:
                pe.wait_ge(s["wT"], at(c, 1, 1))
                for t in range(CT):
                    ins = pe.matmul(pF[0:TP, t // 2, (t % 2) * D:(t % 2 + 1) * D], wT[:, t * TP:(t + 1) * TP],
                                    bd_s[:, :], start=True, stop=True)
            ins.then_inc(s["front"], 1)

        @block.tensor
        def _(pe):
            for n in ("front", "ug", "dn"):
                pe.sem_inc(s[n], CREDIT)
            pe.wait_ge(s_w, N_W)
            pe.wait_ge(s_id, 2)
            for n in range(2):
                ins = pe.transpose(pF[:, 0, n * EA:(n + 1) * EA], bn[:, n, :], ident[0:EA, 0:EA])
            ins.then_inc(s_bn, 1)
            pe.wait_ge(s_bc, 1)
            for step in range(FS):
                front_pe(0, 0, 0, step)

            def up_gate(c, k, e):
                if e == 0:
                    pe.wait_ge(s["xT"], at(c, 2, 2))
                pe.wait_ge(s["ac"], at(c, EA, e - 1))
                for p, ws in ((pU, wu_s), (pG, wg_s)):
                    for cc in range(KT):
                        ins = pe.matmul(p[:, (e + k) % 2, 0:N], ws[:, cc, e, :],
                                        xT[:, k, cc, :], start=(cc == 0), stop=(cc == KT - 1))
                ins.then_inc(s["ug"], 1)

            def down(c, k, e):
                pe.wait_ge(s["ac"], at(c, EA, e + 1))
                pe.wait_ge(s["acc"], at(c, EA, e))
                for t in range(CT):
                    ins = pe.matmul(pD[:, t // 2, (t % 2) * D:(t % 2 + 1) * D],
                                    ac[:, (e + k) % 2, t * TP:(t + 1) * TP], wd_s[:, e, :], start=True, stop=True)
                ins.then_inc(s["dn"], 1)

            up_gate(0, 0, 0)

            def body(c, i, k, last):
                for e in range(EA):
                    if e < EA - 1:
                        up_gate(c, k, e + 1)
                    elif last < 2:
                        up_gate(c + 1, 1 - k, 0)
                    down(c, k, e)
                    if e in FRONT_AT and last < 2:
                        front_pe(c + 1, i + k, 1 - k, FRONT_AT[e])

            two_a_turn(pe, NC, body)

        def front_act(c, i, k, step):
            act = nc.scalar
            if step in (0, 1):
                act.wait_ge(s["front"], at(c, FS, step + 1))
                act.activation(xT[:, k, step, :], pF[0:KC, 0, 0:N], ACT.Copy).then_inc(s["xT"], 1)
            elif step == 3:
                act.wait_ge(s["front"], at(c, FS, 4))
                act.activation(wT[:, :], pF[0:EA, 0, 0:N], ACT.Copy).then_inc(s["wT"], 1)

        def normalise(c, i, k):
            act = nc.scalar
            act.wait_ge(s["stat"], at(c, 1, 1))
            act.wait_ge(s["front"], at(c, FS, 0))
            for t in range(CT):
                ins = act.activation(xn[:, t, :], h[:, k, t, :], ACT.Identity, bias=nb_[:, t:t + 1],
                                     scale=rs[:, t:t + 1])
            ins.then_inc(s["xn"], 1)

        def exps(c):
            act = nc.scalar
            act.wait_ge(s["lg"], at(c, 1, 1))
            act.activation(sc[:, :, :], lg[:, :, :], ACT.Exp).then_inc(s["exp"], 1)

        @block.scalar
        def _(act):
            for n in ("xn", "xT", "wT", "su", "exp"):
                act.sem_inc(s[n], CREDIT)
            act.wait_ge(s_bn, 1)
            act.activation(bc[:, :, :], pF[:, 0, 0:2 * EA].rearrange("p (n e) -> p n e", n=2), ACT.Copy)\
                .then_inc(s_bc, 1)
            act.wait_ge(s_bc, 1)
            normalise(0, 0, 0)
            for step in range(2):
                front_act(0, 0, 0, step)
            exps(0)
            front_act(0, 0, 0, 3)

            def body(c, i, k, last):
                for e in range(EA):
                    r = (e + k) % 2
                    act.wait_ge(s["ug"], at(c, EA, e + 1))
                    act.wait_ge(s["ac"], at(c, EA, e - 1))
                    act.activation(su[:, r, :], pU[:, r, 0:N], ACT.Silu, bias=bc[:, 0, e:e + 1]).then_inc(s["su"], 1)
                    if last < 2:
                        if e == STAT_AT + 1:
                            normalise(c + 1, i + k, 1 - k)
                        if e - 1 in FRONT_AT:
                            front_act(c + 1, i + k, 1 - k, FRONT_AT[e - 1])
                        if ROUTE_AT.get(e - 1) == 0:
                            exps(c + 1)

            two_a_turn(act, NC, body)

        def statistics(c, i, k):
            dve = nc.vector
            st = Steps(dve, s_va, VP, c)
            dve.wait_ge(s_h[k], i * 16 + 16)
            dve.wait_ge(s["xn"], at(c, 1, 0))
            for t in range(CT):
                ins = v.bn_stats(stats[:, t, :], h[:, k, t, :])
            st.after(ins)
            dve.sem_inc(s_go, 1)
            for t in range(CT):
                ins = v.bn_aggr(mv[:, t, :], stats[:, t, :])
            st.after(ins)
            st.after(v.tensor_scalar(ve[:, :], mv[:, :, 1], 1e-5, None, ALU.add))
            rsqrt(nc, st, rs[:, :], ve[:, :], hh[:, :])
            st.end()
            v.scalar_tensor_tensor(nb_[:, :], mv[:, :, 0], -1.0, rs[:, :], ALU.mult, ALU.mult).then_inc(s["stat"], 1)

        def ranks(st, x, n):
            shape = [TP, CT, n, n]
            mine = x.rearrange("p t (e a) -> p t e a", a=1).broadcast_to(shape)
            theirs = x.rearrange("p t (a f) -> p t a f", a=1).broadcast_to(shape)
            a, b = c1[:, :, 0:n, 0:n], c2[:, :, 0:n, 0:n]
            st.after(v.tensor_tensor(a, theirs, mine, ALU.is_gt))
            st.after(v.tensor_tensor(b, theirs, mine, ALU.is_equal))
            tr = tri[:, 0:n, 0:n].rearrange("p (a e) f -> p a e f", a=1).broadcast_to(shape)
            st.after(v.tensor_tensor(b, b, tr, ALU.mult))
            st.after(v.tensor_tensor(a, a, b, ALU.add))
            st.after(v.tensor_reduce(rk[:, :, 0:n], a, AX, ALU.add))

        def route(c, k, part, st):
            dve = nc.vector
            wide = lambda x, n=E: x[:, :].rearrange("p (t a) -> p t a", a=1).broadcast_to([TP, CT, n])
            flat = lambda x: x[:, :].rearrange("p (a e) -> p a e", a=1).broadcast_to([TP, CT, E])
            if part == 0:
                dve.wait_ge(s["front"], at(c, FS, 3))
                st.after(v.tensor_tensor(lg[:, :, :], pF[0:TP, 0, 0:CT * E].rearrange("p (t e) -> p t e", t=CT),
                                         flat(gb_s), ALU.add))
                st.after(v.tensor_reduce(mx[:, :], lg[:, :, :], AX, ALU.max))
                v.tensor_tensor(lg[:, :, :], lg[:, :, :], wide(mx), ALU.subtract).then_inc(s["lg"], 1)
            elif part == 1:
                dve.wait_ge(s["exp"], at(c, 1, 1))
                st.after(v.tensor_reduce(sums[:, :], sc[:, :, :], AX, ALU.add))
                st.after(v.reciprocal(sums[:, :], sums[:, :]))
                st.after(v.tensor_tensor(sc[:, :, :], sc[:, :, :], wide(sums), ALU.mult))
                st.after(v.tensor_tensor(sm[:, :, :], sc[:, :, :], flat(bi_s), ALU.add))
                pair = sm[:, :, :].rearrange("p t (g a) -> p t g a", a=2)
                st.after(v.tensor_tensor(gs[:, :, :], pair[:, :, :, 0], pair[:, :, :, 1], ALU.add))
            elif part == 2:
                ranks(st, gs[:, :, :], G)
                st.after(v.tensor_scalar(gm[:, :, :], rk[:, :, 0:G], 3.5, -3.0e38, ALU.is_gt, ALU.mult))
                pair = sm[:, :, :].rearrange("p t (g a) -> p t g a", a=2)
                st.after(v.tensor_tensor(pair, pair, gm[:, :, :].rearrange("p t (g a) -> p t g a", a=1)
                                         .broadcast_to([TP, CT, G, 2]), ALU.add))
            elif part == 3:
                ranks(st, sm[:, :, :], E)
            else:
                st.after(v.tensor_scalar(rk[:, :, :], rk[:, :, :], 3.5, 2.5, ALU.is_lt, ALU.mult))
                dve.wait_ge(s["acc"], at(c, EA, -EA))
                v.tensor_tensor(w[:, k, :, 0:E], sc[:, :, :], rk[:, :, :], ALU.mult).then_inc(s["w"], 1)
                st.end()

        def first_sum(c, i, k):
            dve = nc.vector
            dve.wait_ge(s["front"], at(c, FS, 5))
            dve.wait_ge(s_out[k], i * 16)
            for n in range(2):
                ins = v.tensor_tensor(y[:, k, 2 * n:2 * n + 2, :],
                                      pF[0:TP, n, 0:2 * D].rearrange("p (t d) -> p t d", t=2),
                                      h[:, k, 2 * n:2 * n + 2, :], ALU.add)
            ins.then_inc(s["y0"], 1)

        @block.vector
        def _(dve):
            for n in ("stat", "lg", "w", "y0", "ac", "acc", "accv"):
                dve.sem_inc(s[n], CREDIT)
            dve.wait_ge(s_w, N_W)
            dve.wait_ge(s_id, 2)
            statistics(0, 0, 0)
            st = Steps(dve, s_ro, RP, 0)
            for part in range(5):
                route(0, 0, part, st)
            first_sum(0, 0, 0)

            def hidden(c, k, e):
                r = (e + k) % 2
                dve.wait_ge(s["su"], at(c, EA, e + 1))
                dve.wait_ge(s["dn"], at(c, EA, e - 1))
                v.scalar_tensor_tensor(ac[:, r, :], pG[:, r, 0:N], bc[:, 1, e:e + 1], su[:, r, :],
                                       ALU.add, ALU.mult).then_inc(s["ac"], 1)

            def weigh(c, k, e):
                dve.wait_ge(s["dn"], at(c, EA, e + 1))
                if e == 0:
                    dve.wait_ge(s["y0"], at(c, 1, 1))
                    dve.wait_ge(s["w"], at(c, 1, 1))
                else:
                    dve.wait_ge(s["acc"], at(c, EA, e))
                for t in range(CT):
                    yt = y[:, k, t, :]
                    ins = v.scalar_tensor_tensor(yt, pD[:, t // 2, (t % 2) * D:(t % 2 + 1) * D],
                                                 w[:, k, t, e:e + 1], yt, ALU.mult, ALU.add)
                ins.then_inc(s["acc"], 1)

            hidden(0, 0, 0)

            def body(c, i, k, last):
                st = Steps(dve, s_ro, RP, c + 1)
                for e in range(EA):
                    if e < EA - 1:
                        hidden(c, k, e + 1)
                    elif last < 2:
                        hidden(c + 1, 1 - k, 0)
                    weigh(c, k, e)
                    if last < 2:
                        if e == STAT_AT:
                            statistics(c + 1, i + k, 1 - k)
                        if e in ROUTE_AT:
                            route(c + 1, 1 - k, ROUTE_AT[e], st)
                        if FRONT_AT.get(e - 1) == 4:
                            first_sum(c + 1, i + k, 1 - k)

            two_a_turn(dve, NC, body)


def LN_SIGNALS():
    return 2 + RSQRT_STEPS + 1


def row_statistics(nc, st, go, rows, n, stats, mv, ve, rs, hh, nb_, eps, done):
    v = nc.vector
    for t in range(n):
        ins = v.bn_stats(stats[:, t, :], rows[:, t, :])
    st.after(ins)
    st.eng.sem_inc(go, 1)
    for t in range(n):
        ins = v.bn_aggr(mv[:, t, :], stats[:, t, :])
    st.after(ins)
    st.after(v.tensor_scalar(ve[:, :], mv[:, :, 1], eps, None, ALU.add))
    rsqrt(nc, st, rs[:, :], ve[:, :], hh[:, :])
    v.scalar_tensor_tensor(nb_[:, :], mv[:, :, 0], -1.0, rs[:, :], ALU.mult, ALU.mult).then_inc(done, 1)


MAGIC = 1.5 * 2.0 ** 23
NHD, HD, HG = 12, 16, 3
HP = 32


def quant_scale(nc, st, sc, inv, amax):
    st.after(nc.vector.tensor_scalar(sc, amax, 1.0 / 127.0, 1e-8, ALU.mult, ALU.max))
    st.after(nc.vector.reciprocal(inv, sc))


def attention_inputs(nc, ctx0, h2, w_qkv, b_qkv, w_proj, xn_d, xt_d, v_d, qk_d, vq_d, K):
    v, a = nc.vector, nc.scalar
    with ExitStack() as ctx:
        sb = lambda name, shape, dt=F32: ctx.enter_context(nc.sbuf_tensor("d_" + name, shape, dt))
        sem = semaphores(nc, ctx, "d_")
        ps = lambda name, shape, dt=F32: ctx.enter_context(nc.psum_tensor("d_" + name, shape, dt))
        h, xn = sb("h", [TP, 2, TT, D]), sb("xn", [TP, 2, TT, D])
        stats, mv = sb("stats", [TP, TT, 6]), sb("mv", [TP, TT, 2])
        ve, rs, hh, nb_ = (sb(n, [TP, TT]) for n in ("ve", "rs", "hh", "nb"))
        m1 = sb("m1", [TP, 1])
        wq_n, wp_n = sb("wq_n", [KC, 6, D]), sb("wp_n", [KC, 2, D])
        wq_b, wp_b = sb("wq_b", [KC, 6, D], BF16), sb("wp_b", [KC, 2, NHD, HP], BF16)
        identf = sb("identf", [128, 128])
        pT = ps("pT", [128, 2, 1024], BF16)
        s_w, s_v, s_v2, s_go, s_id0, s_id, s_all, s_t, s_tc, s_m0, s_gs = (sem(n) for n in (
            "s_w", "s_v", "s_v2", "s_go", "s_id0", "s_id", "s_all", "s_t", "s_tc", "s_m0", "s_gs"))
        s_h = [sem(f"s_h{k}") for k in range(2)]
        s_out = [sem(f"s_out{k}") for k in range(2)]
        s = {n: sem("q_" + n) for n in ("stat", "xn", "max")}
        block = ctx.enter_context(nc.Block())
        rows = lambda x, b: x[bass.ds(b * S, S), :].rearrange("(t p) d -> p t d", p=TP)
        PER = LN_SIGNALS() + 1

        @block.sync
        def _(sp):
            sp.dma_start(wq_n[:, :, :], w_qkv.rearrange("(r p) c -> p r c", p=KC)).then_inc(s_w, 16)
            sp.dma_start(wp_n[:, :, :], w_proj.rearrange("(r p) c -> p r c", p=KC)).then_inc(s_w, 16)
            sp.wait_ge(s_id0, 6)
            for j in range(4):
                src = b_qkv[0:2 * D].rearrange("(g j d) -> j d g", j=4, d=HD)[j]
                sp.dma_start(K["bqk"][HP * j:HP * j + HD, :], src, allow_slow_non_contiguous=True).then_inc(K["s_b"], 16)
            sp.dma_start(K["bv"][:, :], b_qkv[2 * D:3 * D].rearrange("(a d) -> a d", a=1).broadcast_to([TP, D]))\
                .then_inc(s_w, 16)

            def store(b, k):
                sp.wait_ge(s["xn"], at(b, 1, 1))
                sp.sem_inc(s_gs, 1)
                sp.dma_start(xn_d[b], xn[:, k, :, :].rearrange("p t d -> p (t d)")).then_inc(s_out[k], 16)

            sp.dma_start(h[:, 0, :, :], rows(h2, 0)).then_inc(s_h[0], 16)
            sp.dma_start(h[:, 1, :, :], rows(h2, 1)).then_inc(s_h[1], 16)

            def turn(b, i, k, last):
                store(b, k)
                if not last:
                    sp.dma_start(h[:, k, :, :], rows(h2, b + 2)).then_inc(s_h[k], 16)

            two_a_turn(sp, NB, turn)
            for k in range(2):
                sp.wait_ge(s_out[k], 16 * (NB // 2))

        @block.gpsimd
        def _(pool):
            pool.memset(K["ident"][:, :], 0.0).then_inc(s_id0, 1)
            pool.memset(K["wT"][:, :, :], 0.0).then_inc(s_id0, 1)
            pool.memset(wp_b[:, :, :, :], 0.0).then_inc(s_id0, 1)
            pool.memset(K["bqk"][:, :], 0.0).then_inc(s_id0, 1)
            pool.memset(K["amax"][:, :], 0.0).then_inc(s_id0, 1)
            pool.memset(K["pad"][:, :, :], 0.0).then_inc(s_id0, 1)
            pool.wait_ge(s_id0, 6)
            pool.affine_select(out=K["ident"][:, :], in_=K["ident"][:, :], compare_op=ALU.not_equal, fill=1.0, base=0,
                               pattern=[[-1, 128]], channel_multiplier=1).then_inc(s_id, 1)
            pool.wait_ge(s_id, 1)
            pool.affine_select(out=K["pad"][:, :, :], in_=K["pad"][:, :, :], compare_op=ALU.not_equal, fill=1.0,
                               base=-HD, pattern=[[-HP, 4], [-1, 3]], channel_multiplier=1).then_inc(s_id, 1)
            pool.wait_ge(s_m0, 1)
            pool.partition_all_reduce(K["gmax"][:, 0:3], K["amax"][:, 0:3], 128, bass.bass_isa.ReduceOp.max)\
                .then_inc(s_all, 1)

        @block.scalar
        def _(act):
            act.sem_inc(s["xn"], CREDIT)

            def body(b, i, k, last):
                act.wait_ge(s["stat"], at(b, 1, 1))
                act.wait_ge(s["max"], at(b, 1, -1))
                act.wait_ge(s_out[k], i * 16)
                act.sem_inc(s_go, 1)
                for t in range(TT):
                    ins = act.activation(xn[:, k, t, :], h[:, k, t, :], ACT.Identity, bias=nb_[:, t:t + 1],
                                         scale=rs[:, t:t + 1])
                ins.then_inc(s["xn"], 1)

            two_a_turn(act, NB, body)

        @block.vector
        def _(dve):
            dve.sem_inc(s["stat"], CREDIT)
            dve.sem_inc(s["max"], CREDIT)
            dve.wait_ge(s_id0, 6)

            def stat(b, i, k):
                st = Steps(dve, s_v, PER, b)
                dve.wait_ge(s_h[k], i * 16 + 16)
                dve.wait_ge(s["xn"], at(b, 1, 0))
                row_statistics(nc, st, s_go, h[:, k, :, :], TT, stats, mv, ve, rs, hh, nb_, 1e-5, s["stat"])
                return st

            def body(b, i, k, last):
                st = stat(b, i, k)
                dve.wait_ge(s["xn"], at(b, 1, 1))
                st.after(v.tensor_reduce(m1[:, :], xn[:, k, :, :].rearrange("p t d -> p (t d)"), AX, ALU.max,
                                         apply_absolute_value=True))
                v.tensor_tensor(K["amax"][0:TP, 0:1], K["amax"][0:TP, 0:1], m1[:, :], ALU.max).then_inc(s["max"], 1)
                dve.wait_ge(s["max"], at(b, 1, 1))
                st.end()

            two_a_turn(dve, NB, body)
            dve.wait_ge(s_w, 48)
            st = Steps(dve, s_v2)
            st.counted(v.tensor_reduce(K["amax"][0:KC, 1:2], wq_n[:, :, :].rearrange("p r c -> p (r c)"), AX, ALU.max,
                                      apply_absolute_value=True))
            v.tensor_reduce(K["amax"][0:KC, 2:3], wp_n[:, :, :].rearrange("p r c -> p (r c)"), AX, ALU.max,
                            apply_absolute_value=True).then_inc(s_m0, 1)
            dve.wait_ge(s_all, 1)
            quant_scale(nc, st, K["sc"][:, 0:3], K["inv"][:, 0:3], K["gmax"][:, 0:3])
            st.after(v.tensor_scalar(wq_n[:, :, :], wq_n[:, :, :], K["inv"][0:KC, 1:2], MAGIC, ALU.mult, ALU.add))
            st.counted(v.tensor_scalar(wq_b[:, :, :], wq_n[:, :, :], -MAGIC, None, ALU.add))
            st.after(v.tensor_scalar(wp_n[:, :, :], wp_n[:, :, :], K["inv"][0:KC, 2:3], MAGIC, ALU.mult, ALU.add))
            for r in range(2):
                st.after(v.tensor_scalar(wp_b[:, r, :, 0:HD], wp_n[:, r, :].rearrange("p (h d) -> p h d", d=HD),
                                         -MAGIC, None, ALU.add))
            st.after(v.tensor_tensor(K["cq"][:, :], K["sc"][:, 0:1], K["sc"][:, 1:2], ALU.mult))
            dve.sem_inc(s_tc, 1)
            for c in range(KT):
                dve.wait_ge(s_t, c + 1)
                for r in range(4):
                    v.tensor_copy(K["wT"][:, c, r * 6 * HP:(r + 1) * 6 * HP].rearrange("p (h d) -> p h d", d=HP)[:, :, 0:HD],
                                  pT[0:KC, c, r * KC:(r + 1) * KC].rearrange("p (h d) -> p h d", d=HD))
                ins = v.tensor_copy(K["wvT"][:, c, :], pT[0:KC, c, 4 * KC:6 * KC])
            ins.then_inc(s_tc, 1)
            dve.wait_ge(s_t, 3)
            for g in range(HG):
                ins = v.tensor_copy(K["wpT"][:, g, :], pT[:, 0, g * D:(g + 1) * D])
            ins.then_inc(s_tc, 1)

        @block.tensor
        def _(pe):
            pe.wait_ge(s_tc, 1)
            pe.wait_ge(s_id, 1)
            for c in range(KT):
                for r in range(6):
                    ins = pe.transpose(pT[0:KC, c, r * KC:(r + 1) * KC], wq_b[:, r, c * KC:(c + 1) * KC],
                                       K["ident"][0:KC, 0:KC])
                ins.then_inc(s_t, 1)
            pe.wait_ge(s_tc, 2)
            wp = wp_b[:, :, :, :].rearrange("p r h d -> p r (h d)")
            for g in range(HG):
                for r in range(2):
                    ins = pe.transpose(pT[:, 0, g * D + r * KC:g * D + (r + 1) * KC], wp[:, r, g * 128:(g + 1) * 128],
                                       K["ident"][0:KC, 0:KC])
            ins.then_inc(s_t, 1)

    for again in range(2):
        with ExitStack() as ctx:
            pre = "ef"[again] + "_"
            sb = lambda name, shape, dt=F32: ctx.enter_context(nc.sbuf_tensor(pre + name, shape, dt))
            sem = semaphores(nc, ctx, pre)
            ps = lambda name, shape, dt=F32: ctx.enter_context(nc.psum_tensor(pre + name, shape, dt))
            x = sb("x", [TP, 2, TT * D])
            xr = sb("xr", [TP, 2, TT * D])
            xb = sb("xb", [TP, 2, TT * D], BF16)
            xT = sb("xT", [KC, 2, KT, S], BF16)
            vb = sb("vb", [TP, 2, TT, D])
            y = sb("y", [128, 2, S] if again == 0 else [128, 2, 6, S])
            qk = sb("qk", [128, 2, 6, S], BF16)
            vq = sb("vq", [TP, 2, TT, NHD, HP], BF16)
            mt = sb("mt", [128, 3])
            mtq = sb("mtq", [128, 6])
            pT = ps("pT", [KC, 2, 1024], BF16)
            pQ = ps("pQ", [128, 2, 1024])
            s_v, s_go, s_all, s_m0, s_k, s_gs = (sem(n) for n in ("s_v", "s_go", "s_all", "s_m0", "s_k", "s_gs"))
            s_x = [sem(f"s_x{k}") for k in range(2)]
            s_o1 = [sem(f"s_o1{k}") for k in range(2)]
            s_o2 = [sem(f"s_o2{k}") for k in range(2)]
            s = {n: sem("q_" + n) for n in ("xr", "xb", "tr", "xT", "qk", "y", "max", "vb", "vmax", "q")}
            block = ctx.enter_context(nc.Block())

            if again == 0:
                R = 8

                @block.sync
                def _(sp):
                    def body(b, i, k, last):
                        sp.wait_ge(s["xr"], at(b, 1, -1))
                        sp.sem_inc(s_gs, 1)
                        sp.dma_start(x[:, k, :], xn_d[b]).then_inc(s_x[k], 16)

                    def store(b, k):
                        sp.wait_ge(s["xT"], at(b, 1, 1))
                        sp.sem_inc(s_gs, 1)
                        sp.dma_start(xt_d[b], xT[:, k, :, :].rearrange("p c l -> p (c l)")).then_inc(s_o1[k], 16)
                        sp.wait_ge(s["vb"], at(b, 1, 1))
                        sp.sem_inc(s_gs, 1)
                        sp.dma_start(v_d[b], vb[:, k, :, :].rearrange("p t d -> p (t d)")).then_inc(s_o2[k], 16)

                    for k in range(2):
                        body(k, 0, k, 0)

                    def turn(b, i, k, last):
                        if not last:
                            body(b + 2, i + 1, k, 0)
                        store(b, k)

                    two_a_turn(sp, NB, turn)
                    for k in range(2):
                        sp.wait_ge(s_o1[k], 16 * (NB // 2))
                        sp.wait_ge(s_o2[k], 16 * (NB // 2))

                @block.gpsimd
                def _(pool):
                    pool.wait_ge(s_m0, 1)
                    pool.partition_all_reduce(K["gmax"][:, 3:6], K["amax"][:, 3:6], 128, bass.bass_isa.ReduceOp.max)\
                        .then_inc(s_all, 1)

                @block.tensor
                def _(pe):
                    for n in ("tr", "qk"):
                        pe.sem_inc(s[n], CREDIT)

                    def body(b, i, k, last):
                        pe.wait_ge(s["xb"], at(b, 1, 1))
                        pe.wait_ge(s["xT"], at(b, 1, 0))
                        for c in range(KT):
                            for t in range(TT):
                                ins = pe.transpose(pT[:, c, t * (TP + 1):t * (TP + 1) + TP],
                                                   xb[:, k, t * D + c * KC:t * D + (c + 1) * KC],
                                                   K["ident"][0:TP, 0:TP])
                        ins.then_inc(s["tr"], 1)
                        pe.wait_ge(s["xT"], at(b, 1, 1))
                        for r in range(R):
                            if r < 6:
                                pe.wait_ge(s["y"], at(b, 6, r - 1 if r >= 2 else 0))
                                if r < 2:
                                    pe.wait_ge(s["vmax"], at(b, 2, 0))
                                for lo, hi in ((0, 512), (512, S)):
                                    for c in range(KT):
                                        ins = pe.matmul(pQ[:, r % 2, lo:hi], K["wT"][:, c, r * 128:(r + 1) * 128],
                                                        xT[:, k, c, lo:hi], start=(c == 0), stop=(c == KT - 1))
                            else:
                                pe.wait_ge(s["y"], at(b, 6, r - 1))
                                for t in range(4 * (r - 6), min(4 * (r - 6) + 4, TT)):
                                    col = (t % 4) // 2 * 512 + t % 2 * D
                                    for c in range(KT):
                                        ins = pe.matmul(pQ[0:TP, r % 2, col:col + D],
                                                        xT[:, k, c, t * TP:(t + 1) * TP], K["wvT"][:, c, :],
                                                        start=(c == 0), stop=(c == KT - 1))
                            ins.then_inc(s["qk"], 1)

                    two_a_turn(pe, NB, body)

                @block.scalar
                def _(act):
                    for n in ("xT", "y"):
                        act.sem_inc(s[n], CREDIT)

                    def body(b, i, k, last):
                        act.wait_ge(s["tr"], at(b, 1, 1))
                        act.wait_ge(s_o1[k], i * 16)
                        act.wait_ge(s["qk"], at(b, R, -R))
                        for c in range(KT):
                            ins = act.activation(
                                xT[:, k, c, :].rearrange("p (t l) -> p t l", t=TT),
                                pT[:, c, 0:TT * (TP + 1)].rearrange("p (t l) -> p t l", t=TT)[:, :, 0:TP], ACT.Copy)
                        ins.then_inc(s["xT"], 1)
                        for r in range(6):
                            act.wait_ge(s["qk"], at(b, R, r + 1))
                            act.wait_ge(s["max"], at(b, 6, r - 1))
                            act.activation(y[:, r % 2, :], pQ[:, r % 2, 0:S], ACT.Identity,
                                           bias=K["bqk"][:, r:r + 1], scale=K["cq"][:, 0:1]).then_inc(s["y"], 1)

                    two_a_turn(act, NB, body)

                @block.vector
                def _(dve):
                    for n in ("xr", "xb", "max", "vb", "vmax"):
                        dve.sem_inc(s[n], CREDIT)
                    dve.wait_ge(K["s_b"], 64)
                    st0 = Steps(dve, s_k)

                    def integers(b, i, k):
                        dve.wait_ge(s_x[k], i * 16 + 16)
                        dve.wait_ge(s["xb"], at(b, 1, -1))
                        v.tensor_scalar(xr[:, k, :], x[:, k, :], K["inv"][0:TP, 0:1], MAGIC, ALU.mult, ALU.add)\
                            .then_inc(s["xr"], 1)
                        dve.wait_ge(s["xr"], at(b, 1, 1))
                        dve.wait_ge(s["tr"], at(b, 1, -1))
                        v.tensor_scalar(xb[:, k, :], xr[:, k, :], -MAGIC, None, ALU.add).then_inc(s["xb"], 1)

                    integers(0, 0, 0)

                    def body(b, i, k, last):
                        PER = 5
                        st = Steps(dve, s_v, PER, b)
                        for r in range(6):
                            dve.wait_ge(s["y"], at(b, 6, r + 1))
                            v.tensor_reduce(mtq[:, r:r + 1], y[:, r % 2, :], AX, ALU.max,
                                            apply_absolute_value=True).then_inc(s["max"], 1)
                            if r == 2 and last < 2:
                                integers(b + 1, i + k, 1 - k)
                        dve.wait_ge(s_o2[k], i * 16)
                        for r in range(2):
                            dve.wait_ge(s["qk"], at(b, R, 7 + r))
                            for n in range(2 if r == 0 else 1):
                                m = 2 if r == 0 else 1
                                ins = v.scalar_tensor_tensor(
                                    vb[:, k, 4 * r + 2 * n:4 * r + 2 * n + m, :],
                                    pQ[0:TP, r, n * 512:n * 512 + m * D].rearrange("p (t d) -> p t d", t=m),
                                    K["cq"][0:TP, 0:1],
                                    K["bv"][:, :].rearrange("p (a d) -> p a d", a=1).broadcast_to([TP, m, D]),
                                    ALU.mult, ALU.add)
                            ins.then_inc(s["vmax"], 1)
                        dve.wait_ge(s["vmax"], at(b, 2, 2))
                        dve.sem_inc(s["vb"], 1)
                        st.after(v.tensor_reduce(mt[0:TP, 2:3], vb[:, k, :, :].rearrange("p t d -> p (t d)"), AX,
                                                 ALU.max, apply_absolute_value=True))
                        dve.wait_ge(s["max"], at(b, 6, 6))
                        st.after(v.tensor_reduce(mt[:, 0:2], mtq[:, :].rearrange("p (a g) -> p a g", a=2), AX,
                                                 ALU.max))
                        st.after(v.tensor_tensor(K["amax"][:, 3:5], K["amax"][:, 3:5], mt[:, 0:2], ALU.max))
                        st.after(v.tensor_tensor(K["amax"][0:TP, 5:6], K["amax"][0:TP, 5:6], mt[0:TP, 2:3], ALU.max))
                        st.n += 1
                        dve.sem_inc(s_v, 1)
                        st.end()

                    two_a_turn(dve, NB, body)
                    dve.sem_inc(s_m0, 1)
                    dve.wait_ge(s_all, 1)
                    quant_scale(nc, st0, K["sc"][:, 3:6], K["inv"][:, 3:6], K["gmax"][:, 3:6])
                    for n in range(2):
                        st0.counted(v.tensor_tensor(K["cqi"][:, n:n + 1], K["cq"][:, :], K["inv"][:, 3 + n:4 + n],
                                                   ALU.mult))
                        st0.after(v.tensor_scalar(K["bqi"][:, 3 * n:3 * n + 3], K["bqk"][:, 3 * n:3 * n + 3],
                                                  K["inv"][:, 3 + n:4 + n], None, ALU.mult))
                    st0.after(v.tensor_reduce(K["padc"][:, :], K["pad"][:, :, :].rearrange("p j i -> p (j i)"), AX,
                                              ALU.add))
                    st0.after(v.tensor_scalar(K["bqi"][:, 3:6], K["bqi"][:, 3:6], K["padc"][:, 0:1], None, ALU.add))
                    st0.after(v.scalar_tensor_tensor(K["cs"][:, :], K["sc"][:, 3:4], HD ** -0.5, K["sc"][:, 4:5],
                                                     ALU.mult, ALU.mult))
                    st0.after(v.reciprocal(K["csi"][:, :], K["cs"][:, :]))
            else:
                @block.sync
                def _(sp):
                    def load(b, i, k):
                        sp.wait_ge(s["qk"], at(b, 6, -6))
                        sp.sem_inc(s_gs, 1)
                        sp.dma_start(xT[:, k, :, :].rearrange("p c l -> p (c l)"), xt_d[b]).then_inc(s_x[k], 16)
                        sp.wait_ge(s["vb"], at(b, 1, -1))
                        sp.sem_inc(s_gs, 1)
                        sp.dma_start(vb[:, k, :, :].rearrange("p t d -> p (t d)"), v_d[b]).then_inc(s_x[k], 16)

                    def turn(b, i, k, last):
                        if not last:
                            load(b + 2, i + 1, k)
                        sp.wait_ge(s["q"], at(b, 1, 1))
                        sp.sem_inc(s_gs, 1)
                        sp.dma_start(qk_d[b], qk[:, k, :, :].rearrange("p g l -> p (g l)")).then_inc(s_o1[k], 16)
                        sp.wait_ge(s["xb"], at(b, 1, 1))
                        sp.sem_inc(s_gs, 1)
                        sp.dma_start(vq_d[b], vq[:, k, :, :, :].rearrange("p t h d -> p (t h d)")).then_inc(s_o2[k], 16)

                    for k in range(2):
                        load(k, 0, k)
                    two_a_turn(sp, NB, turn)
                    for k in range(2):
                        sp.wait_ge(s_o1[k], 16 * (NB // 2))
                        sp.wait_ge(s_o2[k], 16 * (NB // 2))

                @block.gpsimd
                def _(pool):
                    pool.memset(vq[:, :, :, :, :], 0.0).then_inc(s_m0, 1)

                @block.tensor
                def _(pe):
                    pe.sem_inc(s["qk"], CREDIT)

                    def body(b, i, k, last):
                        pe.wait_ge(s_x[k], i * 32 + 32)
                        for r in range(6):
                            pe.wait_ge(s["y"], at(b, 6, r - 1))
                            for lo, hi in ((0, 512), (512, S)):
                                for c in range(KT):
                                    ins = pe.matmul(pQ[:, r % 2, lo:hi], K["wT"][:, c, r * 128:(r + 1) * 128],
                                                    xT[:, k, c, lo:hi], start=(c == 0), stop=(c == KT - 1))
                            ins.then_inc(s["qk"], 1)

                    two_a_turn(pe, NB, body)

                @block.scalar
                def _(act):
                    act.sem_inc(s["y"], CREDIT)

                    def body(b, i, k, last):
                        act.wait_ge(s["max"], at(b, 1, -1))
                        for r in range(6):
                            act.wait_ge(s["qk"], at(b, 6, r + 1))
                            act.activation(y[:, k, r, :], pQ[:, r % 2, 0:S], ACT.Identity,
                                           bias=K["bqi"][:, r:r + 1], scale=K["cqi"][:, r // 3:r // 3 + 1])\
                                .then_inc(s["y"], 1)

                    two_a_turn(act, NB, body)

                @block.vector
                def _(dve):
                    for n in ("max", "vb", "xb", "q"):
                        dve.sem_inc(s[n], CREDIT)
                    dve.wait_ge(s_m0, 1)

                    def body(b, i, k, last):
                        dve.wait_ge(s_x[k], i * 32 + 32)
                        dve.wait_ge(s["xb"], at(b, 1, -1))
                        v.tensor_scalar(xr[:, k, :], vb[:, k, :, :].rearrange("p t d -> p (t d)"),
                                        K["inv"][0:TP, 5:6], MAGIC, ALU.mult, ALU.add).then_inc(s["vb"], 1)
                        dve.wait_ge(s["vb"], at(b, 1, 1))
                        dve.wait_ge(s_o2[k], i * 16)
                        dve.sem_inc(s_go, 1)
                        v.tensor_scalar(vq[:, k, :, :, 0:HD].rearrange("p t h d -> p (t h) d"),
                                        xr[:, k, :].rearrange("p (t d) -> p t d", d=HD), -MAGIC, None,
                                        ALU.add).then_inc(s["xb"], 1)
                        dve.wait_ge(s["y"], at(b, 6, 6))
                        dve.wait_ge(s_o1[k], i * 16)
                        v.tensor_scalar(qk[:, k, :, :], y[:, k, :, :], MAGIC, -MAGIC, ALU.add, ALU.add)\
                            .then_inc(s["q"], 1)
                        dve.wait_ge(s["q"], at(b, 1, 1))
                        dve.sem_inc(s["max"], 1)

                    two_a_turn(dve, NB, body)


def attention(nc, h2, w_qkv, b_qkv, w_proj, b_proj, scratch, h3, until=9):
    with ExitStack() as ctx0:
        sb = lambda name, shape, dt=F32: ctx0.enter_context(nc.sbuf_tensor("k_" + name, shape, dt))
        K = {
            "ident": sb("ident", [128, 128], BF16), "pad": sb("pad", [128, 4, 3]), "padc": sb("padc", [128, 1]),
            "wT": sb("wT", [KC, KT, 2 * NHD * HP], BF16), "wvT": sb("wvT", [KC, KT, D], BF16),
            "wpT": sb("wpT", [128, HG, D], BF16), "bqk": sb("bqk", [128, 6]), "bqi": sb("bqi", [128, 6]),
            "bv": sb("bv", [TP, D]), "amax": sb("amax", [128, 8]), "gmax": sb("gmax", [128, 8]),
            "sc": sb("sc", [128, 8]), "inv": sb("inv", [128, 8]), "cq": sb("cq", [128, 1]),
            "cqi": sb("cqi", [128, 2]), "co": sb("co", [128, 3]), "cs": sb("cs", [128, 1]), "csi": sb("csi", [128, 1]),
            "s_b": ctx0.enter_context(nc.semaphore("k_s_b")),
        }
        attention_inputs(nc, ctx0, h2, w_qkv, b_qkv, w_proj, scratch["xn"], scratch["xt"], scratch["v"],
                         scratch["qk"], scratch["vq"], K)
        if until >= 1:
            attention_heads(nc, scratch, K, b_proj, h2, h3)


def attention_heads(nc, scratch, K, b_proj, h2, h3):
    v = nc.vector
    NQ = NHD * TT
    MAXR = bass.bass_isa.ReduceOp.max
    with ExitStack() as ctx:
        sb = lambda name, shape, dt=F32: ctx.enter_context(nc.sbuf_tensor("g_" + name, shape, dt))
        sem = semaphores(nc, ctx, "g_")
        RING = 4
        qk = sb("qk", [128, 2, 6, S], BF16)
        junk = sb("junk", [TP, 2, S], BF16)
        csn = sb("csn", [TP, 1])
        stt = sb("stt", [TP, 2, 2, NQ])
        low, m1 = sb("low", [TP, 1]), sb("m1", [TP, 1])
        pS = ctx.enter_context(nc.psum_tensor("g_pS", [TP, RING, 1024], F32))
        s_m0, s_all, s_v, s_go, s_i, s_c = (sem(n) for n in ("s_m0", "s_all", "s_v", "s_go", "s_i", "s_c"))
        s_q = [sem(f"s_q{k}") for k in range(2)]
        s_o = [sem(f"s_o{k}") for k in range(2)]
        s = {n: sem("q_" + n) for n in ("S", "mn", "exp", "min")}
        block = ctx.enter_context(nc.Block())

        @block.sync
        def _(sp):
            def load(b, i, k):
                sp.wait_ge(s["S"], at(b, NQ, -NQ))
                sp.sem_inc(s_go, 1)
                sp.dma_start(qk[:, k, :, :].rearrange("p g l -> p (g l)"), scratch["qk"][b]).then_inc(s_q[k], 16)

            def turn(b, i, k, last):
                if not last:
                    load(b + 2, i + 1, k)
                sp.wait_ge(s["exp"], at(b, NQ, NQ))
                sp.sem_inc(s_go, 1)
                sp.dma_start(scratch["st"][b], stt[:, k, :, :].rearrange("p a q -> p (a q)")).then_inc(s_o[k], 16)

            for k in range(2):
                load(k, 0, k)
            two_a_turn(sp, NB, turn)
            for k in range(2):
                sp.wait_ge(s_o[k], 16 * (NB // 2))

        @block.gpsimd
        def _(pool):
            pool.memset(low[:, :], 3.0e38).then_inc(s_i, 1)
            pool.memset(stt[:, :, :, :], 3.0e38).then_inc(s_i, 1)
            pool.wait_ge(s_m0, 1)
            pool.partition_all_reduce(K["gmax"][:, 6:7], K["amax"][:, 6:7], 128, MAXR).then_inc(s_all, 1)

        @block.tensor
        def _(pe):
            pe.sem_inc(s["S"], CREDIT)

            def body(b, i, k, last):
                pe.wait_ge(s_q[k], i * 16 + 16)
                for q in range(NQ):
                    pe.wait_ge(s["exp"], at(b, NQ, q + 1 - RING))
                    g, t, j = q // 20, q // 4 % 5, q % 4
                    at_ = slice(HP * j, HP * j + HD)
                    for lo, hi in ((0, 512), (512, S)):
                        ins = pe.matmul(pS[:, q % RING, lo:hi], qk[at_, k, g, t * TP:(t + 1) * TP],
                                        qk[at_, k, 3 + g, lo:hi], start=True, stop=True)
                    ins.then_inc(s["S"], 1)

            two_a_turn(pe, NB, body)

        @block.scalar
        def _(act):
            act.sem_inc(s["exp"], CREDIT)
            act.wait_ge(s_i, 2)

            def body(b, i, k, last):
                act.wait_ge(s_o[k], i * 16)
                act.wait_ge(s["min"], at(b, 1, 0))
                for q in range(NQ):
                    act.wait_ge(s["mn"], at(b, NQ, q + 1))
                    x = pS[:, q % RING, 0:S]
                    nc.scalar.activation(x, x, ACT.Exp, bias=stt[:, k, 0, q:q + 1], scale=K["cs"][0:TP, 0:1],
                                         accum_out=stt[:, k, 1, q:q + 1]).then_inc(s["exp"], 1)

            two_a_turn(act, NB, body)

        @block.vector
        def _(dve):
            for n in ("mn", "min"):
                dve.sem_inc(s[n], CREDIT)
            dve.wait_ge(s_i, 2)
            v.tensor_scalar(csn[:, :], K["cs"][0:TP, 0:1], -1.0, None, ALU.mult).then_inc(s_c, 1)
            dve.wait_ge(s_c, 1)

            def lowest(b, k):
                st = Steps(dve, s_v, 1, b + 1)
                dve.wait_ge(s["exp"], at(b, NQ, NQ))
                st.after(v.tensor_reduce(m1[:, :], stt[:, k, 1, :], AX, ALU.min))
                v.tensor_tensor(low[:, :], low[:, :], m1[:, :], ALU.min).then_inc(s["min"], 1)
                dve.wait_ge(s["min"], at(b, 1, 2))

            def body(b, i, k, last):
                dve.wait_ge(s_o[k], i * 16)
                for q in range(NQ):
                    dve.wait_ge(s["S"], at(b, NQ, q + 1))
                    dve.wait_ge(s["mn"], at(b, NQ, q - 1))
                    v.tensor_scalar(junk[:, q % 2, :], pS[:, q % RING, 0:S], csn[:, 0:1], 3.0e38, ALU.mult, ALU.min,
                                    accum_out=stt[:, k, 0, q:q + 1]).then_inc(s["mn"], 1)
                    if q == 6:
                        lowest(b - 1, 1 - k)

            two_a_turn(dve, NB, body)
            lowest(NB - 1, 1)
            st = Steps(dve, s_go)
            v.reciprocal(K["amax"][0:TP, 6:7], low[:, :]).then_inc(s_m0, 1)
            dve.wait_ge(s_all, 1)
            st2 = Steps(dve, s_v, 1, NB + 1)
            quant_scale(nc, st2, K["sc"][:, 6:7], K["inv"][:, 6:7], K["gmax"][:, 6:7])

    with ExitStack() as ctx:
        sb = lambda name, shape, dt=F32: ctx.enter_context(nc.sbuf_tensor("h_" + name, shape, dt))
        sem = semaphores(nc, ctx, "h_")
        RING = 4
        qk = sb("qk", [128, 2, 6, S], BF16)
        vq = sb("vq", [TP, 2, TT, NHD, HP], BF16)
        stt = sb("stt", [TP, NB, 2, NQ])
        ln, r1 = sb("ln", [TP, NB, NQ]), sb("r1", [TP, NQ])
        A = sb("A", [TP, HG, TT, 4, HP], BF16)
        ex = sb("ex", [TP, RING, S])
        pr = sb("pr", [TP, RING, S], BF16)
        oT = sb("oT", [128, 2, HG, S])
        om = sb("om", [128, 1])
        pS = ctx.enter_context(nc.psum_tensor("h_pS", [128, 3, 1024], F32))
        pO = ctx.enter_context(nc.psum_tensor("h_pO", [128, 1024], F32))
        s_m0, s_all, s_v, s_go, s_i, s_om, s_st, s_ln, s_a = (sem(n) for n in (
            "s_m0", "s_all", "s_v", "s_go", "s_i", "s_om", "s_st", "s_ln", "s_a"))
        s_in = [sem(f"s_in{k}") for k in range(2)]
        s_o = [sem(f"s_o{k}") for k in range(2)]
        s = {n: sem("q_" + n) for n in ("A", "T", "qa", "S", "E", "P", "AV", "ev", "om")}
        block = ctx.enter_context(nc.Block())

        SEQ = []
        for u in range(NQ):
            SEQ.append(("tile", u))
            if u in (19, 34, 49):
                SEQ.append(("rows", (19, 34, 49).index(u)))
        L = len(SEQ)
        assert L % 3 == 0

        @block.sync
        def _(sp):
            def load(b, i, k):
                sp.wait_ge(s["AV"], at(b, NQ, -NQ))
                sp.sem_inc(s_go, 1)
                sp.dma_start(qk[:, k, :, :].rearrange("p g l -> p (g l)"), scratch["qk"][b]).then_inc(s_in[k], 16)
                sp.dma_start(vq[:, k, :, :, :].rearrange("p t h d -> p (t h d)"), scratch["vq"][b])\
                    .then_inc(s_in[k], 16)

            def turn(b, i, k, last):
                sp.wait_ge(s["om"], at(b, 1, 1))
                sp.sem_inc(s_go, 1)
                sp.dma_start(scratch["o"][b], oT[:, k, :, :].rearrange("p g l -> p (g l)")).then_inc(s_o[k], 16)
                if not last:
                    load(b + 2, i + 1, k)

            sp.dma_start(stt[:, :, :, :].rearrange("p b a q -> p b (a q)"), scratch["st"].rearrange("b p q -> p b q"))\
                .then_inc(s_st, 16)
            for k in range(2):
                load(k, 0, k)
            two_a_turn(sp, NB, turn)
            for k in range(2):
                sp.wait_ge(s_o[k], 16 * (NB // 2))

        @block.gpsimd
        def _(pool):
            pool.memset(A[:, :, :, :, :], 0.0).then_inc(s_i, 1)
            pool.wait_ge(s_m0, 1)
            pool.partition_all_reduce(K["gmax"][:, 7:8], K["amax"][:, 7:8], 128, MAXR).then_inc(s_all, 1)

        @block.tensor
        def _(pe):
            for n in ("T", "S", "AV"):
                pe.sem_inc(s[n], CREDIT)

            def transpose_rows(b, slot, g):
                pe.wait_ge(s["A"], at(b, 1, 1))
                out = pS[:, slot, :].bitcast(BF16)
                for t in range(TT):
                    ins = pe.transpose(out[:, t * (TP + 1):t * (TP + 1) + TP],
                                       A[:, g, t, :, :].rearrange("p j e -> p (j e)"), K["ident"][0:TP, 0:TP])
                ins.then_inc(s["T"], 1)

            def user(pos, last):
                p = pos - 3
                while p >= 0 and last and SEQ[p][0] == "rows":
                    p -= 3
                return (SEQ[p], False) if p >= 0 else (SEQ[p + L], True)

            def fill(b, i, k, pos, last):
                (kind, n), before = user(pos, last)
                assert not (before and kind == "rows")
                if kind == "tile":
                    pe.wait_ge(s["E"], at(b, NQ, n + 1 - (NQ if before else 0)))
                else:
                    pe.wait_ge(s["qa"], at(b, 3, 3 + n + 1))
                kind, n = SEQ[pos]
                if kind == "rows":
                    transpose_rows(b + 1, pos % 3, n)
                    return
                g, j, m = n // 20, n // 5 % 4, n % 5
                if n == 0:
                    pe.wait_ge(s_in[k], i * 32 + 32)
                    pe.wait_ge(s["qa"], at(b, 3, 3))
                at_ = slice(HP * j, HP * j + HD + 3)
                for lo, hi in ((0, 512), (512, S)):
                    ins = pe.matmul(pS[0:TP, pos % 3, lo:hi], qk[at_, k, 3 + g, m * TP:(m + 1) * TP],
                                    qk[at_, k, g, lo:hi], start=True, stop=True)
                ins.then_inc(s["S"], 1)

            def combine(b, k, u):
                g, j, m = u // 20, u // 5 % 4, u % 5
                pe.wait_ge(s["P"], at(b, NQ, u + 1))
                if u % 20 == 0:
                    pe.wait_ge(s["ev"], at(b, 3, g))
                for lo, hi in ((0, 512), (512, S)):
                    ins = pe.matmul(pO[HP * j:HP * j + HP, lo:hi], vq[:, k, m, 4 * g + j, :],
                                    pr[:, u % RING, lo:hi], start=(m == 0), stop=(m == TT - 1),
                                    skip_group_check=True)
                ins.then_inc(s["AV"], 1)

            pe.wait_ge(s_in[0], 32)
            for g in range(3):
                transpose_rows(0, g, g)
            pe.wait_ge(s["qa"], at(0, 3, 3))
            for pos in range(2):
                fill(0, 0, 0, pos, False)

            def body(b, i, k, last):
                for pos in range(L):
                    nxt = pos + 2
                    if nxt < L:
                        if not (last == 2 and SEQ[nxt][0] == "rows"):
                            fill(b, i, k, nxt, last == 2)
                    elif last < 2:
                        fill(b + 1, i + k, 1 - k, nxt - L, last == 1)
                    if pos > 0 and SEQ[pos - 1][0] == "tile":
                        combine(b, k, SEQ[pos - 1][1])
                combine(b, k, NQ - 1)

            two_a_turn(pe, NB, body)

        @block.scalar
        def _(act):
            act.sem_inc(s["E"], CREDIT)
            act.wait_ge(s_st, 16)
            nc.scalar.activation(ln[:, :, :], stt[:, :, 1, :], ACT.Ln, scale=K["sc"][0:TP, 6:7]).then_inc(s_ln, 1)

            def body(b, i, k, last):
                for u in range(NQ):
                    act.wait_ge(s["S"], at(b, NQ, u + 1))
                    act.wait_ge(s["P"], at(b, NQ, u + 1 - RING))
                    slot = SEQ.index(("tile", u)) % 3
                    nc.scalar.activation(ex[:, u % RING, :], pS[0:TP, slot, 0:S], ACT.Exp,
                                         scale=K["cs"][0:TP, 0:1]).then_inc(s["E"], 1)

            two_a_turn(act, NB, body)

        @block.vector
        def _(dve):
            for n in ("A", "qa", "P", "ev", "om"):
                dve.sem_inc(s[n], CREDIT)
            dve.wait_ge(s_i, 1)

            def constants(b, i, k):
                st = Steps(dve, s_v, 3, b)
                flat = A[:, :, :, :, :].rearrange("p g t j e -> p (g t j) e")
                a1 = ln[:, bass.ds(b, 1), :].rearrange("p a q -> p (a q)")
                dve.wait_ge(s["T"], at(b, 3, 0))
                dve.sem_inc(s_go, 1)
                st.after(v.tensor_copy(flat[:, :, HD], a1))
                dve.sem_inc(s_go, 1)
                st.after(v.tensor_tensor(r1[:, :], a1, flat[:, :, HD], ALU.subtract))
                st.after(v.tensor_copy(flat[:, :, HD + 1], r1[:, :]))
                v.tensor_tensor(flat[:, :, HD + 2], r1[:, :], flat[:, :, HD + 1], ALU.subtract).then_inc(s["A"], 1)

            def add_rows(b, i, k, g, slot):
                dve.wait_ge(s["T"], at(b, 3, g + 1))
                if g == 0:
                    dve.wait_ge(s_in[k], i * 32 + 32)
                x = qk[:, k, g, :].rearrange("p (t l) -> p t l", t=TT)
                rows = pS[:, slot, :].bitcast(BF16)[:, 0:TT * (TP + 1)].rearrange("p (t l) -> p t l", t=TT)[:, :, 0:TP]
                v.tensor_tensor(x, x, rows, ALU.add).then_inc(s["qa"], 1)

            dve.wait_ge(s_ln, 1)
            v.tensor_tensor(ln[:, :, :], stt[:, :, 0, :], ln[:, :, :], ALU.subtract).then_inc(s_a, 1)
            dve.wait_ge(s_a, 1)
            v.tensor_scalar(ln[:, :, :], ln[:, :, :], K["csi"][0:TP, 0:1], None, ALU.mult).then_inc(s_a, 1)
            dve.wait_ge(s_a, 2)
            constants(0, 0, 0)
            for g in range(3):
                add_rows(0, 0, 0, g, g)

            def body(b, i, k, last):
                for pos, (kind, n) in enumerate(SEQ):
                    if kind == "rows":
                        if last < 2:
                            add_rows(b + 1, i + k, 1 - k, n, pos % 3)
                        continue
                    u = n
                    dve.wait_ge(s["E"], at(b, NQ, u + 1))
                    dve.wait_ge(s["AV"], at(b, NQ, u + 1 - RING))
                    v.tensor_scalar(pr[:, u % RING, :], ex[:, u % RING, :], MAGIC, -MAGIC, ALU.add, ALU.add)\
                        .then_inc(s["P"], 1)
                    if u == 12 and last < 2:
                        constants(b + 1, i + k, 1 - k)
                    if u % 20 == 19:
                        g = u // 20
                        dve.wait_ge(s["AV"], at(b, NQ, u + 1))
                        if g == 0:
                            dve.wait_ge(s_o[k], i * 16)
                        v.tensor_copy(oT[:, k, g, :], pO[:, 0:S]).then_inc(s["ev"], 1)
                dve.wait_ge(s["ev"], at(b, 3, 3))
                v.tensor_reduce(om[:, :], oT[:, k, :, :].rearrange("p g l -> p (g l)"), AX, ALU.max,
                                apply_absolute_value=True).then_inc(s_om, 1)
                dve.wait_ge(s_om, b + 1)
                v.tensor_tensor(K["amax"][:, 7:8], K["amax"][:, 7:8], om[:, :], ALU.max).then_inc(s["om"], 1)
                dve.wait_ge(s["om"], at(b, 1, 1))

            two_a_turn(dve, NB, body)
            dve.sem_inc(s_m0, 1)
            dve.wait_ge(s_all, 1)
            st = Steps(dve, s_v, 3, NB)
            st.after(v.tensor_tensor(K["co"][:, 0:1], K["sc"][:, 6:7], K["sc"][:, 5:6], ALU.mult))
            st.after(v.tensor_tensor(K["gmax"][:, 7:8], K["gmax"][:, 7:8], K["co"][:, 0:1], ALU.mult))
            quant_scale(nc, st, K["sc"][:, 7:8], K["inv"][:, 7:8], K["gmax"][:, 7:8])
            st.after(v.tensor_tensor(K["co"][:, 1:2], K["co"][:, 0:1], K["inv"][:, 7:8], ALU.mult))
            st.after(v.tensor_tensor(K["co"][:, 2:3], K["sc"][:, 7:8], K["sc"][:, 2:3], ALU.mult))

    with ExitStack() as ctx:
        sb = lambda name, shape, dt=F32: ctx.enter_context(nc.sbuf_tensor("i_" + name, shape, dt))
        sem = semaphores(nc, ctx, "i_")
        o, orr = sb("o", [128, 2, HG * S]), sb("orr", [128, 2, HG * S])
        oq = sb("oq", [128, 2, HG, S], BF16)
        h, hb, y = sb("h", [TP, 2, TT, D]), sb("hb", [TP, 2, TT, D]), sb("y", [TP, 2, TT, D])
        bp, mg = sb("bp", [TP, D]), sb("mg", [128, 1])
        pY = ctx.enter_context(nc.psum_tensor("i_pY", [TP, 2, 4, 512], F32))
        s_w, s_go, s_m = sem("s_w"), sem("s_go"), sem("s_m")
        s_in = [sem(f"s_in{k}") for k in range(2)]
        s_h = [sem(f"s_h{k}") for k in range(2)]
        s_o = [sem(f"s_o{k}") for k in range(2)]
        s = {n: sem("q_" + n) for n in ("hb", "rr", "oq", "Y", "y")}
        block = ctx.enter_context(nc.Block())
        rows = lambda x, b: x[bass.ds(b * S, S), :].rearrange("(t p) d -> p t d", p=TP)

        @block.sync
        def _(sp):
            sp.dma_start(bp[:, :], b_proj.rearrange("(a d) -> a d", a=1).broadcast_to([TP, D])).then_inc(s_w, 16)

            def load(b, i, k):
                sp.wait_ge(s["rr"], at(b, 1, -1))
                sp.wait_ge(s["hb"], at(b, 1, -1))
                sp.sem_inc(s_go, 1)
                sp.dma_start(o[:, k, :], scratch["o"][b]).then_inc(s_in[k], 16)
                sp.dma_start(h[:, k, :, :], rows(h2, b)).then_inc(s_h[k], 16)

            def turn(b, i, k, last):
                if not last:
                    load(b + 2, i + 1, k)
                sp.wait_ge(s["y"], at(b, 1, 1))
                sp.sem_inc(s_go, 1)
                sp.dma_start(rows(h3, b), y[:, k, :, :]).then_inc(s_o[k], 16)

            for k in range(2):
                load(k, 0, k)
            two_a_turn(sp, NB, turn)
            for k in range(2):
                sp.wait_ge(s_o[k], 16 * (NB // 2))

        @block.gpsimd
        def _(pool):
            pool.sem_inc(s["hb"], CREDIT)
            pool.memset(mg[:, :], MAGIC).then_inc(s_m, 1)
            pool.wait_ge(s_w, 16)

            def body(b, i, k, last):
                pool.wait_ge(s_h[k], i * 16 + 16)
                pool.wait_ge(s["y"], at(b, 1, -1))
                pool.tensor_tensor(hb[:, k, :, :], h[:, k, :, :],
                                   bp[:, :].rearrange("p (a d) -> p a d", a=1).broadcast_to([TP, TT, D]),
                                   ALU.add).then_inc(s["hb"], 1)

            two_a_turn(pool, NB, body)

        @block.scalar
        def _(act):
            act.sem_inc(s["rr"], CREDIT)
            act.wait_ge(s_m, 1)

            def body(b, i, k, last):
                act.wait_ge(s_in[k], i * 16 + 16)
                act.wait_ge(s["oq"], at(b, 1, -1))
                nc.scalar.activation(orr[:, k, :], o[:, k, :], ACT.Identity, bias=mg[:, 0:1],
                                     scale=K["co"][:, 1:2]).then_inc(s["rr"], 1)

            two_a_turn(act, NB, body)

        @block.tensor
        def _(pe):
            pe.sem_inc(s["Y"], CREDIT)

            def body(b, i, k, last):
                pe.wait_ge(s["oq"], at(b, 1, 1))
                pe.wait_ge(s["y"], at(b, 1, -1))
                for t in range(TT):
                    for g in range(HG):
                        ins = pe.matmul(pY[:, k, t // 2, t % 2 * D:(t % 2 + 1) * D], oq[:, k, g, t * TP:(t + 1) * TP],
                                        K["wpT"][:, g, :], start=(g == 0), stop=(g == HG - 1))
                ins.then_inc(s["Y"], 1)

            two_a_turn(pe, NB, body)

        @block.vector
        def _(dve):
            for n in ("oq", "y"):
                dve.sem_inc(s[n], CREDIT)

            def integers(b, i, k):
                dve.wait_ge(s["rr"], at(b, 1, 1))
                dve.wait_ge(s["Y"], at(b, 1, -1))
                v.tensor_scalar(oq[:, k, :, :].rearrange("p g l -> p (g l)"), orr[:, k, :], -MAGIC, None, ALU.add)\
                    .then_inc(s["oq"], 1)

            integers(0, 0, 0)

            def body(b, i, k, last):
                if last < 2:
                    integers(b + 1, i + k, 1 - k)
                dve.wait_ge(s["Y"], at(b, 1, 1))
                dve.wait_ge(s["hb"], at(b, 1, 1))
                dve.wait_ge(s_o[k], i * 16)
                for c in range(3):
                    n = 2 if c < 2 else 1
                    ins = v.scalar_tensor_tensor(y[:, k, 2 * c:2 * c + n, :],
                                                 pY[:, k, c, 0:n * D].rearrange("p (t d) -> p t d", t=n),
                                                 K["co"][0:TP, 2:3], hb[:, k, 2 * c:2 * c + n, :], ALU.mult, ALU.add)
                ins.then_inc(s["y"], 1)

            two_a_turn(dve, NB, body)


def switch_experts(nc, h3, ln_w, w_router, wi, wo, slot_x, slot_y, out):
    E, F, CAP = 16, 768, 64
    FT = F // 128
    NT = NB * TT
    SLOTS = E * NB * CAP
    EPS1, EPS2 = 1e-5, 1e-6
    v = nc.vector
    with ExitStack() as keep:
        sbk = lambda name, shape, dt=F32: keep.enter_context(nc.sbuf_tensor("m_" + name, shape, dt))
        ident = sbk("ident", [128, 128])
        base = sbk("base", [TP, NT, D])
        nrm = sbk("nrm", [TP, NT, D])
        prob = sbk("prob", [TP, NT])
        dest = sbk("dest", [TP, NT], U32)

        with ExitStack() as ctx:
            sb = lambda name, shape, dt=F32: ctx.enter_context(nc.sbuf_tensor("n_" + name, shape, dt))
            ps = lambda name, shape: ctx.enter_context(nc.psum_tensor("n_" + name, shape, F32))
            sem = semaphores(nc, ctx, "n_")
            ZW = 3072
            zero = sb("zero", [128, ZW])
            lnw, wr = sb("lnw", [TP, D]), sb("wr", [KC, KT, E])
            tri, ones = sb("tri", [TP, TP], BF16), sb("ones", [TP, TP], BF16)
            desc = sb("desc", [TP, E])
            stats, mv = sb("stats", [TP, TT, 6]), sb("mv", [TP, TT, 2])
            ve, rs, hh, nb_ = (sb(n, [TP, 2, TT]) for n in ("ve", "rs", "hh", "nb"))
            xs = sb("xs", [TP, TT, D])
            nx = sb("nx", [TP, 2, TT, D])
            xT = sb("xT", [KC, 2 * TT, TP])
            eq, lg, ex, pr = (sb(n, [TP, TT, E]) for n in ("eq", "lg", "ex", "pr"))
            oh = sb("oh", [TP, TT, E], BF16)
            mx, first, sums, place, over, slot = (sb(n, [TP, TT]) for n in ("mx", "first", "sums", "place", "over", "slot"))
            sbase = sb("sbase", [TP, 1])
            to = sb("to", [TP, 2, TT], U32)
            pT = ps("pT", [KC, 3, 512])
            pL, pC = ps("pL", [TP, TT, E]), ps("pC", [TP, TT, E])
            SLOT_OF = [(n // 4, (n % 4) * TP) for n in range(2 * TT)]

            s_z0, s_zero, s_w, s_i0, s_i, s_go, s_dv = (sem(n) for n in (
                "s_z0", "s_zero", "s_w", "s_i0", "s_i", "s_go", "s_dv"))
            s_sc = [sem(f"s_sc{k}") for k in range(2)]
            s_ro = sem("s_ro")
            VS, VR = 4 + RSQRT_STEPS, 12
            s_h = [sem(f"s_h{k}") for k in range(2)]
            s = {n: sem("q_" + n) for n in ("stat", "xs", "nrm", "bas", "T", "xT", "L", "lg", "ex", "oh", "cum", "dest")}
            block = ctx.enter_context(nc.Block())

            @block.sync
            def _(sp):
                for k in range(2):
                    sp.dma_start(base[:, k * TT:(k + 1) * TT, :], h3[k * S:(k + 1) * S, :].rearrange(
                        "(t p) d -> p t d", p=TP)).then_inc(s_h[k], 16)
                sp.dma_start(lnw[:, :], ln_w.rearrange("(a d) -> a d", a=1).broadcast_to([TP, D])).then_inc(s_w, 16)
                sp.dma_start(wr[:, :, :], w_router.rearrange("(c p) e -> p c e", p=KC)).then_inc(s_w, 16)
                sp.wait_ge(s_z0, 1)
                for n in range(SLOTS * D // (128 * ZW)):
                    rows = 128 * ZW // D
                    sp.dma_start(slot_x[n * rows:(n + 1) * rows, :].rearrange("(p r) d -> p (r d)", p=128),
                                 zero[:, :]).then_inc(s_zero, 16)

                def body(c, i, k, last):
                    if not last:
                        sp.wait_ge(s["stat"], at(c, 1, 1))
                        sp.sem_inc(s_go, 1)
                        sp.dma_start(base[:, bass.ds(c * TT + 2 * TT, TT), :],
                                     h3[bass.ds(c * S + 2 * S, S), :].rearrange("(t p) d -> p t d", p=TP))\
                            .then_inc(s_h[k], 16)

                two_a_turn(sp, NB, body)

            @block.gpsimd
            def _(pool):
                pool.memset(zero[:, :], 0.0).then_inc(s_z0, 1)
                pool.memset(ident[:, :], 0.0).then_inc(s_i0, 1)
                pool.memset(tri[:, :], 1.0).then_inc(s_i0, 1)
                pool.memset(ones[:, :], 1.0).then_inc(s_i0, 1)
                for e in range(E):
                    pool.memset(desc[:, e:e + 1], float(E - e)).then_inc(s_i0, 1)
                pool.wait_ge(s_i0, 3 + E)
                pool.affine_select(out=ident[:, :], in_=ident[:, :], compare_op=ALU.not_equal, fill=1.0, base=0,
                                   pattern=[[-1, 128]], channel_multiplier=1).then_inc(s_i, 1)
                pool.wait_ge(s_i, 1)
                pool.affine_select(out=tri[:, :], in_=tri[:, :], compare_op=ALU.is_ge, fill=0.0, base=0,
                                   pattern=[[1, TP]], channel_multiplier=-1).then_inc(s_i, 1)
                last_slot = pool.to_reg(SLOTS - 1)
                pool.wait_ge(s_zero, 16 * (SLOTS * D // (128 * ZW)))

                def body(c, i, k, last):
                    pool.wait_ge(s["dest"], at(c, 1, 1))
                    pool.sem_inc(s_go, 1)
                    for t in range(TT):
                        pool.indirect_dma_start(slot_x, bass.IndirectOffsetOnAxis(ap=to[:, k, t:t + 1], axis=0),
                                                nx[:, k, t, :], None,
                                                bounds_check=last_slot, oob_is_err=False).then_inc(s_sc[k], 16)

                two_a_turn(pool, NB, body)
                for k in range(2):
                    pool.wait_ge(s_sc[k], 16 * TT * (NB // 2))

            def front_pe(pe, c, k):
                pe.wait_ge(s["nrm"], at(c, 1, 1))
                pe.wait_ge(s["xT"], at(c, 1, 0))
                for n in range(2 * TT):
                    b_, o = SLOT_OF[n]
                    ins = pe.transpose(pT[:, b_, o:o + TP], nx[:, k, n // 2, (n % 2) * KC:(n % 2 + 1) * KC],
                                       ident[0:TP, 0:TP])
                ins.then_inc(s["T"], 1)
                pe.wait_ge(s["xT"], at(c, 1, 1))
                pe.wait_ge(s["oh"], at(c, 1, 0))
                for t in range(TT):
                    for cc in range(KT):
                        ins = pe.matmul(pL[:, t, :], xT[:, 2 * t + cc, :], wr[:, cc, :], start=(cc == 0),
                                        stop=(cc == KT - 1))
                ins.then_inc(s["L"], 1)

            @block.tensor
            def _(pe):
                for n in ("T", "L", "cum"):
                    pe.sem_inc(s[n], CREDIT)
                pe.wait_ge(s_w, 32)
                pe.wait_ge(s_i, 2)
                front_pe(pe, 0, 0)

                def body(c, i, k, last):
                    pe.wait_ge(s["oh"], at(c, 1, 1))
                    pe.wait_ge(s["dest"], at(c, 1, 0))
                    pe.matmul(pC[:, :, :], tri[:, :], oh[:, :, :], start=True, stop=False)
                    for d in range(1, TT):
                        ins = pe.matmul(pC[:, d:TT, :], ones[:, :], oh[:, 0:TT - d, :], start=False, stop=(d == TT - 1))
                    ins.then_inc(s["cum"], 1)
                    if last < 2:
                        front_pe(pe, c + 1, 1 - k)

                two_a_turn(pe, NB, body)

            def rows_act(act, c):
                act.wait_ge(s["stat"], at(c, 1, 1))
                act.wait_ge(s["nrm"], at(c, 1, 0))
                act.sem_inc(s_go, 1)
                for t in range(TT):
                    ins = nc.scalar.activation(xs[:, t, :], base[:, bass.ds(c * TT + t, 1), :].rearrange("p a d -> p (a d)"),
                                               ACT.Identity, bias=nb_[:, 1, t:t + 1], scale=rs[:, 1, t:t + 1])
                ins.then_inc(s["xs"], 1)

            def base_act(act, c):
                act.wait_ge(s["xs"], at(c, 1, 1))
                act.sem_inc(s_go, 1)
                for t in range(TT):
                    rows = base[:, bass.ds(c * TT + t, 1), :].rearrange("p a d -> p (a d)")
                    ins = nc.scalar.activation(rows, rows, ACT.Identity, bias=nb_[:, 0, t:t + 1], scale=ve[:, 0, t:t + 1])
                ins.then_inc(s["bas"], 1)

            def copies_act(act, c):
                act.wait_ge(s["T"], at(c, 1, 1))
                act.wait_ge(s["L"], at(c, 1, 0))
                for lo in range(0, 2 * TT, 4):
                    w_ = min(4, 2 * TT - lo)
                    ins = nc.scalar.activation(xT[:, lo:lo + w_, :], pT[:, lo // 4, 0:w_ * TP].rearrange(
                        "p (n l) -> p n l", n=w_), ACT.Copy)
                ins.then_inc(s["xT"], 1)

            @block.scalar
            def _(act):
                for n in ("xs", "bas", "xT", "ex"):
                    act.sem_inc(s[n], CREDIT)
                rows_act(act, 0)
                base_act(act, 0)
                copies_act(act, 0)

                def body(c, i, k, last):
                    if last < 2:
                        rows_act(act, c + 1)
                    act.wait_ge(s["lg"], at(c, 1, 1))
                    nc.scalar.activation(ex[:, :, :], lg[:, :, :], ACT.Exp).then_inc(s["ex"], 1)
                    if last < 2:
                        base_act(act, c + 1)
                        copies_act(act, c + 1)

                two_a_turn(act, NB, body)

            def statistics(dve, c, i, k):
                st = Steps(dve, s_dv, VS, c)
                dve.wait_ge(s_h[k], i * 16 + 16)
                dve.wait_ge(s["bas"], at(c, 1, 0))
                dve.sem_inc(s_go, 1)
                for t in range(TT):
                    ins = v.bn_stats(stats[:, t, :], base[:, bass.ds(c * TT + t, 1), :].rearrange("p a d -> p (a d)"))
                st.after(ins)
                dve.sem_inc(s_go, 1)
                for t in range(TT):
                    ins = v.bn_aggr(mv[:, t, :], stats[:, t, :])
                st.after(ins)
                v.tensor_scalar(ve[:, 0, :], mv[:, :, 1], EPS1, None, ALU.add)
                st.after(v.tensor_scalar(ve[:, 1, :], mv[:, :, 1], 1.0 + EPS2, EPS1 * EPS2, ALU.mult, ALU.add))
                rsqrt(nc, st, rs[:, :, :], ve[:, :, :], hh[:, :, :])
                for n in range(2):
                    ins = v.scalar_tensor_tensor(nb_[:, n, :], mv[:, :, 0], -1.0, rs[:, n, :], ALU.mult, ALU.mult)
                st.after(ins)
                v.tensor_scalar(ve[:, 0, :], rs[:, 0, :], 1.0, None, ALU.add).then_inc(s["stat"], 1)
                st.end()

            def normed(dve, c, i, k):
                dve.wait_ge(s["xs"], at(c, 1, 1))
                dve.wait_ge(s["T"], at(c, 1, -1))
                dve.wait_ge(s_sc[k], i * (16 * TT))
                w3 = lnw[:, :].rearrange("p (a d) -> p a d", a=1).broadcast_to([TP, TT, D])
                v.tensor_tensor(nx[:, k, :, :], xs[:, :, :], w3, ALU.mult)
                dve.sem_inc(s_go, 1)
                v.tensor_tensor(nrm[:, bass.ds(c * TT, TT), :], xs[:, :, :], w3, ALU.mult).then_inc(s["nrm"], 1)

            @block.vector
            def _(dve):
                for n in ("stat", "nrm", "lg", "oh", "dest"):
                    dve.sem_inc(s[n], CREDIT)
                dve.wait_ge(s_w, 32)
                dve.wait_ge(s_i, 2)
                v.memset(sbase[:, :], -1.0)
                statistics(dve, 0, 0, 0)
                normed(dve, 0, 0, 0)
                wide = lambda x: x[:, :].rearrange("p (t a) -> p t a", a=1).broadcast_to([TP, TT, E])

                def body(c, i, k, last):
                    st = Steps(dve, s_ro, VR, c)
                    dve.wait_ge(s["L"], at(c, 1, 1))
                    st.after(v.tensor_reduce(mx[:, :], pL[:, :, :], AX, ALU.max))
                    v.tensor_tensor(eq[:, :, :], pL[:, :, :], wide(mx), ALU.is_equal)
                    v.tensor_tensor(lg[:, :, :], pL[:, :, :], wide(mx), ALU.subtract).then_inc(s["lg"], 1)
                    dve.wait_ge(s["lg"], at(c, 1, 1))
                    st.after(v.tensor_tensor(eq[:, :, :], eq[:, :, :], desc[:, :].rearrange("p (a e) -> p a e", a=1)
                                             .broadcast_to([TP, TT, E]), ALU.mult))
                    st.after(v.tensor_reduce(first[:, :], eq[:, :, :], AX, ALU.max))
                    v.tensor_tensor(oh[:, :, :], eq[:, :, :], wide(first), ALU.is_equal).then_inc(s["oh"], 1)
                    st.after(v.tensor_scalar(slot[:, :], first[:, :], -float(NB * CAP), float(E * NB * CAP),
                                             ALU.mult, ALU.add))
                    dve.wait_ge(s["oh"], at(c, 1, 1))
                    if last < 2:
                        statistics(dve, c + 1, i + k, 1 - k)
                    dve.wait_ge(s["cum"], at(c, 1, 1))
                    st.after(v.tensor_tensor(pr[:, :, :], pC[:, :, :], oh[:, :, :], ALU.mult))
                    st.after(v.tensor_reduce(place[:, :], pr[:, :, :], AX, ALU.add))
                    st.after(v.tensor_scalar(over[:, :], place[:, :], float(CAP), 1.0e6, ALU.is_gt, ALU.mult))
                    st.after(v.tensor_tensor(slot[:, :], slot[:, :], place[:, :], ALU.add))
                    dve.wait_ge(s_sc[k], i * (16 * TT))
                    v.scalar_tensor_tensor(to[:, k, :], slot[:, :], sbase[:, 0:1], over[:, :],
                                           ALU.add, ALU.add).then_inc(s["dest"], 1)
                    dve.wait_ge(s["dest"], at(c, 1, 1))
                    dve.sem_inc(s_go, 1)
                    st.after(v.tensor_copy(dest[:, bass.ds(c * TT, TT)], to[:, k, :]))
                    st.after(v.tensor_scalar(sbase[:, :], sbase[:, :], float(CAP), None, ALU.add))
                    dve.wait_ge(s["ex"], at(c, 1, 1))
                    st.after(v.tensor_reduce(sums[:, :], ex[:, :, :], AX, ALU.add))
                    dve.sem_inc(s_go, 1)
                    st.after(v.reciprocal(prob[:, bass.ds(c * TT, TT)], sums[:, :]))
                    if last < 2:
                        normed(dve, c + 1, i + k, 1 - k)
                    st.end()

                two_a_turn(dve, NB, body)

        with ExitStack() as ctx:
            sb = lambda name, shape, dt=F32: ctx.enter_context(nc.sbuf_tensor("o_" + name, shape, dt))
            ps = lambda name, shape: ctx.enter_context(nc.psum_tensor("o_" + name, shape, F32))
            sem = semaphores(nc, ctx, "o_")
            CT, CE = 2, 4
            CS = CT * 128
            CB, NTURN = 2 * CE, E // 2
            XR = 4
            assert CE * CS == NB * CAP
            wi_s, wo_s = sb("wi_s", [KC, 2, KT, F]), sb("wo_s", [128, 2, FT, D])
            xr = sb("xr", [128, XR, CT, D])
            xT = sb("xT", [KC, 2, KT, CS])
            hT = sb("hT", [128, 2, FT, CS])
            yr = sb("yr", [128, 2, CT, D])
            pT, pH, pY = ps("pT", [KC, 2, KT, CS]), ps("pH", [128, 3, 512]), ps("pY", [128, 2, 512])
            s_w = [sem(f"s_w{k}") for k in range(2)]
            s_x = [sem(f"s_x{k}") for k in range(XR)]
            s_y = [sem(f"s_y{k}") for k in range(2)]
            s_go = sem("s_go")
            s = {n: sem("q_" + n) for n in ("T", "xT", "H", "ha", "hv", "Y", "y")}
            block = ctx.enter_context(nc.Block())

            def turns(eng, body):
                with eng.Fori(0, NTURN - 1) as i:
                    for j in range(CB):
                        body(i * CB + j, i, j, False)
                for j in range(CB):
                    body((NTURN - 1) * CB + j, NTURN - 1, j, True)

            @block.sync
            def _(sp):
                def weights(e, k):
                    sp.dma_start(wi_s[:, k, :, :], wi[e].rearrange("(c p) f -> p c f", p=KC)).then_inc(s_w[k], 16)
                    sp.dma_start(wo_s[:, k, :, :], wo[e].rearrange("(c p) d -> p c d", p=128)).then_inc(s_w[k], 16)

                def rows(c, r):
                    sp.dma_start(xr[:, r, :, :], slot_x[bass.ds(c * CS, CS), :].rearrange("(p t) d -> p t d", p=128))\
                        .then_inc(s_x[r], 16)

                rows(0, 0)
                weights(0, 0)
                for r in range(1, XR):
                    rows(r, r)
                weights(1, 1)

                def body(c, i, j, last):
                    if not last or j + XR < CB:
                        sp.wait_ge(s["T"], at(c, 1, 1))
                        sp.sem_inc(s_go, 1)
                        rows(c + XR, j % XR)
                    sp.wait_ge(s["y"], at(c, 1, 1))
                    sp.sem_inc(s_go, 1)
                    sp.dma_start(slot_y[bass.ds(c * CS, CS), :].rearrange("(p t) d -> p t d", p=128),
                                 yr[:, j % 2, :, :]).then_inc(s_y[j % 2], 16)
                    if j % CE == CE - 1 and not last:
                        weights(i * 2 + (2 + j // CE), j // CE)

                turns(sp, body)
                for k in range(2):
                    sp.wait_ge(s_y[k], 16 * NTURN * CE)

            @block.tensor
            def _(pe):
                for n in ("T", "H", "Y"):
                    pe.sem_inc(s[n], CREDIT)

                def transposes(c, i, j):
                    pe.wait_ge(s_x[j % XR], i * (16 * CB // XR) + 16 * (j // XR + 1))
                    pe.wait_ge(s["xT"], at(c, 1, -1))
                    for t in range(CT):
                        for cc in range(KT):
                            ins = pe.transpose(pT[:, j % 2, cc, t * 128:(t + 1) * 128],
                                               xr[:, j % XR, t, cc * KC:(cc + 1) * KC], ident[:, :])
                    ins.then_inc(s["T"], 1)

                def hidden(c, i, j):
                    k = j // CE
                    if j % CE == 0:
                        pe.wait_ge(s_w[k], i * 32 + 32)
                    pe.wait_ge(s["xT"], at(c, 1, 1))
                    for q in range(3):
                        if q < 2:
                            pe.wait_ge(s["ha"], at(c, 2, q - 1))
                        else:
                            pe.wait_ge(s["hv"], at(c, 1, 0))
                        for f in (2 * q, 2 * q + 1):
                            for cc in range(KT):
                                ins = pe.matmul(pH[:, q, (f % 2) * CS:(f % 2 + 1) * CS],
                                                wi_s[:, k, cc, f * 128:(f + 1) * 128], xT[:, j % 2, cc, :],
                                                start=(cc == 0), stop=(cc == KT - 1))
                        ins.then_inc(s["H"], 1)

                def result(c, i, j):
                    pe.wait_ge(s["ha"], at(c, 2, 2))
                    pe.wait_ge(s["hv"], at(c, 1, 1))
                    pe.wait_ge(s["y"], at(c, 1, -1))
                    for t in range(CT):
                        for f in range(FT):
                            ins = pe.matmul(pY[:, j % 2, t * D:(t + 1) * D], hT[:, j % 2, f, t * 128:(t + 1) * 128],
                                            wo_s[:, j // CE, f, :], start=(f == 0), stop=(f == FT - 1))
                    ins.then_inc(s["Y"], 1)

                transposes(0, 0, 0)
                transposes(1, 0, 1)
                hidden(0, 0, 0)

                def body(c, i, j, last):
                    if not last or j + 2 < CB:
                        transposes(c + 2, i + (j + 2) // CB, (j + 2) % CB)
                    if not last or j + 1 < CB:
                        hidden(c + 1, i + (j + 1) // CB, (j + 1) % CB)
                    result(c, i, j)

                turns(pe, body)

            @block.scalar
            def _(act):
                act.sem_inc(s["ha"], CREDIT)

                def body(c, i, j, last):
                    act.wait_ge(s["Y"], at(c, 1, -1))
                    for q in range(2):
                        act.wait_ge(s["H"], at(c, 3, q + 1))
                        nc.scalar.activation(hT[:, j % 2, 2 * q:2 * q + 2, :], pH[:, q, :].rearrange(
                            "p (f n) -> p f n", f=2), ACT.Relu).then_inc(s["ha"], 1)

                turns(act, body)

            @block.vector
            def _(dve):
                for n in ("xT", "hv", "y"):
                    dve.sem_inc(s[n], CREDIT)

                def columns(c, i, j):
                    dve.wait_ge(s["T"], at(c, 1, 1))
                    dve.wait_ge(s["H"], at(c, 3, -3))
                    v.tensor_copy(xT[:, j % 2, :, :], pT[:, j % 2, :, :]).then_inc(s["xT"], 1)

                def relu(c, i, j):
                    dve.wait_ge(s["H"], at(c, 3, 3))
                    dve.wait_ge(s["Y"], at(c, 1, -1))
                    v.tensor_scalar(hT[:, j % 2, 4:6, :], pH[:, 2, :].rearrange("p (f n) -> p f n", f=2), 0.0, None,
                                    ALU.max).then_inc(s["hv"], 1)

                columns(0, 0, 0)
                columns(1, 0, 1)
                relu(0, 0, 0)

                def body(c, i, j, last):
                    if not last or j + 2 < CB:
                        columns(c + 2, i + (j + 2) // CB, (j + 2) % CB)
                    if not last or j + 1 < CB:
                        relu(c + 1, i + (j + 1) // CB, (j + 1) % CB)
                    dve.wait_ge(s["Y"], at(c, 1, 1))
                    dve.wait_ge(s_y[j % 2], i * (16 * CE) + 16 * (j // 2))
                    v.tensor_copy(yr[:, j % 2, :, :], pY[:, j % 2, 0:CT * D].rearrange("p (t d) -> p t d", t=CT))\
                        .then_inc(s["y"], 1)

                turns(dve, body)

        with ExitStack() as ctx:
            sem = semaphores(nc, ctx, "r_")
            s_g = [sem(f"s_g{k}") for k in range(2)]
            s_sum, s_out, s_go, s_at = sem("s_sum"), sem("s_out"), sem("s_go"), sem("s_at")
            at_ = ctx.enter_context(nc.sbuf_tensor("r_at", [TP, 2, TT], U32))
            got = ctx.enter_context(nc.sbuf_tensor("r_got", [TP, 2, TT, D], F32))
            block = ctx.enter_context(nc.Block())
            flat = lambda x, n: x[:, bass.ds(n, 1), :].rearrange("p a d -> p (a d)")

            @block.gpsimd
            def _(pool):
                last_slot = pool.to_reg(SLOTS - 1)
                pool.sem_inc(s_go, 1)

                def body(c, i, k, last):
                    pool.wait_ge(s_at, at(c, 1, 1))
                    pool.sem_inc(s_go, 1)
                    for t in range(TT):
                        pool.indirect_dma_start(got[:, k, t, :], None, slot_y,
                                                bass.IndirectOffsetOnAxis(ap=at_[:, k, t:t + 1], axis=0),
                                                bounds_check=last_slot, oob_is_err=False).then_inc(s_g[k], 16)

                two_a_turn(pool, NB, body)

            @block.vector
            def _(dve):
                dve.sem_inc(s_sum, CREDIT)
                dve.sem_inc(s_at, CREDIT)
                dve.sem_inc(s_go, 1)
                def prepare(c, k):
                    v.tensor_copy(at_[:, k, :], dest[:, bass.ds(c * TT, TT)])
                    v.tensor_copy(got[:, k, :, :], nrm[:, bass.ds(c * TT, TT), :]).then_inc(s_at, 1)

                for k in range(2):
                    prepare(k, k)

                def body(c, i, k, last):
                    dve.wait_ge(s_g[k], i * (16 * TT) + 16 * TT)
                    dve.sem_inc(s_go, 1)
                    for t in range(TT):
                        n = c * TT + t
                        ins = v.scalar_tensor_tensor(flat(base, n), got[:, k, t, :], prob[:, bass.ds(n, 1)], flat(base, n),
                                                     ALU.mult, ALU.add)
                    ins.then_inc(s_sum, 1)
                    if not last:
                        dve.wait_ge(s_sum, at(c, 1, 1))
                        dve.sem_inc(s_go, 1)
                        prepare(c + 2, k)

                two_a_turn(dve, NB, body)

            @block.sync
            def _(sp):
                def body(c, i, k, last):
                    sp.wait_ge(s_sum, at(c, 1, 1))
                    sp.sem_inc(s_go, 1)
                    sp.dma_start(out[c].rearrange("(t p) d -> p t d", p=TP), base[:, bass.ds(c * TT, TT), :])\
                        .then_inc(s_out, 16)

                two_a_turn(sp, NB, body)
                sp.wait_ge(s_out, 16 * NB)


def trunk(nc, x, tok_gamma, tok_beta, tok_w, tok_b, ssm_lam, ssm_wd, ssm_bd, ssm_wb, ssm_wc, ssm_wout, ssm_bout,
          gate_w, gate_b, gate_bias, wu, bu, wg, bg, wd, bd, swu, sbu, swg, sbg, swd, sbd,
          w_qkv, b_qkv, w_proj, b_proj, ln_w, w_router, wi, wo, out):
    dram = lambda name, shape, dt=F32: nc.dram_tensor("dram_" + name, shape, dt, kind="Internal").ap()
    h0, h1, h2, h3 = (dram(f"h{n}", (T, D)) for n in range(4))
    token_selection(nc, x, tok_gamma, tok_beta, tok_w, tok_b, dram("score", (NB, N_IN)), h0)
    ssm(nc, h0, ssm_lam, ssm_wd, ssm_bd, ssm_wb, ssm_wc, ssm_wout, ssm_bout, dram("ct", (NB, 16, S)), h1)
    dense_experts(nc, h1, gate_w, gate_b, gate_bias, wu, bu, wg, bg, wd, bd, swu, sbu, swg, sbg, swd, sbd, h2)
    scratch = {
        "xn": dram("xn", (NB, TP, TT * D)), "xt": dram("xt", (NB, KC, KT * S), BF16),
        "v": dram("v", (NB, TP, TT * D)), "qk": dram("qk", (NB, 128, 6 * S), BF16),
        "vq": dram("vq", (NB, TP, TT * NHD * HP), BF16), "st": dram("st", (NB, TP, 2 * NHD * TT)),
        "o": dram("o", (NB, 128, 3 * S)),
    }
    attention(nc, h2, w_qkv, b_qkv, w_proj, b_proj, scratch, h3)
    slots = 16 * NB * 64
    switch_experts(nc, h3, ln_w, w_router, wi, wo, dram("slot_x", (slots, D)), dram("slot_y", (slots, D)), out)


_INS = ['x', 'L0_tok_gamma', 'L0_tok_beta', 'L0_tok_w', 'L0_tok_b',
        'L0_attn_log_lambda', 'L0_attn_Wd', 'L0_attn_bd', 'L0_attn_WB', 'L0_attn_WC', 'L0_attn_Wout', 'L0_attn_bout',
        'L0_ffn_gate_w', 'L0_ffn_gate_b', 'L0_ffn_bias', 'L0_ffn_Wu', 'L0_ffn_bu', 'L0_ffn_Wg', 'L0_ffn_bg',
        'L0_ffn_Wd', 'L0_ffn_bd', 'L0_ffn_sWu', 'L0_ffn_sbu', 'L0_ffn_sWg', 'L0_ffn_sbg', 'L0_ffn_sWd', 'L0_ffn_sbd',
        'L1_attn_w_qkv', 'L1_attn_b_qkv', 'L1_attn_w_proj', 'L1_attn_b_proj',
        'L1_ffn_ln_w', 'L1_ffn_w_router', 'L1_ffn_wi', 'L1_ffn_wo']
_OUTS = [((NB, S, D), 'float32')]


def kernel(**inputs):
    import numpy as _np
    import concourse.bacc as _bacc
    from concourse import mybir as _mybir
    from concourse.bass_utils import run_bass_kernel_spmd as _run

    nc = _bacc.Bacc("TRN2", target_bir_lowering=False, num_devices=1)
    arrays, args = {}, []
    for name in _INS:
        a = _np.ascontiguousarray(inputs[name])
        arrays[f"in_{name}_dram"] = a
        args.append(nc.dram_tensor(f"in_{name}_dram", a.shape, _mybir.dt.from_np(a.dtype), kind="ExternalInput").ap())
    for i, (shape, dtype) in enumerate(_OUTS):
        dt = _mybir.dt.from_np(_np.dtype(dtype))
        args.append(nc.dram_tensor(f"out_{i}_dram", shape, dt, kind="ExternalOutput").ap())
    trunk(nc, *args)
    r = _run(nc, [arrays], core_ids=[0])
    return tuple(r.results[0][f"out_{i}_dram"] for i in range(len(_OUTS)))[0]
```

```python
from contextlib import ExitStack

import concourse.bass as bass
from concourse import mybir

F32 = mybir.dt.float32
BF16 = mybir.dt.bfloat16
F32R = mybir.dt.float32r
I32 = mybir.dt.int32
U32 = mybir.dt.uint32
ALU = mybir.AluOpType
ACT = mybir.ActivationFunctionType
AX = mybir.AxisListType.X

NB, N_IN, D = 16, 750, 192
S = 525
T = NB * S
TP, TT = 105, 5
OFF = 512 - (S + 1) // 2
CUT = ((0, 512 - OFF), (512 - OFF, S))
KC, KT = 96, 2


def semaphores(nc, ctx, prefix):
    mine = []

    def sem(name):
        mine.append(nc.alloc_semaphore(prefix + name))
        return mine[-1]

    def clear():
        nc.clear_and_free_semaphores(mine)
        nc.all_engine_barrier()

    ctx.callback(clear)
    return sem


class Steps:

    def __init__(self, eng, sem, per=0, turn=0):
        self.eng, self.sem, self.base, self.n, self.per = eng, sem, turn * per, 0, per

    def after(self, ins):
        ins.then_inc(self.sem, 1)
        self.n += 1
        self.eng.wait_ge(self.sem, self.base + self.n)

    def counted(self, ins):
        ins.then_inc(self.sem, 1)
        self.n += 1

    def wait(self, back=0):
        if self.n > back:
            self.eng.wait_ge(self.sem, self.base + (self.n - back))

    def end(self):
        assert self.n == self.per, (self.n, self.per)


RSQRT_STEPS = 11


def rsqrt(nc, st, y, v, h):
    st.after(nc.vector.tensor_scalar(h.bitcast(I32), v.bitcast(I32), 1, None, ALU.logical_shift_right))
    st.after(nc.vector.tensor_scalar(y.bitcast(I32), h.bitcast(I32), -1.0, float(0x5F3759DF), ALU.mult, ALU.add))
    for _ in range(3):
        st.after(nc.vector.tensor_tensor(h, y, y, ALU.mult))
        st.after(nc.vector.scalar_tensor_tensor(h, h, -0.5, v, ALU.mult, ALU.mult))
        st.after(nc.vector.scalar_tensor_tensor(y, h, 1.5, y, ALU.add, ALU.mult))


def token_selection(nc, x, gamma, beta, w, b0, score_d, h0):
    P, G = 125, N_IN // 125
    R = 4
    PER_S, PER_R = 3 + RSQRT_STEPS + 3, (2 * G - 1) + 3

    with ExitStack() as ctx:
        sb = lambda name, shape, dt=F32: ctx.enter_context(nc.sbuf_tensor("a_" + name, shape, dt))
        sem = semaphores(nc, ctx, "a_")
        xt = sb("xt", [P, R, G * D])
        prod = sb("prod", [P, G * D])
        gam, bet, wr, bb = sb("gam", [P, D]), sb("bet", [P, D]), sb("wr", [P, D]), sb("bb", [P, 1])
        gw, bw, sgw, cst = sb("gw", [P, D]), sb("bw", [P, D]), sb("sgw", [P, 1]), sb("cst", [P, 1])
        stats, mv = sb("stats", [P, G, 6]), sb("mv", [P, G, 2])
        dot, ve, rs, hh = (sb(n, [P, G]) for n in ("dot", "ve", "rs", "hh"))
        sc = sb("sc", [P, 2, G])
        srow = sb("srow", [P, 2, N_IN])
        earlier = sb("earlier", [P, G, N_IN], BF16)
        junk = sb("junk", [P, 4, N_IN], BF16)
        above, ties = sb("above", [P, G]), sb("ties", [P, G])
        rank, over, base = sb("rank", [P, G]), sb("over", [P, G]), sb("base", [P, 1])
        dest = sb("dest", [P, R, G], U32)

        s_const = sem("s_const")
        s_mask0, s_mask = sem("s_mask0"), sem("s_mask")
        s_x = [sem(f"s_x{k}") for k in range(R)]
        s_score, s_scored = sem("s_score"), sem("s_scored")
        s_row = [sem(f"s_row{k}") for k in range(2)]
        s_ranked = sem("s_ranked")
        s_dest = sem("s_dest")
        s_kept = [sem(f"s_kept{k}") for k in range(R)]
        s_v, s_r = sem("s_v"), sem("s_r")
        s_go = sem("s_go")
        s_pre = sem("s_pre")

        block = ctx.enter_context(nc.Block())

        @block.sync
        def _(sp):
            for dst, src in ((gam, gamma), (bet, beta), (wr, w)):
                sp.dma_start(dst[:, :], src.rearrange("(a d) -> a d", a=1).broadcast_to([P, D])).then_inc(s_const, 16)
            sp.dma_start(bb[:, :], b0.rearrange("(a d) -> a d", a=1).broadcast_to([P, 1])).then_inc(s_const, 16)
            def body(b, i, k, left):
                sp.wait_ge(s_kept[k], i * (16 * G))
                sp.dma_start(xt[:, k, :], x[b].rearrange("(p g) d -> p (g d)", p=P)).then_inc(s_x[k], 16)

            turns(sp, NB, R, body)

        @block.scalar
        def _(act):
            def body(b, i, k, left):
                act.wait_ge(s_score, b + 1)
                act.dma_start(score_d[b].rearrange("(p g) -> p g", p=P), sc[:, k % 2, :]).then_inc(s_scored, 16)
                act.wait_ge(s_scored, b * 16 + 16)
                act.wait_ge(s_ranked, at(b, 1, -1))
                act.dma_start(srow[:, k % 2, :], score_d[b].rearrange("(a n) -> a n", a=1).broadcast_to([P, N_IN]))\
                    .then_inc(s_row[k % 2], 16)

            turns(act, NB, R, body)

        @block.gpsimd
        def _(pool):
            pool.memset(earlier[:, :, :], 1.0).then_inc(s_mask0, 1)
            pool.wait_ge(s_mask0, 1)
            pool.affine_select(out=earlier[:, :, :], in_=earlier[:, :, :], compare_op=ALU.is_gt, fill=0.0,
                               base=0, pattern=[[1, G], [-1, N_IN]], channel_multiplier=G).then_inc(s_mask, 1)
            last_row = pool.to_reg(T - 1)

            def body(b, i, k, left):
                pool.wait_ge(s_dest, b + 1)
                pool.sem_inc(s_go, 1)
                for g in range(G):
                    pool.indirect_dma_start(h0, bass.IndirectOffsetOnAxis(ap=dest[:, k, g:g + 1], axis=0),
                                            xt[:, k, g * D:(g + 1) * D], None,
                                            bounds_check=last_row, oob_is_err=False).then_inc(s_kept[k], 16)

            turns(pool, NB, R, body)
            for k in range(R):
                pool.wait_ge(s_kept[k], 16 * G * (NB // R))

        @block.vector
        def _(dve):
            v = nc.vector
            dve.wait_ge(s_const, 64)
            dve.wait_ge(s_mask, 1)
            pre = Steps(dve, s_pre)
            pre.after(v.tensor_tensor(gw[:, :], gam[:, :], wr[:, :], ALU.mult))
            pre.after(v.tensor_tensor(bw[:, :], bet[:, :], wr[:, :], ALU.mult))
            pre.after(v.tensor_reduce(sgw[:, :], gw[:, :], AX, ALU.add))
            pre.after(v.tensor_reduce(cst[:, :], bw[:, :], AX, ALU.add))
            pre.after(v.tensor_tensor(cst[:, :], cst[:, :], bb[:, :], ALU.add))
            pre.after(v.memset(base[:, :], 0.0))
            dve.sem_inc(s_ranked, CREDIT)

            def scores(b, i, k):
                st = Steps(dve, s_v, PER_S, b)
                dve.wait_ge(s_x[k], i * 16 + 16)
                x3 = xt[:, k, :].rearrange("p (g d) -> p g d", g=G)
                v.tensor_tensor(prod[:, :].rearrange("p (g d) -> p g d", g=G), x3,
                                gw[:, :].rearrange("p (a d) -> p a d", a=1).broadcast_to([P, G, D]), ALU.mult)
                for g in range(G):
                    ins = v.bn_stats(stats[:, g, :], x3[:, g, :])
                st.after(ins)
                v.tensor_reduce(dot[:, :], prod[:, :].rearrange("p (g d) -> p g d", g=G), AX, ALU.add)
                for g in range(G):
                    ins = v.bn_aggr(mv[:, g, :], stats[:, g, :])
                st.after(ins)
                st.after(v.tensor_scalar(ve[:, :], mv[:, :, 1], 1e-5, None, ALU.add))
                rsqrt(nc, st, rs[:, :], ve[:, :], hh[:, :])
                st.after(v.tensor_scalar(hh[:, :], mv[:, :, 0], sgw[:, 0:1], None, ALU.mult))
                st.after(v.tensor_tensor(hh[:, :], dot[:, :], hh[:, :], ALU.subtract))
                st.after(v.tensor_tensor(hh[:, :], hh[:, :], rs[:, :], ALU.mult))
                dve.wait_ge(s_scored, b * 16)
                v.tensor_scalar(sc[:, k % 2, :], hh[:, :], cst[:, 0:1], None, ALU.add).then_inc(s_score, 1)
                st.end()

            scores(0, 0, 0)

            def body(b, i, k, left):
                if left:
                    scores(b + 1, i + (k + 1) // R, (k + 1) % R)
                n = k % 2
                st = Steps(dve, s_r, PER_R, b)
                dve.wait_ge(s_score, b + 1)
                dve.wait_ge(s_row[n], i * (16 * R // 2) + 16 * (k // 2 + 1))
                for g in range(G):
                    st.wait(3)
                    st.counted(v.tensor_scalar(junk[:, 2 * (g % 2), :], srow[:, n, :], sc[:, n, g:g + 1], 0.0,
                                               ALU.is_gt, ALU.add, accum_out=above[:, g:g + 1]))
                    st.wait(3)
                    ins = v.scalar_tensor_tensor(junk[:, 2 * (g % 2) + 1, :], srow[:, n, :], sc[:, n, g:g + 1],
                                                 earlier[:, g, :], ALU.is_equal, ALU.mult,
                                                 accum_out=ties[:, g:g + 1])
                    if g < G - 1:
                        st.counted(ins)
                ins.then_inc(s_ranked, 1)
                dve.wait_ge(s_ranked, at(b, 1, 1))
                st.after(v.tensor_tensor(rank[:, :], above[:, :], ties[:, :], ALU.add))
                st.after(v.tensor_scalar(over[:, :], rank[:, :], float(S), 1.0e6, ALU.is_ge, ALU.mult))
                dve.wait_ge(s_kept[k], i * (16 * G))
                v.scalar_tensor_tensor(dest[:, k, :], rank[:, :], base[:, 0:1], over[:, :],
                                       ALU.add, ALU.add).then_inc(s_dest, 1)
                dve.wait_ge(s_dest, b + 1)
                st.after(v.tensor_scalar(base[:, :], base[:, :], float(S), None, ALU.add))
                st.end()

            turns(dve, NB, R, body)


def at(turn, per, n):
    return turn * per + (CREDIT + n)


def turns(eng, n, r, body):
    with eng.Fori(0, n // r - 1) as i:
        for k in range(r):
            body(i * r + k, i, k, r)
    for k in range(r):
        body(n - r + k, n // r - 1, k, r - 1 - k)


def two_a_turn(eng, n, body):
    with eng.Fori(0, n // 2 - 1) as i:
        for k in range(2):
            body(i * 2 + k, i, k, 0)
    for k in range(2):
        body(n - 2 + k, n // 2 - 1, k, 1 + k)


CREDIT = 64


def ssm(nc, h0, loglam, wd, bd, wb, wc, wout, bout, ct_d, h1):
    NS, NU, NA = 16, 24, 128
    NH = D - NA
    H0W = 263
    HALF = [(0, H0W), (H0W, S)]
    RING = YR = 4
    HI_LAG, LO_LAG, LAG = 2, 3, 4
    HI, LO = 0, 1
    PARTS = ((HI, HI), (HI, LO), (LO, HI))
    NSP = NU * 2 // 3
    is_split = lambda u: u % 3 < 2
    splits = lambda u: u // 3 * 2 + min(u % 3 + 1, 2)
    unit_of = lambda n: n // 2 * 3 + n % 2
    FS = 9
    GU, NG = 4, NU // 4
    FRONT_AT = {2 * s + 3: s for s in range(FS)}
    VP = 1 + 1 + RSQRT_STEPS + 1
    with ExitStack() as ctx:
        sb = lambda name, shape, dt=F32: ctx.enter_context(nc.sbuf_tensor("b_" + name, shape, dt))
        ps = lambda name, shape: ctx.enter_context(nc.psum_tensor("b_" + name, shape, F32))
        sem = semaphores(nc, ctx, "b_")
        ident = sb("ident", [128, 128])
        wd_n, wout_n = sb("wd_n", [KC, 2, D]), sb("wout_n", [KC, 2, D * NS])
        wb_n, wc_n = sb("wb_n", [NS, D]), sb("wc_n", [NS, D])
        w_hi = sb("w_hi", [KC, 2, NS // 2, 128])
        wdT = sb("wdT", [KC, KT, 256])
        wbcT = sb("wbcT", [KC, KT, 128])
        woutT = [sb(f"woutT{p}", [128, NSP, D], F32R) for p in range(2)]
        woutP = sb("woutP", [128, NU - NSP, D])
        ll, la, nlam = sb("ll", [128, NU]), sb("la", [128, NU]), sb("nlam", [128, NU])
        bdc = sb("bdc", [128, 2])
        bo = sb("bo", [TP, D])
        sel = sb("sel", [96, NU, 128], BF16)
        h = sb("h", [TP, 2, TT, D])
        hb = sb("hb", [TP, 2, TT, D])
        ho = sb("ho", [TP, 2, TT, D])
        xn = sb("xn", [TP, TT, D])
        stats, mv = sb("stats", [TP, TT, 6]), sb("mv", [TP, TT, 2])
        ve, rs, hh, nb_ = (sb(n, [TP, TT]) for n in ("ve", "rs", "hh", "nb"))
        xT = sb("xT", [KC, KT, S])
        za, zr, zl = sb("za", [128, 2, H0W]), sb("zr", [128, 2, H0W]), sb("zl", [128, 2, H0W])
        delta = sb("delta", [128, 2, 2, S])
        bs = sb("bs", [96, 2, S], BF16)
        br, b2 = sb("br", [96, H0W]), sb("b2", [96, H0W], BF16)
        cs = sb("cs", [128, 2, S])
        cb = sb("cb", [128, 3, GU, S])
        ae, bm, hs, ys = (sb(n, [128, RING, S]) for n in ("ae", "bm", "hs", "ys"))
        yp = [sb(f"yp{p}", [128, YR, S], F32R) for p in range(2)]
        pB = ps("pB", [128, 2, 1024])
        pF = ps("pF", [128, 512])
        pA = ps("pA", [TP, 3, 512])

        s_w, s_id0, s_id, s_wT, s_wTc, s_lam, s_pre = (sem(n) for n in (
            "s_w", "s_id0", "s_id", "s_wT", "s_wTc", "s_lam", "s_pre"))
        s_h = [sem(f"s_h{k}") for k in range(2)]
        s_cb = [sem(f"s_cb{k}") for k in range(3)]
        s_ct = [sem(f"s_ct{k}") for k in range(2)]
        s_out = [sem(f"s_out{k}") for k in range(2)]
        names = ("stat", "xn", "front", "faR", "b1", "bR", "b2", "bs", "ln", "delta", "B", "bm", "ae", "hs", "ys",
                 "yh", "yl", "wo", "fin", "hb")
        s = {n: sem("q_" + n) for n in names}
        s_va, s_aa, s_go = sem("s_va"), sem("s_aa"), sem("s_go")
        s_ws = sem("s_ws")
        block = ctx.enter_context(nc.Block())
        v, a = nc.vector, nc.scalar

        def batches(eng, body):
            for k in range(2):
                body(k, 0, k, k == 0, False)
            with eng.Fori(1, NB // 2 - 1) as i:
                for k in range(2):
                    body(i * 2 + k, i, k, False, False)
            for k in range(2):
                body(NB - 2 + k, NB // 2 - 1, k, False, k == 1)

        @block.sync
        def _(sp):
            sp.dma_start(wd_n[:, :, :], wd.rearrange("(c p) d -> p c d", p=KC)).then_inc(s_w, 16)
            sp.dma_start(wout_n[:, :, :], wout.rearrange("(c p) d -> p c d", p=KC)).then_inc(s_w, 16)
            sp.dma_start(wb_n[:, :], wb).then_inc(s_w, 16)
            sp.dma_start(wc_n[:, :], wc).then_inc(s_w, 16)
            sp.dma_start(ll[:, 0:NS], loglam[0:NA, :]).then_inc(s_w, 16)
            two = loglam[NA:D, :].rearrange("e (j t) -> t e j", t=2)
            for t in range(2):
                sp.dma_start(ll[64 * t:64 * t + 64, NS:NU], two[t], allow_slow_non_contiguous=True).then_inc(s_w, 16)
                sp.dma_start(bdc[64 * t:64 * t + 64, 1:2], bd[NA:D].rearrange("(e a) -> e a", a=1)).then_inc(s_w, 16)
            sp.dma_start(bdc[:, 0:1], bd[0:NA].rearrange("(e a) -> e a", a=1)).then_inc(s_w, 16)
            sp.dma_start(bo[:, :], bout.rearrange("(a d) -> a d", a=1).broadcast_to([TP, D])).then_inc(s_w, 16)
            rows = lambda x, b: x[bass.ds(b * S, S), :].rearrange("(t p) d -> p t d", p=TP)
            sp.dma_start(h[:, 0, :, :], rows(h0, 0)).then_inc(s_h[0], 16)

            def body(b, i, k, first, last):
                if not last:
                    sp.wait_ge(s["xn"], at(b, 1, 0))
                    sp.wait_ge(s["hb"], at(b, 1, 0))
                    sp.dma_start(h[:, 1 - k, :, :], rows(h0, b + 1)).then_inc(s_h[1 - k], 16)
                sp.wait_ge(s_ct[k], i * 32 + 32)
                for g in range(NG):
                    sp.wait_ge(s["ys"], at(b, NU, (g - 2) * GU))
                    if g * GU < NS:
                        src = ct_d[b, g * GU:(g + 1) * GU, :].rearrange("(a n) l -> a (n l)", a=1)
                        sp.dma_start(cb[:, g % 3, :, :].rearrange("p n l -> p (n l)"),
                                     src.broadcast_to([128, GU * S])).then_inc(s_cb[g % 3], 16)
                    else:
                        j = g * GU - NS
                        for t in range(2):
                            src = ct_d[b, 2 * j:2 * j + 2 * GU, :].rearrange("(n t) l -> t n l", t=2)
                            sp.dma_start(cb[64 * t:64 * t + 64, g % 3, :, :],
                                         src[t:t + 1].broadcast_to([64, GU, S])).then_inc(s_cb[g % 3], 16)
                    if g == 3 and not first:
                        store(b - 1, 1 - k)

            def store(b, k):
                sp.wait_ge(s["fin"], at(b, 1, 1))
                sp.dma_start(rows(h1, b), ho[:, k, :, :]).then_inc(s_out[k], 16)

            batches(sp, body)
            store(NB - 1, 1)
            for k in range(2):
                sp.wait_ge(s_out[k], 16 * (NB // 2))

        def cb_count(g):
            return sum(16 if q * GU < NS else 32 for q in range(g % 3, g + 1, 3))
        CB_ALL = [cb_count(3 + q) for q in range(3)]

        @block.gpsimd
        def _(pool):
            for n in ("ys", "hb"):
                pool.sem_inc(s[n], CREDIT)
            pool.memset(ident[:, :], 0.0).then_inc(s_id0, 1)
            pool.memset(sel[:, :, :], 0.0).then_inc(s_id0, 1)
            pool.memset(wbcT[:, :, :], 0.0).then_inc(s_id0, 1)
            pool.wait_ge(s_id0, 3)
            pool.affine_select(out=ident[:, :], in_=ident[:, :], compare_op=ALU.not_equal, fill=1.0, base=0,
                               pattern=[[-1, 128]], channel_multiplier=1).then_inc(s_id, 1)
            for g in range(3):
                pool.wait_ge(s_id, 1 + 2 * g)
                m = sel[32 * g:32 * g + 32, 0:NS, :]
                pool.affine_select(out=m, in_=m, compare_op=ALU.not_equal, fill=1.0, base=0,
                                   pattern=[[-1, NS], [0, 128]], channel_multiplier=1).then_inc(s_id, 1)
                pool.wait_ge(s_id, 2 + 2 * g)
                m = sel[32 * g:32 * g + 32, NS:NU, :].rearrange("p j (t e) -> p j t e", t=2)
                pool.affine_select(out=m, in_=m, compare_op=ALU.not_equal, fill=1.0, base=0,
                                   pattern=[[-2, NS // 2], [-1, 2], [0, NH]], channel_multiplier=1).then_inc(s_id, 1)

            def body(b, i, k, first, last):
                pool.wait_ge(s_h[k], i * 16 + 16)
                pool.wait_ge(s["fin"], at(b, 1, -1))
                pool.tensor_tensor(hb[:, k, :, :], h[:, k, :, :],
                                   bo[:, :].rearrange("p (a d) -> p a d", a=1).broadcast_to([TP, TT, D]),
                                   ALU.add).then_inc(s["hb"], 1)
                for u in range(NU):
                    g = u // GU
                    if u % GU == 0:
                        pool.wait_ge(s_cb[g % 3], b * CB_ALL[g % 3] + cb_count(g))
                    pool.wait_ge(s["hs"], at(b, NU, u + 1))
                    if is_split(u - RING):
                        pool.wait_ge(s["yl"], at(b, NSP, splits(u - RING)))
                    else:
                        pool.wait_ge(s["wo"], at(b, NU, u + 1 - RING))
                    pool.tensor_tensor(ys[:, u % RING, :], hs[:, u % RING, :], cb[:, g % 3, u % GU, :],
                                       ALU.mult).then_inc(s["ys"], 1)

            pool.wait_ge(s_w, 16 * 11)
            for r in range(2):
                pool.wait_ge(s_id, 7 + r)
                pool.tensor_copy(w_hi[:, r, :, :].rearrange("p j (t e) -> p (j t) e", t=2),
                                 wout_n[:, r, :].rearrange("p (d n) -> p n d", n=NS)[:, :, NA:D]).then_inc(s_id, 1)
            batches(pool, body)

        def front_act(b, i, k, step, ln_ready=None):
            a_eng = nc.scalar
            a_eng.wait_ge(s["front"], at(b, FS, step + 1))
            if step < 3:
                if step == 1:
                    dst = xT[:, :, 4 * TP:S]
                    src = pF[0:KC, 0:2 * TP].rearrange("p (c l) -> p c l", c=2)
                else:
                    dst, src = xT[:, step // 2, 0:4 * TP], pF[0:KC, 0:4 * TP]
                a_eng.activation(dst, src, ACT.Copy).then_inc(s["faR"], 1)
            elif step < 7:
                q, half = (step - 3) // 2, (step - 3) % 2
                w = HALF[half][1] - HALF[half][0]
                if step == 3:
                    a_eng.wait_ge(s["delta"], at(b, 4, 0))
                else:
                    a_eng.wait_ge(s["delta"], at(b, 4, step - 4))
                a_eng.activation(za[:, half, 0:w], pF[:, 0:w], ACT.Abs, bias=bdc[:, q:q + 1]).then_inc(s_aa, 1)
                a_eng.activation(zr[:, half, 0:w], pF[:, 0:w], ACT.Relu, bias=bdc[:, q:q + 1]).then_inc(s["faR"], 1)
                base = b * 8 + 2 * (step - 3)
                a_eng.wait_ge(s_aa, base + 1)
                a_eng.activation(za[:, half, 0:w], za[:, half, 0:w], ACT.Exp, scale=-1.0).then_inc(s_aa, 1)
                a_eng.wait_ge(s_aa, base + 2)
                a_eng.activation(zl[:, half, 0:w], za[:, half, 0:w], ACT.Ln, bias=1.0).then_inc(s["ln"], 1)
            else:
                half = step - 7
                lo, hi = HALF[half]
                if half == 0:
                    a_eng.wait_ge(s["B"], at(b, NU, -NU))
                a_eng.activation(bs[:, k, lo:hi], pF[0:96, 0:hi - lo], ACT.Copy).then_inc(s["b1"], 1)
                if half == 0:
                    a_eng.wait_ge(s_ct[k], i * 32)
                a_eng.activation(cs[96:96 + NS, k, lo:hi], pF[96:96 + NS, 0:hi - lo], ACT.Copy)\
                    .then_inc(s["faR"], 1)

        def front_act_late(b, i, k, step):
            if step >= 7:
                half = step - 7
                lo, hi = HALF[half]
                a_eng = nc.scalar
                a_eng.wait_ge(s["bR"], at(b, 2, half + 1))
                a_eng.activation(bs[32:64, k, lo:hi], br[32:64, 0:hi - lo], ACT.Copy)
                a_eng.activation(b2[64:96, 0:hi - lo], br[64:96, 0:hi - lo], ACT.Copy).then_inc(s["b2"], 1)
                a_eng.wait_ge(s["faR"], at(b, FS, step + 1))
                a_eng.dma_start(ct_d[b, :, lo:hi], cs[96:96 + NS, k, lo:hi]).then_inc(s_ct[k], 16)

        def front_ln_act(b, i, k):
            nc.scalar.wait_ge(s["stat"], at(b, 1, 1))
            nc.scalar.wait_ge(s["front"], at(b, FS, 0))
            for t in range(TT):
                ins = nc.scalar.activation(xn[:, t, :], h[:, k, t, :], ACT.Identity, bias=nb_[:, t:t + 1],
                                           scale=rs[:, t:t + 1])
            ins.then_inc(s["xn"], 1)

        @block.scalar
        def _(act):
            for n in ("faR", "b1", "b2", "ln", "ae", "xn"):
                act.sem_inc(s[n], CREDIT)
            act.wait_ge(s_w, 16 * 11)
            chain = Steps(act, s_lam)
            chain.after(act.activation(la[:, :], ll[:, :], ACT.Abs))
            act.preload_act_table_set("natural_log_exp_and_others")
            chain.after(act.activation(la[:, :], la[:, :], ACT.Exp, scale=-1.0))
            chain.after(act.activation(la[:, :], la[:, :], ACT.Ln, bias=1.0))
            chain.after(act.activation(ll[:, :], ll[:, :], ACT.Relu))
            front_ln_act(0, 0, 0)
            for step in range(FS):
                front_act(0, 0, 0, step)
                front_act_late(0, 0, 0, step)
            act.wait_ge(s_pre, 1)

            act.sem_inc(s["yh"], CREDIT)

            def high(b, u):
                act.wait_ge(s["ys"], at(b, NU, u + 1))
                act.wait_ge(s["wo"], at(b, NU, unit_of(splits(u) - 1 - YR) + 1))
                act.activation(yp[HI][:, (splits(u) - 1) % YR, :], ys[:, u % RING, :], ACT.Copy).then_inc(s["yh"], 1)

            def body(b, i, k, first, last):
                for u in range(NU):
                    q = 0 if u < NS else 1
                    if u == 0:
                        act.wait_ge(s["delta"], at(b, 4, 4))
                    act.wait_ge(s["hs"], at(b, NU, u + 1 - RING))
                    act.activation(ae[:, u % RING, :], delta[:, k, q, :], ACT.Exp, scale=nlam[:, u:u + 1])\
                        .then_inc(s["ae"], 1)
                    if (u >= HI_LAG or not first) and is_split(u - HI_LAG):
                        high(b, u - HI_LAG)
                    if not last:
                        ii = i + k
                        if u == 2:
                            front_ln_act(b + 1, ii, 1 - k)
                        if u - 1 in FRONT_AT:
                            front_act(b + 1, ii, 1 - k, FRONT_AT[u - 1])
                        if u - 2 in FRONT_AT:
                            front_act_late(b + 1, ii, 1 - k, FRONT_AT[u - 2])

            batches(act, body)
            for u in range(NU - HI_LAG, NU):
                if is_split(u):
                    high(NB - 1, u)

        def front_pe(b, i, k, step):
            pe = nc.tensor
            if step == 0:
                pe.wait_ge(s["xn"], at(b, 1, 1))
            pe.wait_ge(s["faR"], at(b, FS, step))
            if step < 3:
                if step == 1:
                    tiles = [(c, 4, c * TP) for c in range(KT)]
                else:
                    tiles = [(step // 2, t, t * TP) for t in range(4)]
                for c, t, col in tiles:
                    ins = pe.transpose(pF[0:KC, col:col + TP], xn[:, t, c * KC:(c + 1) * KC], ident[0:TP, 0:TP])
            else:
                if step == 8:
                    pe.wait_ge(s["bR"], at(b, 2, 1))
                half = (step - 3) % 2
                lo, hi = HALF[half]
                for c in range(KT):
                    lhs = wdT[:, c, 128 * ((step - 3) // 2):][:, 0:128] if step < 7 else wbcT[:, c, :]
                    ins = pe.matmul(pF[:, 0:hi - lo], lhs, xT[:, c, lo:hi], start=(c == 0), stop=(c == KT - 1))
            ins.then_inc(s["front"], 1)

        @block.tensor
        def _(pe):
            for n in ("front", "B", "wo"):
                pe.sem_inc(s[n], CREDIT)
            pe.wait_ge(s_w, 16 * 11)
            pe.wait_ge(s_id, 9)
            w4 = wout_n[:, :, :].rearrange("p c (d n) -> p c n d", n=NS)
            for c in range(KT):
                for r in range(2):
                    ins = pe.transpose(pF[0:KC, (2 * c + r) * KC:(2 * c + r + 1) * KC], wd_n[:, r, c * KC:(c + 1) * KC],
                                       ident[0:KC, 0:KC])
            ins.then_inc(s_wT, 1)
            pe.wait_ge(s_wTc, 1)
            for c in range(KT):
                pe.transpose(pF[0:KC, c * NS:(c + 1) * NS], wb_n[:, c * KC:(c + 1) * KC], ident[0:NS, 0:NS])
                ins = pe.transpose(pF[0:KC, (2 + c) * NS:(3 + c) * NS], wc_n[:, c * KC:(c + 1) * KC], ident[0:NS, 0:NS])
            ins.then_inc(s_wT, 1)
            for u in range(NU):
                pe.wait_ge(s_wTc, u + 1 if u >= 2 else 2)
                bank = pB[:, u % 2, 0:D]
                for r in range(2):
                    if u < NS:
                        src = w4[:, r, u, 0:NA]
                    else:
                        src = w_hi[:, r, u - NS, :]
                    ins = pe.transpose(bank[:, r * KC:(r + 1) * KC], src, ident[0:KC, 0:KC])
                ins.then_inc(s_wT, 1)
            pe.wait_ge(s_wTc, 2 + NU)
            for step in range(FS):
                front_pe(0, 0, 0, step)

            def spread(b, k, u):
                if u == 0:
                    pe.wait_ge(s["bs"], at(b, 2, 2))
                pe.wait_ge(s["bm"], at(b, NU, u + 1 - 2))
                for lo, hi in CUT:
                    ins = pe.matmul(pB[:, u % 2, OFF + lo:OFF + hi], sel[:, u, :], bs[:, k, lo:hi], start=True, stop=True)
                ins.then_inc(s["B"], 1)

            def project(b, u):
                if is_split(u):
                    pe.wait_ge(s["yl"], at(b, NSP, splits(u)))
                else:
                    pe.wait_ge(s["ys"], at(b, NU, u + 1))
                if u == 0:
                    pe.wait_ge(s["fin"], at(b, 1, 0))
                for t in range(TT):
                    into = pA[:, t // 2, (t % 2) * D:(t % 2 + 1) * D]
                    if is_split(u):
                        m = splits(u) - 1
                        for n, (p, q) in enumerate(PARTS):
                            ins = pe.matmul(into, yp[p][:, m % YR, t * TP:(t + 1) * TP], woutT[q][:, m % NSP, :],
                                            start=(u == 0 and t % 2 == 0 and n == 0), stop=False, skip_group_check=True)
                    else:
                        ins = pe.matmul(into, ys[:, u % RING, t * TP:(t + 1) * TP], woutP[:, u % NU // 3, :],
                                        start=False, stop=(u % NU == NU - 1), skip_group_check=True)
                ins.then_inc(s["wo"], 1)

            for u in range(2):
                spread(0, 0, u)

            def body(b, i, k, first, last):
                for u in range(NU):
                    if u < NU - 2:
                        spread(b, k, u + 2)
                    elif not last:
                        spread(b + 1, 1 - k, u + 2 - NU)
                    if u >= LAG or not first:
                        project(b, u - LAG)
                    if u in FRONT_AT and not last:
                        front_pe(b + 1, i + k, 1 - k, FRONT_AT[u])

            batches(pe, body)
            for u in range(NU - LAG, NU):
                project(NB - 1, u)

        def front_stat(b, i, k):
            dve = nc.vector
            st = Steps(dve, s_va, VP, b)
            dve.wait_ge(s_h[k], i * 16 + 16)
            dve.wait_ge(s["xn"], at(b, 1, 0))
            for t in range(TT):
                ins = v.bn_stats(stats[:, t, :], h[:, k, t, :])
            st.after(ins)
            dve.sem_inc(s_go, 1)
            for t in range(TT):
                ins = v.bn_aggr(mv[:, t, :], stats[:, t, :])
            st.after(ins)
            st.after(v.tensor_scalar(ve[:, :], mv[:, :, 1], 1e-5, None, ALU.add))
            rsqrt(nc, st, rs[:, :], ve[:, :], hh[:, :])
            st.end()
            v.scalar_tensor_tensor(nb_[:, :], mv[:, :, 0], -1.0, rs[:, :], ALU.mult, ALU.mult).then_inc(s["stat"], 1)

        def front_dve(b, i, k, step):
            dve = nc.vector
            if 3 <= step < 7:
                q, half = (step - 3) // 2, (step - 3) % 2
                lo, hi = HALF[half]
                dve.wait_ge(s["ln"], at(b, 4, step - 2))
                v.tensor_tensor(delta[:, k, q, lo:hi], zr[:, half, 0:hi - lo], zl[:, half, 0:hi - lo], ALU.add)\
                    .then_inc(s["delta"], 1)
            if step >= 7:
                half = step - 7
                lo, hi = HALF[half]
                dve.wait_ge(s["b1"], at(b, 2, half + 1))
                v.tensor_tensor(br[:, 0:hi - lo], pF[0:96, 0:hi - lo], bs[:, k, lo:hi], ALU.subtract)\
                    .then_inc(s["bR"], 1)

        def front_dve_late(b, i, k, step):
            dve = nc.vector
            if step >= 7:
                half = step - 7
                lo, hi = HALF[half]
                dve.wait_ge(s["b2"], at(b, 2, half + 1))
                v.tensor_tensor(bs[64:96, k, lo:hi], br[64:96, 0:hi - lo], b2[64:96, 0:hi - lo],
                                ALU.subtract)\
                    .then_inc(s["bs"], 1)
                dve.wait_ge(s["bs"], at(b, 2, half + 1))

        @block.vector
        def _(dve):
            for n in ("stat", "bR", "bs", "delta", "bm", "hs", "fin"):
                dve.sem_inc(s[n], CREDIT)
            front_stat(0, 0, 0)
            dve.wait_ge(s_wT, 1)
            for c in range(KT):
                ins = v.tensor_copy(wdT[:, c, 0:D], pF[0:KC, 2 * c * KC:(2 * c + 2) * KC])
            for c in range(KT):
                ins = v.tensor_copy(wdT[:, c, D:256], pF[0:KC, 2 * c * KC + NA:(2 * c + 2) * KC])
            ins.then_inc(s_wTc, 1)
            dve.wait_ge(s_wT, 2)
            dve.wait_ge(s_id0, 3)
            for c in range(KT):
                for g in range(3):
                    v.tensor_copy(wbcT[:, c, 32 * g:32 * g + NS], pF[0:KC, c * NS:(c + 1) * NS])
                ins = v.tensor_copy(wbcT[:, c, 96:96 + NS], pF[0:KC, (2 + c) * NS:(3 + c) * NS])
            ins.then_inc(s_wTc, 1)
            for u in range(NU):
                dve.wait_ge(s_wT, u + 3)
                if is_split(u):
                    m = splits(u) - 1
                    v.tensor_copy(woutT[HI][:, m, :], pB[:, u % 2, 0:D]).then_inc(s_ws, 1)
                    dve.wait_ge(s_ws, m + 1)
                    v.tensor_tensor(woutT[LO][:, m, :], pB[:, u % 2, 0:D], woutT[HI][:, m, :].bitcast(F32),
                                    ALU.subtract).then_inc(s_wTc, 1)
                else:
                    v.tensor_copy(woutP[:, u // 3, :], pB[:, u % 2, 0:D]).then_inc(s_wTc, 1)
            dve.wait_ge(s_lam, 4)
            v.scalar_tensor_tensor(nlam[:, :], ll[:, :], -1.0, la[:, :], ALU.mult, ALU.subtract).then_inc(s_pre, 1)
            for step in range(FS):
                front_dve(0, 0, 0, step)
                front_dve_late(0, 0, 0, step)

            def weigh(b, k, u):
                if u == 0:
                    dve.wait_ge(s["delta"], at(b, 4, 4))
                dve.wait_ge(s["B"], at(b, NU, u + 1))
                dve.wait_ge(s["hs"], at(b, NU, u + 1 - RING))
                v.tensor_tensor(bm[:, u % RING, :], delta[:, k, 0 if u < NS else 1, :], pB[:, u % 2, OFF:OFF + S], ALU.mult)\
                    .then_inc(s["bm"], 1)

            def finish(b, i, k):
                dve.wait_ge(s["wo"], at(b, NU, NU))
                dve.wait_ge(s["hb"], at(b, 1, 1))
                dve.wait_ge(s_out[k], i * 16)
                for c in range(3):
                    n = 2 if c < 2 else 1
                    ins = v.tensor_tensor(ho[:, k, 2 * c:2 * c + n, :],
                                          pA[:, c, 0:n * D].rearrange("p (t d) -> p t d", t=n),
                                          hb[:, k, 2 * c:2 * c + n, :], ALU.add)
                ins.then_inc(s["fin"], 1)

            dve.sem_inc(s["yl"], CREDIT)

            def low(b, u):
                m = splits(u) - 1
                dve.wait_ge(s["yh"], at(b, NSP, m + 1))
                v.tensor_tensor(yp[LO][:, m % YR, :], ys[:, u % RING, :], yp[HI][:, m % YR, :].bitcast(F32),
                                ALU.subtract).then_inc(s["yl"], 1)

            weigh(0, 0, 0)

            def body(b, i, k, first, last):
                for u in range(NU):
                    if u < NU - 1:
                        weigh(b, k, u + 1)
                    elif not last:
                        weigh(b + 1, 1 - k, 0)
                    dve.wait_ge(s["ae"], at(b, NU, u + 1))
                    dve.wait_ge(s["bm"], at(b, NU, u + 1))
                    dve.wait_ge(s["ys"], at(b, NU, u + 1 - RING))
                    v.tensor_tensor_scan(hs[:, u % RING, :], ae[:, u % RING, :], bm[:, u % RING, :], 0.0,
                                         ALU.mult, ALU.add).then_inc(s["hs"], 1)
                    if (u >= LO_LAG or not first) and is_split(u - LO_LAG):
                        low(b, u - LO_LAG)
                    if u == LAG and not first:
                        finish(b - 1, i - 1 + k, 1 - k)
                    if not last:
                        if u == 0:
                            front_stat(b + 1, i + k, 1 - k)
                        if u - 3 in FRONT_AT:
                            front_dve_late(b + 1, i + k, 1 - k, FRONT_AT[u - 3])
                        if FRONT_AT.get(u - 3, FS) < 7:
                            front_dve(b + 1, i + k, 1 - k, FRONT_AT[u - 3])
                        if FRONT_AT.get(u - 1, 0) >= 7:
                            front_dve(b + 1, i + k, 1 - k, FRONT_AT[u - 1])

            batches(dve, body)
            for u in range(NU - LO_LAG, NU):
                if is_split(u):
                    low(NB - 1, u)
            finish(NB - 1, NB // 2 - 1, 1)


def dense_experts(nc, h1, gate_w, gate_b, bias, wu, bu, wg, bg, wd, bd, swu, sbu, swg, sbg, swd, sbd, h2):
    E, HID, G = 16, 128, 8
    EA = E + 1
    CT, NC = 4, T // (4 * TP)
    N = CT * TP
    STAT_AT, FRONT_AT = 0, {3: 0, 4: 1, 5: 2, 15: 3, 16: 4}
    ROUTE_AT = {6: (0,), 8: (1,), 9: (2,), 10: (3,), 11: (4,), 12: (5,), 13: (6,), 14: (7, 8)}
    FS = 5
    VP = 1 + 1 + RSQRT_STEPS + 1
    RP = 20
    HI, LO = 0, 1
    PARTS = ((HI, HI), (HI, LO), (LO, HI))
    keep = ExitStack()
    sbk = lambda name, shape: keep.enter_context(nc.sbuf_tensor("cw_" + name, shape, F32R))
    wu_s, wg_s = ([sbk(f"{n}{p}", [KC, KT, EA, HID]) for p in range(2)] for n in ("wu", "wg"))
    wd_s = [sbk(f"wd{p}", [HID, EA, D]) for p in range(2)]

    with ExitStack() as ctx:
        sem = semaphores(nc, ctx, "cw_")
        raw = [ctx.enter_context(nc.sbuf_tensor(f"cw_raw{n}", [HID if n == 2 else KC, EA * (D if n == 2 else KT * HID)], F32))
               for n in range(3)]
        s_raw, s_hi, s_lo = [sem(f"s_raw{n}") for n in range(3)], sem("s_hi"), sem("s_lo")
        flat = [[w[:, :, :, :].rearrange("p c e n -> p (c e n)") for w in wu_s],
                [w[:, :, :, :].rearrange("p c e n -> p (c e n)") for w in wg_s],
                [w[:, :, :].rearrange("p e n -> p (e n)") for w in wd_s]]
        block = ctx.enter_context(nc.Block())

        @block.sync
        def _(sp):
            for n, (we, ws) in enumerate(((wu, swu), (wg, swg))):
                dst = raw[n][:, :].rearrange("p (c e n) -> p c e n", c=KT, e=EA)
                for c in range(KT):
                    sp.dma_start(dst[:, c, 0:E, :], we[:, c * KC:(c + 1) * KC, :].rearrange("e p n -> p e n"))\
                        .then_inc(s_raw[n], 16)
                sp.dma_start(dst[:, :, E, :], ws.rearrange("(c p) n -> p c n", p=KC)).then_inc(s_raw[n], 16)
            dst = raw[2][:, :].rearrange("p (e n) -> p e n", e=EA)
            sp.dma_start(dst[:, 0:E, :], wd.rearrange("e p n -> p e n")).then_inc(s_raw[2], 16)
            sp.dma_start(dst[:, E, :], swd).then_inc(s_raw[2], 16)

        @block.scalar
        def _(act):
            for n in range(3):
                act.wait_ge(s_raw[n], 48 if n < 2 else 32)
                act.activation(flat[n][HI], raw[n][:, :], ACT.Copy).then_inc(s_hi, 1)

        @block.vector
        def _(dve):
            for n in range(3):
                dve.wait_ge(s_hi, n + 1)
                nc.vector.tensor_tensor(flat[n][LO], raw[n][:, :], flat[n][HI].bitcast(F32), ALU.subtract).then_inc(s_lo, 1)

    with keep, ExitStack() as ctx:
        sb = lambda name, shape, dt=F32: ctx.enter_context(nc.sbuf_tensor("c_" + name, shape, dt))
        ps = lambda name, shape: ctx.enter_context(nc.psum_tensor("c_" + name, shape, F32))
        sem = semaphores(nc, ctx, "c_")
        ident = sb("ident", [128, 128])
        bn = sb("bn", [EA, 2, HID])
        bc = sb("bc", [HID, 2, EA])
        bd_s = sb("bd_s", [EA, D])
        gw_s = sb("gw_s", [KC, KT, E])
        gb_s, bi_s = sb("gb_s", [TP, E]), sb("bi_s", [TP, E])
        tri = sb("tri", [TP, E, E])
        h, y = sb("h", [TP, 2, CT, D]), sb("y", [TP, 2, CT, D])
        xn = sb("xn", [TP, CT, D])
        stats, mv = sb("stats", [TP, CT, 6]), sb("mv", [TP, CT, 2])
        ve, rs, hh, nb_ = (sb(n, [TP, CT]) for n in ("ve", "rs", "hh", "nb"))
        xT = sb("xT", [KC, 2, KT, N])
        xp = [sb(f"xp{p}", [KC, 2, KT, N], F32R) for p in range(2)]
        lg, sc, sm = sb("lg", [TP, CT, E]), sb("sc", [TP, CT, E]), sb("sm", [TP, CT, E])
        mx, sums = sb("mx", [TP, CT]), sb("sums", [TP, CT])
        gs, gm = sb("gs", [TP, CT, G]), sb("gm", [TP, CT, G])
        c1, c2 = sb("c1", [TP, CT, E, E]), sb("c2", [TP, CT, E, E])
        rk = sb("rk", [TP, CT, E])
        w = sb("w", [TP, 2, CT, EA])
        wT = sb("wT", [EA, N])
        su, ac = sb("su", [HID, 2, N]), sb("ac", [HID, 2, N])
        ap = [sb(f"ap{p}", [HID, 2, N], F32R) for p in range(2)]
        pU, pG = ps("pU", [HID, 2, 512]), ps("pG", [HID, 2, 512])
        pD, pF = ps("pD", [TP, 2, 512]), ps("pF", [128, 2, 512])

        s_w, s_id0, s_id, s_bn, s_bc, s_va, s_ro, s_go = (sem(n) for n in (
            "s_w", "s_id0", "s_id", "s_bn", "s_bc", "s_va", "s_ro", "s_go"))
        s_h = [sem(f"s_h{k}") for k in range(2)]
        s_out = [sem(f"s_out{k}") for k in range(2)]
        s = {n: sem("q_" + n) for n in ("stat", "xn", "front", "xT", "lg", "lg0", "exp", "w", "wT", "y0", "ug", "su", "xh", "xl", "hi", "lo",
                                        "ac", "dn", "acc", "accv")}
        N_W = 16 * 9
        block = ctx.enter_context(nc.Block())
        v = nc.vector
        tiles = lambda x, c: x[bass.ds(c * N, N), :].rearrange("(t p) d -> p t d", p=TP)

        @block.sync
        def _(sp):
            row = lambda x: x.rearrange("(a d) -> a d", a=1)
            for c in range(2):
                sp.dma_start(h[:, c, :, :], tiles(h1, c)).then_inc(s_h[c], 16)
            sp.dma_start(gw_s[:, :, :], gate_w.rearrange("(c p) e -> p c e", p=KC)).then_inc(s_w, 16)
            sp.dma_start(gb_s[:, :], row(gate_b).broadcast_to([TP, E])).then_inc(s_w, 16)
            sp.dma_start(bi_s[:, :], row(bias).broadcast_to([TP, E])).then_inc(s_w, 16)
            for n, (be, bsh) in enumerate(((bu, sbu), (bg, sbg))):
                sp.dma_start(bn[0:E, n, :], be).then_inc(s_w, 16)
                sp.dma_start(bn[E:EA, n, :], row(bsh)).then_inc(s_w, 16)
            sp.dma_start(bd_s[0:E, :], bd).then_inc(s_w, 16)
            sp.dma_start(bd_s[E:EA, :], row(sbd)).then_inc(s_w, 16)

            def body(c, i, k, last):
                if not last:
                    sp.wait_ge(s["y0"], at(c, 1, 1))
                    sp.dma_start(h[:, k, :, :], tiles(h1, c + 2)).then_inc(s_h[k], 16)
                sp.wait_ge(s["acc"], at(c, EA, EA))
                sp.dma_start(tiles(h2, c), y[:, k, :, :]).then_inc(s_out[k], 16)

            two_a_turn(sp, NC, body)
            for k in range(2):
                sp.wait_ge(s_out[k], 16 * (NC // 2))

        @block.gpsimd
        def _(pool):
            pool.memset(ident[:, :], 0.0).then_inc(s_id0, 1)
            pool.memset(tri[:, :, :], 0.0).then_inc(s_id0, 1)
            pool.memset(w[:, :, :, :], 1.0).then_inc(s_id0, 1)
            pool.wait_ge(s_id0, 3)
            pool.affine_select(out=ident[:, :], in_=ident[:, :], compare_op=ALU.not_equal, fill=1.0, base=0,
                               pattern=[[-1, 128]], channel_multiplier=1).then_inc(s_id, 1)
            pool.wait_ge(s_id, 1)
            pool.affine_select(out=tri[:, :, :], in_=tri[:, :, :], compare_op=ALU.is_ge, fill=1.0, base=0,
                               pattern=[[-1, E], [1, E]], channel_multiplier=0).then_inc(s_id, 1)

            for n in ("lo", "xl"):
                pool.sem_inc(s[n], CREDIT)

            def x_low(c, k):
                pool.wait_ge(s["xh"], at(c, 1, 1))
                nc.gpsimd.tensor_tensor(xp[LO][:, k, :, :], xT[:, k, :, :], xp[HI][:, k, :, :].bitcast(F32), ALU.subtract)\
                    .then_inc(s["xl"], 1)

            x_low(0, 0)

            def body(c, i, k, last):
                for e in range(EA):
                    r = (e + k) % 2
                    pool.wait_ge(s["hi"], at(c, EA, e + 1))
                    pool.wait_ge(s["dn"], at(c, EA, e - 1))
                    nc.gpsimd.tensor_tensor(ap[LO][:, r, :], ac[:, r, :], ap[HI][:, r, :].bitcast(F32), ALU.subtract)\
                        .then_inc(s["lo"], 1)
                    if e == 8 and last < 2:
                        x_low(c + 1, 1 - k)

            two_a_turn(pool, NC, body)

        def front_pe(c, i, k, step):
            pe = nc.tensor
            if step < 2:
                if step == 0:
                    pe.wait_ge(s["xn"], at(c, 1, 1))
                    pe.wait_ge(s["y0"], at(c, 1, 0))
                else:
                    pe.wait_ge(s["xT"], at(c, 2, 1))
                for t in range(CT):
                    ins = pe.transpose(pF[0:KC, 0, t * TP:(t + 1) * TP], xn[:, t, step * KC:(step + 1) * KC],
                                       ident[0:TP, 0:TP])
            elif step == 2:
                pe.wait_ge(s["xT"], at(c, 2, 2))
                for t in range(CT):
                    for cc in range(KT):
                        ins = pe.matmul(pF[0:TP, 0, t * E:(t + 1) * E], xT[:, k, cc, t * TP:(t + 1) * TP],
                                        gw_s[:, cc, :], start=(cc == 0), stop=(cc == KT - 1))
            elif step == 3:
                pe.wait_ge(s["w"], at(c, 1, 1))
                for t in range(CT):
                    ins = pe.transpose(pF[0:EA, 0, t * TP:(t + 1) * TP], w[:, k, t, :], ident[0:TP, 0:TP])
            else:
                pe.wait_ge(s["wT"], at(c, 1, 1))
                for t in range(CT):
                    ins = pe.matmul(pF[0:TP, t // 2, (t % 2) * D:(t % 2 + 1) * D], wT[:, t * TP:(t + 1) * TP],
                                    bd_s[:, :], start=True, stop=True)
            ins.then_inc(s["front"], 1)

        @block.tensor
        def _(pe):
            for n in ("front", "ug", "dn"):
                pe.sem_inc(s[n], CREDIT)
            pe.wait_ge(s_w, N_W)
            pe.wait_ge(s_id, 2)
            for n in range(2):
                ins = pe.transpose(pF[:, 0, n * EA:(n + 1) * EA], bn[:, n, :], ident[0:EA, 0:EA])
            ins.then_inc(s_bn, 1)
            pe.wait_ge(s_bc, 1)
            for step in range(FS):
                front_pe(0, 0, 0, step)

            def up_gate(c, k, e):
                if e == 0:
                    pe.wait_ge(s["xl"], at(c, 1, 1))
                pe.wait_ge(s["ac"], at(c, EA, e - 1))
                for p, ws in ((pU, wu_s), (pG, wg_s)):
                    for n, (cc, (a, b)) in enumerate((cc, ab) for cc in range(KT) for ab in PARTS):
                        ins = pe.matmul(p[:, (e + k) % 2, 0:N], ws[b][:, cc, e, :], xp[a][:, k, cc, :],
                                        start=(n == 0), stop=(n == 3 * KT - 1))
                ins.then_inc(s["ug"], 1)

            def down(c, k, e):
                pe.wait_ge(s["lo"], at(c, EA, e + 1))
                pe.wait_ge(s["acc"], at(c, EA, e))
                for t in range(CT):
                    for n, (a, b) in enumerate(PARTS):
                        ins = pe.matmul(pD[:, t // 2, (t % 2) * D:(t % 2 + 1) * D],
                                        ap[a][:, (e + k) % 2, t * TP:(t + 1) * TP], wd_s[b][:, e, :],
                                        start=(n == 0), stop=(n == 2))
                ins.then_inc(s["dn"], 1)

            up_gate(0, 0, 0)

            def body(c, i, k, last):
                for e in range(EA):
                    if e < EA - 1:
                        up_gate(c, k, e + 1)
                    elif last < 2:
                        up_gate(c + 1, 1 - k, 0)
                    if e > 0:
                        down(c, k, e - 1)
                    if e in FRONT_AT and last < 2:
                        front_pe(c + 1, i + k, 1 - k, FRONT_AT[e])
                down(c, k, EA - 1)

            two_a_turn(pe, NC, body)

        def front_act(c, i, k, step):
            act = nc.scalar
            if step in (0, 1):
                act.wait_ge(s["front"], at(c, FS, step + 1))
                act.activation(xT[:, k, step, :], pF[0:KC, 0, 0:N], ACT.Copy).then_inc(s["xT"], 1)
                if step == 1:
                    act.wait_ge(s["xT"], at(c, 2, 2))
                    act.wait_ge(s["ug"], at(c, EA, -EA))
                    act.activation(xp[HI][:, k, :, :], xT[:, k, :, :], ACT.Copy).then_inc(s["xh"], 1)
            elif step == 3:
                act.wait_ge(s["front"], at(c, FS, 4))
                act.activation(wT[:, :], pF[0:EA, 0, 0:N], ACT.Copy).then_inc(s["wT"], 1)

        def normalise(c, i, k):
            act = nc.scalar
            act.wait_ge(s["stat"], at(c, 1, 1))
            act.wait_ge(s["front"], at(c, FS, 0))
            for t in range(CT):
                ins = act.activation(xn[:, t, :], h[:, k, t, :], ACT.Identity, bias=nb_[:, t:t + 1],
                                     scale=rs[:, t:t + 1])
            ins.then_inc(s["xn"], 1)

        def exps(c):
            act = nc.scalar
            act.wait_ge(s["lg"], at(c, 1, 1))
            act.activation(sc[:, :, :], lg[:, :, :], ACT.Exp).then_inc(s["exp"], 1)

        @block.scalar
        def _(act):
            for n in ("xn", "xT", "wT", "su", "exp", "xh", "hi"):
                act.sem_inc(s[n], CREDIT)
            act.wait_ge(s_bn, 1)
            act.activation(bc[:, :, :], pF[:, 0, 0:2 * EA].rearrange("p (n e) -> p n e", n=2), ACT.Copy)\
                .then_inc(s_bc, 1)
            act.wait_ge(s_bc, 1)
            normalise(0, 0, 0)
            for step in range(2):
                front_act(0, 0, 0, step)
            exps(0)
            front_act(0, 0, 0, 3)

            def body(c, i, k, last):
                for e in range(EA):
                    r = (e + k) % 2
                    act.wait_ge(s["ug"], at(c, EA, e + 1))
                    act.wait_ge(s["ac"], at(c, EA, e - 1))
                    act.activation(su[:, r, :], pU[:, r, 0:N], ACT.Silu, bias=bc[:, 0, e:e + 1]).then_inc(s["su"], 1)
                    act.wait_ge(s["ac"], at(c, EA, e + 1))
                    act.wait_ge(s["dn"], at(c, EA, e - 1))
                    act.activation(ap[HI][:, r, :], ac[:, r, :], ACT.Copy).then_inc(s["hi"], 1)
                    if last < 2:
                        if e == STAT_AT + 2:
                            normalise(c + 1, i + k, 1 - k)
                        if e - 1 in FRONT_AT:
                            front_act(c + 1, i + k, 1 - k, FRONT_AT[e - 1])
                        if 0 in ROUTE_AT.get(e - 1, ()):
                            exps(c + 1)

            two_a_turn(act, NC, body)

        def statistics(c, i, k):
            dve = nc.vector
            st = Steps(dve, s_va, VP, c)
            dve.wait_ge(s_h[k], i * 16 + 16)
            dve.wait_ge(s["xn"], at(c, 1, 0))
            for t in range(CT):
                ins = v.bn_stats(stats[:, t, :], h[:, k, t, :])
            st.after(ins)
            dve.sem_inc(s_go, 1)
            for t in range(CT):
                ins = v.bn_aggr(mv[:, t, :], stats[:, t, :])
            st.after(ins)
            st.after(v.tensor_scalar(ve[:, :], mv[:, :, 1], 1e-5, None, ALU.add))
            rsqrt(nc, st, rs[:, :], ve[:, :], hh[:, :])
            st.end()
            v.scalar_tensor_tensor(nb_[:, :], mv[:, :, 0], -1.0, rs[:, :], ALU.mult, ALU.mult).then_inc(s["stat"], 1)

        def ranks(st, x, n, steps=range(5)):
            shape = [TP, CT, n, n]
            mine = x.rearrange("p t (e a) -> p t e a", a=1).broadcast_to(shape)
            theirs = x.rearrange("p t (a f) -> p t a f", a=1).broadcast_to(shape)
            a, b = c1[:, :, 0:n, 0:n], c2[:, :, 0:n, 0:n]
            tr = tri[:, 0:n, 0:n].rearrange("p (a e) f -> p a e f", a=1).broadcast_to(shape)
            for step in steps:
                if step == 0:
                    st.after(v.tensor_tensor(a, theirs, mine, ALU.is_gt))
                elif step == 1:
                    st.after(v.tensor_tensor(b, theirs, mine, ALU.is_equal))
                elif step == 2:
                    st.after(v.tensor_tensor(b, b, tr, ALU.mult))
                elif step == 3:
                    st.after(v.tensor_tensor(a, a, b, ALU.add))
                else:
                    st.after(v.tensor_reduce(rk[:, :, 0:n], a, AX, ALU.add))

        def route(c, k, part, st):
            dve = nc.vector
            wide = lambda x, n=E: x[:, :].rearrange("p (t a) -> p t a", a=1).broadcast_to([TP, CT, n])
            flat = lambda x: x[:, :].rearrange("p (a e) -> p a e", a=1).broadcast_to([TP, CT, E])
            if part == 0:
                dve.wait_ge(s["front"], at(c, FS, 3))
                st.after(v.tensor_tensor(lg[:, :, :], pF[0:TP, 0, 0:CT * E].rearrange("p (t e) -> p t e", t=CT),
                                         flat(gb_s), ALU.add))
                st.after(v.tensor_reduce(mx[:, :], lg[:, :, :], AX, ALU.max))
                v.tensor_tensor(lg[:, :, :], lg[:, :, :], wide(mx), ALU.subtract).then_inc(s["lg"], 1)
            elif part == 1:
                dve.wait_ge(s["exp"], at(c, 1, 1))
                st.after(v.tensor_reduce(sums[:, :], sc[:, :, :], AX, ALU.add))
                st.after(v.reciprocal(sums[:, :], sums[:, :]))
                st.after(v.tensor_tensor(sc[:, :, :], sc[:, :, :], wide(sums), ALU.mult))
                st.after(v.tensor_tensor(sm[:, :, :], sc[:, :, :], flat(bi_s), ALU.add))
                pair = sm[:, :, :].rearrange("p t (g a) -> p t g a", a=2)
                st.after(v.tensor_tensor(gs[:, :, :], pair[:, :, :, 0], pair[:, :, :, 1], ALU.add))
            elif part == 2:
                ranks(st, gs[:, :, :], G)
                st.after(v.tensor_scalar(gm[:, :, :], rk[:, :, 0:G], 3.5, -3.0e38, ALU.is_gt, ALU.mult))
                pair = sm[:, :, :].rearrange("p t (g a) -> p t g a", a=2)
                st.after(v.tensor_tensor(pair, pair, gm[:, :, :].rearrange("p t (g a) -> p t g a", a=1)
                                         .broadcast_to([TP, CT, G, 2]), ALU.add))
            elif part < 8:
                ranks(st, sm[:, :, :], E, (part - 3,))
            else:
                st.after(v.tensor_scalar(rk[:, :, :], rk[:, :, :], 3.5, 2.5, ALU.is_lt, ALU.mult))
                dve.wait_ge(s["acc"], at(c, EA, -EA))
                v.tensor_tensor(w[:, k, :, 0:E], sc[:, :, :], rk[:, :, :], ALU.mult).then_inc(s["w"], 1)
                st.end()

        def first_sum(c, i, k):
            dve = nc.vector
            dve.wait_ge(s["front"], at(c, FS, 5))
            dve.wait_ge(s_out[k], i * 16)
            for n in range(2):
                ins = v.tensor_tensor(y[:, k, 2 * n:2 * n + 2, :],
                                      pF[0:TP, n, 0:2 * D].rearrange("p (t d) -> p t d", t=2),
                                      h[:, k, 2 * n:2 * n + 2, :], ALU.add)
            ins.then_inc(s["y0"], 1)

        @block.vector
        def _(dve):
            for n in ("stat", "lg", "w", "y0", "ac", "acc", "accv"):
                dve.sem_inc(s[n], CREDIT)
            dve.wait_ge(s_w, N_W)
            dve.wait_ge(s_id, 2)
            statistics(0, 0, 0)
            st = Steps(dve, s_ro, RP, 0)
            for part in range(9):
                route(0, 0, part, st)
            first_sum(0, 0, 0)

            def hidden(c, k, e):
                r = (e + k) % 2
                dve.wait_ge(s["su"], at(c, EA, e + 1))
                dve.wait_ge(s["lo"], at(c, EA, e - 1))
                v.scalar_tensor_tensor(ac[:, r, :], pG[:, r, 0:N], bc[:, 1, e:e + 1], su[:, r, :],
                                       ALU.add, ALU.mult).then_inc(s["ac"], 1)

            def weigh(c, k, e):
                dve.wait_ge(s["dn"], at(c, EA, e + 1))
                if e == 0:
                    dve.wait_ge(s["y0"], at(c, 1, 1))
                    dve.wait_ge(s["w"], at(c, 1, 1))
                else:
                    dve.wait_ge(s["acc"], at(c, EA, e))
                for t in range(CT):
                    yt = y[:, k, t, :]
                    ins = v.scalar_tensor_tensor(yt, pD[:, t // 2, (t % 2) * D:(t % 2 + 1) * D],
                                                 w[:, k, t, e:e + 1], yt, ALU.mult, ALU.add)
                ins.then_inc(s["acc"], 1)

            hidden(0, 0, 0)

            def body(c, i, k, last):
                st = Steps(dve, s_ro, RP, c + 1)
                for e in range(EA):
                    if e < EA - 1:
                        hidden(c, k, e + 1)
                    elif last < 2:
                        hidden(c + 1, 1 - k, 0)
                    if e > 0:
                        weigh(c, k, e - 1)
                    if last < 2:
                        if e == STAT_AT:
                            statistics(c + 1, i + k, 1 - k)
                        for part in ROUTE_AT.get(e, ()):
                            route(c + 1, 1 - k, part, st)
                weigh(c, k, EA - 1)
                if last < 2:
                    first_sum(c + 1, i + k, 1 - k)

            two_a_turn(dve, NC, body)


def LN_SIGNALS():
    return 2 + RSQRT_STEPS + 1


def row_statistics(nc, st, go, rows, n, stats, mv, ve, rs, hh, nb_, eps, done):
    v = nc.vector
    for t in range(n):
        ins = v.bn_stats(stats[:, t, :], rows[:, t, :])
    st.after(ins)
    st.eng.sem_inc(go, 1)
    for t in range(n):
        ins = v.bn_aggr(mv[:, t, :], stats[:, t, :])
    st.after(ins)
    st.after(v.tensor_scalar(ve[:, :], mv[:, :, 1], eps, None, ALU.add))
    rsqrt(nc, st, rs[:, :], ve[:, :], hh[:, :])
    v.scalar_tensor_tensor(nb_[:, :], mv[:, :, 0], -1.0, rs[:, :], ALU.mult, ALU.mult).then_inc(done, 1)


MAGIC = 1.5 * 2.0 ** 23
NHD, HD, HG = 12, 16, 3
HP = 32


def quant_scale(nc, st, sc, inv, amax):
    st.after(nc.vector.tensor_scalar(sc, amax, 1.0 / 127.0, 1e-8, ALU.mult, ALU.max))
    st.after(nc.vector.reciprocal(inv, sc))


def attention_inputs(nc, h2, w_qkv, b_qkv, w_proj, xn_d, xt_d, v_d, qk_d, vq_d, K):
    v, a = nc.vector, nc.scalar
    with ExitStack() as ctx:
        sb = lambda name, shape, dt=F32: ctx.enter_context(nc.sbuf_tensor("d_" + name, shape, dt))
        sem = semaphores(nc, ctx, "d_")
        ps = lambda name, shape, dt=F32: ctx.enter_context(nc.psum_tensor("d_" + name, shape, dt))
        h, xn = sb("h", [TP, 2, TT, D]), sb("xn", [TP, 2, TT, D])
        stats, mv = sb("stats", [TP, TT, 6]), sb("mv", [TP, TT, 2])
        ve, hh = sb("ve", [TP, TT]), sb("hh", [TP, TT])
        rs, nb_ = sb("rs", [TP, 2, TT]), sb("nb", [TP, 2, TT])
        m1 = sb("m1", [TP, 1])
        wq_n, wp_n = sb("wq_n", [KC, 6, D]), sb("wp_n", [KC, 2, D])
        wq_b, wp_b = sb("wq_b", [KC, 6, D], BF16), sb("wp_b", [KC, 2, NHD, HP], BF16)
        pT = ps("pT", [128, 2, 1024], BF16)
        s_mx = sem("s_mx")
        s_w, s_v, s_v2, s_go, s_id0, s_id, s_all, s_t, s_tc, s_m0, s_gs = (sem(n) for n in (
            "s_w", "s_v", "s_v2", "s_go", "s_id0", "s_id", "s_all", "s_t", "s_tc", "s_m0", "s_gs"))
        s_h = [sem(f"s_h{k}") for k in range(2)]
        s_out = [sem(f"s_out{k}") for k in range(2)]
        s = {n: sem("q_" + n) for n in ("stat", "xn", "max")}
        block = ctx.enter_context(nc.Block())
        rows = lambda x, b: x[bass.ds(b * S, S), :].rearrange("(t p) d -> p t d", p=TP)
        PER = LN_SIGNALS()

        @block.sync
        def _(sp):
            sp.dma_start(wq_n[:, :, :], w_qkv.rearrange("(r p) c -> p r c", p=KC)).then_inc(s_w, 16)
            sp.dma_start(wp_n[:, :, :], w_proj.rearrange("(r p) c -> p r c", p=KC)).then_inc(s_w, 16)
            sp.wait_ge(s_id0, 6)
            for j in range(4):
                src = b_qkv[0:2 * D].rearrange("(g j d) -> j d g", j=4, d=HD)[j]
                sp.dma_start(K["bqk"][HP * j:HP * j + HD, :], src, allow_slow_non_contiguous=True).then_inc(K["s_b"], 16)
            sp.dma_start(K["bv"][:, :], b_qkv[2 * D:3 * D].rearrange("(a d) -> a d", a=1).broadcast_to([TP, D]))\
                .then_inc(s_w, 16)

            def store(b, k):
                sp.wait_ge(s["xn"], at(b, 1, 1))
                sp.sem_inc(s_gs, 1)
                sp.dma_start(xn_d[b], xn[:, k, :, :].rearrange("p t d -> p (t d)")).then_inc(s_out[k], 16)

            sp.dma_start(h[:, 0, :, :], rows(h2, 0)).then_inc(s_h[0], 16)
            sp.dma_start(h[:, 1, :, :], rows(h2, 1)).then_inc(s_h[1], 16)

            def turn(b, i, k, last):
                store(b, k)
                if not last:
                    sp.dma_start(h[:, k, :, :], rows(h2, b + 2)).then_inc(s_h[k], 16)

            two_a_turn(sp, NB, turn)
            for k in range(2):
                sp.wait_ge(s_out[k], 16 * (NB // 2))

        @block.gpsimd
        def _(pool):
            pool.memset(K["ident"][:, :], 0.0).then_inc(s_id0, 1)
            pool.memset(K["wT"][:, :, :], 0.0).then_inc(s_id0, 1)
            pool.memset(wp_b[:, :, :, :], 0.0).then_inc(s_id0, 1)
            pool.memset(K["bqk"][:, :], 0.0).then_inc(s_id0, 1)
            pool.memset(K["amax"][:, :], 0.0).then_inc(s_id0, 1)
            pool.memset(K["pad"][:, :, :], 0.0).then_inc(s_id0, 1)
            pool.wait_ge(s_id0, 6)
            pool.affine_select(out=K["ident"][:, :], in_=K["ident"][:, :], compare_op=ALU.not_equal, fill=1.0, base=0,
                               pattern=[[-1, 128]], channel_multiplier=1).then_inc(s_id, 1)
            pool.wait_ge(s_id, 1)
            pool.affine_select(out=K["pad"][:, :, :], in_=K["pad"][:, :, :], compare_op=ALU.not_equal, fill=1.0,
                               base=-HD, pattern=[[-HP, 4], [-1, 3]], channel_multiplier=1).then_inc(s_id, 1)
            pool.wait_ge(s_m0, 1)
            pool.partition_all_reduce(K["gmax"][:, 0:3], K["amax"][:, 0:3], 128, bass.bass_isa.ReduceOp.max)\
                .then_inc(s_all, 1)

        @block.scalar
        def _(act):
            act.sem_inc(s["xn"], CREDIT)

            def body(b, i, k, last):
                act.wait_ge(s["stat"], at(b, 1, 1))
                act.wait_ge(s["max"], at(b, 1, -1))
                act.wait_ge(s_out[k], i * 16)
                act.sem_inc(s_go, 1)
                for t in range(TT):
                    ins = act.activation(xn[:, k, t, :], h[:, k, t, :], ACT.Identity, bias=nb_[:, k, t:t + 1],
                                         scale=rs[:, k, t:t + 1])
                ins.then_inc(s["xn"], 1)

            two_a_turn(act, NB, body)

        @block.vector
        def _(dve):
            dve.sem_inc(s["stat"], CREDIT)
            dve.sem_inc(s["max"], CREDIT)
            dve.wait_ge(s_id0, 6)

            def stat(b, i, k):
                st = Steps(dve, s_v, PER, b)
                dve.wait_ge(s_h[k], i * 16 + 16)
                dve.wait_ge(s["xn"], at(b, 1, -1))
                row_statistics(nc, st, s_go, h[:, k, :, :], TT, stats, mv, ve, rs[:, k, :], hh, nb_[:, k, :], 1e-5,
                               s["stat"])
                st.end()

            stat(0, 0, 0)

            def body(b, i, k, last):
                if last < 2:
                    stat(b + 1, i + k, 1 - k)
                dve.wait_ge(s["xn"], at(b, 1, 1))
                st = Steps(dve, s_mx, 1, b)
                st.after(v.tensor_reduce(m1[:, :], xn[:, k, :, :].rearrange("p t d -> p (t d)"), AX, ALU.max,
                                         apply_absolute_value=True))
                v.tensor_tensor(K["amax"][0:TP, 0:1], K["amax"][0:TP, 0:1], m1[:, :], ALU.max).then_inc(s["max"], 1)
                dve.wait_ge(s["max"], at(b, 1, 1))
                st.end()

            two_a_turn(dve, NB, body)
            dve.wait_ge(s_w, 48)
            st = Steps(dve, s_v2)
            st.counted(v.tensor_reduce(K["amax"][0:KC, 1:2], wq_n[:, :, :].rearrange("p r c -> p (r c)"), AX, ALU.max,
                                      apply_absolute_value=True))
            v.tensor_reduce(K["amax"][0:KC, 2:3], wp_n[:, :, :].rearrange("p r c -> p (r c)"), AX, ALU.max,
                            apply_absolute_value=True).then_inc(s_m0, 1)
            dve.wait_ge(s_all, 1)
            quant_scale(nc, st, K["sc"][:, 0:3], K["inv"][:, 0:3], K["gmax"][:, 0:3])
            st.after(v.tensor_scalar(wq_n[:, :, :], wq_n[:, :, :], K["inv"][0:KC, 1:2], MAGIC, ALU.mult, ALU.add))
            st.counted(v.tensor_scalar(wq_b[:, :, :], wq_n[:, :, :], -MAGIC, None, ALU.add))
            st.after(v.tensor_scalar(wp_n[:, :, :], wp_n[:, :, :], K["inv"][0:KC, 2:3], MAGIC, ALU.mult, ALU.add))
            for r in range(2):
                st.after(v.tensor_scalar(wp_b[:, r, :, 0:HD], wp_n[:, r, :].rearrange("p (h d) -> p h d", d=HD),
                                         -MAGIC, None, ALU.add))
            st.after(v.tensor_tensor(K["cq"][:, :], K["sc"][:, 0:1], K["sc"][:, 1:2], ALU.mult))
            dve.sem_inc(s_tc, 1)
            for c in range(KT):
                dve.wait_ge(s_t, c + 1)
                for r in range(4):
                    v.tensor_copy(K["wT"][:, c, r * 6 * HP:(r + 1) * 6 * HP].rearrange("p (h d) -> p h d", d=HP)[:, :, 0:HD],
                                  pT[0:KC, c, r * KC:(r + 1) * KC].rearrange("p (h d) -> p h d", d=HD))
                ins = v.tensor_copy(K["wvT"][:, c, :], pT[0:KC, c, 4 * KC:6 * KC])
            ins.then_inc(s_tc, 1)
            dve.wait_ge(s_t, 3)
            for g in range(HG):
                ins = v.tensor_copy(K["wpT"][:, g, :], pT[:, 0, g * D:(g + 1) * D])
            ins.then_inc(s_tc, 1)

        @block.tensor
        def _(pe):
            pe.wait_ge(s_tc, 1)
            pe.wait_ge(s_id, 1)
            for c in range(KT):
                for r in range(6):
                    ins = pe.transpose(pT[0:KC, c, r * KC:(r + 1) * KC], wq_b[:, r, c * KC:(c + 1) * KC],
                                       K["ident"][0:KC, 0:KC])
                ins.then_inc(s_t, 1)
            pe.wait_ge(s_tc, 2)
            wp = wp_b[:, :, :, :].rearrange("p r h d -> p r (h d)")
            for g in range(HG):
                for r in range(2):
                    ins = pe.transpose(pT[:, 0, g * D + r * KC:g * D + (r + 1) * KC], wp[:, r, g * 128:(g + 1) * 128],
                                       K["ident"][0:KC, 0:KC])
            ins.then_inc(s_t, 1)

    for again in range(2):
        with ExitStack() as ctx:
            pre = "ef"[again] + "_"
            sb = lambda name, shape, dt=F32: ctx.enter_context(nc.sbuf_tensor(pre + name, shape, dt))
            sem = semaphores(nc, ctx, pre)
            ps = lambda name, shape, dt=F32: ctx.enter_context(nc.psum_tensor(pre + name, shape, dt))
            x = sb("x", [TP, 2, TT * D])
            xr = sb("xr", [TP, 2, TT * D])
            xb = sb("xb", [TP, 2, TT * D], BF16)
            xT = sb("xT", [KC, 2, KT, S], BF16)
            vb = sb("vb", [TP, 2, TT, D])
            y = sb("y", [128, 2, S] if again == 0 else [128, 2, 6, S])
            qk = sb("qk", [128, 2, 6, S], BF16)
            vq = sb("vq", [TP, 2, TT, NHD, HP], BF16)
            mt = sb("mt", [128, 3])
            mtq = sb("mtq", [128, 6])
            pT = ps("pT", [KC, 2, 1024], BF16)
            pQ = ps("pQ", [128, 3, 1024])
            s_v, s_go, s_all, s_m0, s_k, s_gs = (sem(n) for n in ("s_v", "s_go", "s_all", "s_m0", "s_k", "s_gs"))
            s_x = [sem(f"s_x{k}") for k in range(2)]
            s_o1 = [sem(f"s_o1{k}") for k in range(2)]
            s_o2 = [sem(f"s_o2{k}") for k in range(2)]
            s = {n: sem("q_" + n) for n in ("xr", "xb", "tr", "xT", "qk", "y", "max", "vb", "vmax", "q")}
            block = ctx.enter_context(nc.Block())

            if again == 0:
                R = 8

                @block.sync
                def _(sp):
                    def body(b, i, k, last):
                        sp.wait_ge(s["xr"], at(b, 1, -1))
                        sp.sem_inc(s_gs, 1)
                        sp.dma_start(x[:, k, :], xn_d[b]).then_inc(s_x[k], 16)

                    def store(b, k):
                        sp.wait_ge(s["xT"], at(b, 1, 1))
                        sp.sem_inc(s_gs, 1)
                        sp.dma_start(xt_d[b], xT[:, k, :, :].rearrange("p c l -> p (c l)")).then_inc(s_o1[k], 16)
                        sp.wait_ge(s["vb"], at(b, 1, 1))
                        sp.sem_inc(s_gs, 1)
                        sp.dma_start(v_d[b], vb[:, k, :, :].rearrange("p t d -> p (t d)")).then_inc(s_o2[k], 16)

                    for k in range(2):
                        body(k, 0, k, 0)

                    def turn(b, i, k, last):
                        if not last:
                            body(b + 2, i + 1, k, 0)
                        store(b, k)

                    two_a_turn(sp, NB, turn)
                    for k in range(2):
                        sp.wait_ge(s_o1[k], 16 * (NB // 2))
                        sp.wait_ge(s_o2[k], 16 * (NB // 2))

                @block.gpsimd
                def _(pool):
                    pool.wait_ge(s_m0, 1)
                    pool.partition_all_reduce(K["gmax"][:, 3:6], K["amax"][:, 3:6], 128, bass.bass_isa.ReduceOp.max)\
                        .then_inc(s_all, 1)

                @block.tensor
                def _(pe):
                    for n in ("tr", "qk"):
                        pe.sem_inc(s[n], CREDIT)

                    def body(b, i, k, last):
                        pe.wait_ge(s["xb"], at(b, 1, 1))
                        pe.wait_ge(s["xT"], at(b, 1, 0))
                        for c in range(KT):
                            for t in range(TT):
                                ins = pe.transpose(pT[:, c, t * (TP + 1):t * (TP + 1) + TP],
                                                   xb[:, k, t * D + c * KC:t * D + (c + 1) * KC],
                                                   K["ident"][0:TP, 0:TP])
                        ins.then_inc(s["tr"], 1)
                        pe.wait_ge(s["xT"], at(b, 1, 1))
                        for r in range(R):
                            if r < 6:
                                pe.wait_ge(s["y"], at(b, 6, r - 1 if r >= 2 else 0))
                                if r < 2:
                                    pe.wait_ge(s["vmax"], at(b, 2, 0))
                                for lo, hi in CUT:
                                    for c in range(KT):
                                        ins = pe.matmul(pQ[:, r % 2, OFF + lo:OFF + hi], K["wT"][:, c, r * 128:(r + 1) * 128],
                                                        xT[:, k, c, lo:hi], start=(c == 0), stop=(c == KT - 1))
                            else:
                                pe.wait_ge(s["y"], at(b, 6, r - 1))
                                for t in range(4 * (r - 6), min(4 * (r - 6) + 4, TT)):
                                    col = (t % 4) // 2 * 512 + t % 2 * D
                                    for c in range(KT):
                                        ins = pe.matmul(pQ[0:TP, r % 2, col:col + D],
                                                        xT[:, k, c, t * TP:(t + 1) * TP], K["wvT"][:, c, :],
                                                        start=(c == 0), stop=(c == KT - 1))
                            ins.then_inc(s["qk"], 1)

                    two_a_turn(pe, NB, body)

                @block.scalar
                def _(act):
                    for n in ("xT", "y"):
                        act.sem_inc(s[n], CREDIT)

                    def body(b, i, k, last):
                        act.wait_ge(s["tr"], at(b, 1, 1))
                        act.wait_ge(s_o1[k], i * 16)
                        act.wait_ge(s["qk"], at(b, R, -R))
                        for c in range(KT):
                            ins = act.activation(
                                xT[:, k, c, :].rearrange("p (t l) -> p t l", t=TT),
                                pT[:, c, 0:TT * (TP + 1)].rearrange("p (t l) -> p t l", t=TT)[:, :, 0:TP], ACT.Copy)
                        ins.then_inc(s["xT"], 1)
                        for r in range(6):
                            act.wait_ge(s["qk"], at(b, R, r + 1))
                            act.wait_ge(s["max"], at(b, 6, r - 1))
                            act.activation(y[:, r % 2, :], pQ[:, r % 2, OFF:OFF + S], ACT.Identity,
                                           bias=K["bqk"][:, r:r + 1], scale=K["cq"][:, 0:1]).then_inc(s["y"], 1)

                    two_a_turn(act, NB, body)

                @block.vector
                def _(dve):
                    for n in ("xr", "xb", "max", "vb", "vmax"):
                        dve.sem_inc(s[n], CREDIT)
                    dve.wait_ge(K["s_b"], 64)
                    st0 = Steps(dve, s_k)

                    def integers(b, i, k):
                        dve.wait_ge(s_x[k], i * 16 + 16)
                        dve.wait_ge(s["xb"], at(b, 1, -1))
                        v.tensor_scalar(xr[:, k, :], x[:, k, :], K["inv"][0:TP, 0:1], MAGIC, ALU.mult, ALU.add)\
                            .then_inc(s["xr"], 1)
                        dve.wait_ge(s["xr"], at(b, 1, 1))
                        dve.wait_ge(s["tr"], at(b, 1, -1))
                        v.tensor_scalar(xb[:, k, :], xr[:, k, :], -MAGIC, None, ALU.add).then_inc(s["xb"], 1)

                    integers(0, 0, 0)

                    def body(b, i, k, last):
                        PER = 5
                        st = Steps(dve, s_v, PER, b)
                        for r in range(6):
                            dve.wait_ge(s["y"], at(b, 6, r + 1))
                            v.tensor_reduce(mtq[:, r:r + 1], y[:, r % 2, :], AX, ALU.max,
                                            apply_absolute_value=True).then_inc(s["max"], 1)
                            if r == 2 and last < 2:
                                integers(b + 1, i + k, 1 - k)
                        dve.wait_ge(s_o2[k], i * 16)
                        for r in range(2):
                            dve.wait_ge(s["qk"], at(b, R, 7 + r))
                            for n in range(2 if r == 0 else 1):
                                m = 2 if r == 0 else 1
                                ins = v.scalar_tensor_tensor(
                                    vb[:, k, 4 * r + 2 * n:4 * r + 2 * n + m, :],
                                    pQ[0:TP, r, n * 512:n * 512 + m * D].rearrange("p (t d) -> p t d", t=m),
                                    K["cq"][0:TP, 0:1],
                                    K["bv"][:, :].rearrange("p (a d) -> p a d", a=1).broadcast_to([TP, m, D]),
                                    ALU.mult, ALU.add)
                            ins.then_inc(s["vmax"], 1)
                        dve.wait_ge(s["vmax"], at(b, 2, 2))
                        dve.sem_inc(s["vb"], 1)
                        st.after(v.tensor_reduce(mt[0:TP, 2:3], vb[:, k, :, :].rearrange("p t d -> p (t d)"), AX,
                                                 ALU.max, apply_absolute_value=True))
                        dve.wait_ge(s["max"], at(b, 6, 6))
                        st.after(v.tensor_reduce(mt[:, 0:2], mtq[:, :].rearrange("p (a g) -> p a g", a=2), AX,
                                                 ALU.max))
                        st.after(v.tensor_tensor(K["amax"][:, 3:5], K["amax"][:, 3:5], mt[:, 0:2], ALU.max))
                        st.after(v.tensor_tensor(K["amax"][0:TP, 5:6], K["amax"][0:TP, 5:6], mt[0:TP, 2:3], ALU.max))
                        st.n += 1
                        dve.sem_inc(s_v, 1)
                        st.end()

                    two_a_turn(dve, NB, body)
                    dve.sem_inc(s_m0, 1)
                    dve.wait_ge(s_all, 1)
                    quant_scale(nc, st0, K["sc"][:, 3:6], K["inv"][:, 3:6], K["gmax"][:, 3:6])
                    for n in range(2):
                        st0.counted(v.tensor_tensor(K["cqi"][:, n:n + 1], K["cq"][:, :], K["inv"][:, 3 + n:4 + n],
                                                   ALU.mult))
                        st0.after(v.tensor_scalar(K["bqi"][:, 3 * n:3 * n + 3], K["bqk"][:, 3 * n:3 * n + 3],
                                                  K["inv"][:, 3 + n:4 + n], None, ALU.mult))
                    st0.after(v.tensor_reduce(K["padc"][:, :], K["pad"][:, :, :].rearrange("p j i -> p (j i)"), AX,
                                              ALU.add))
                    st0.after(v.tensor_scalar(K["bqi"][:, 3:6], K["bqi"][:, 3:6], K["padc"][:, 0:1], None, ALU.add))
                    st0.after(v.scalar_tensor_tensor(K["cs"][:, :], K["sc"][:, 3:4], HD ** -0.5, K["sc"][:, 4:5],
                                                     ALU.mult, ALU.mult))
                    st0.after(v.reciprocal(K["csi"][:, :], K["cs"][:, :]))
            else:
                @block.sync
                def _(sp):
                    def load(b, i, k):
                        sp.wait_ge(s["qk"], at(b, 6, -6))
                        sp.sem_inc(s_gs, 1)
                        sp.dma_start(xT[:, k, :, :].rearrange("p c l -> p (c l)"), xt_d[b]).then_inc(s_x[k], 16)
                        sp.wait_ge(s["vb"], at(b, 1, -1))
                        sp.sem_inc(s_gs, 1)
                        sp.dma_start(vb[:, k, :, :].rearrange("p t d -> p (t d)"), v_d[b]).then_inc(s_x[k], 16)

                    def turn(b, i, k, last):
                        if not last:
                            load(b + 2, i + 1, k)
                        sp.wait_ge(s["q"], at(b, 1, 1))
                        sp.sem_inc(s_gs, 1)
                        sp.dma_start(qk_d[b], qk[:, k, :, :].rearrange("p g l -> p (g l)")).then_inc(s_o1[k], 16)
                        sp.wait_ge(s["xb"], at(b, 1, 1))
                        sp.sem_inc(s_gs, 1)
                        sp.dma_start(vq_d[b], vq[:, k, :, :, :].rearrange("p t h d -> p (t h d)")).then_inc(s_o2[k], 16)

                    for k in range(2):
                        load(k, 0, k)
                    two_a_turn(sp, NB, turn)
                    for k in range(2):
                        sp.wait_ge(s_o1[k], 16 * (NB // 2))
                        sp.wait_ge(s_o2[k], 16 * (NB // 2))

                @block.gpsimd
                def _(pool):
                    pool.memset(vq[:, :, :, :, :], 0.0).then_inc(s_m0, 1)

                @block.tensor
                def _(pe):
                    pe.sem_inc(s["qk"], CREDIT)

                    def body(b, i, k, last):
                        pe.wait_ge(s_x[k], i * 32 + 32)
                        for r in range(6):
                            pe.wait_ge(s["y"], at(b, 6, r - 2))
                            for lo, hi in CUT:
                                for c in range(KT):
                                    ins = pe.matmul(pQ[:, r % 3, OFF + lo:OFF + hi], K["wT"][:, c, r * 128:(r + 1) * 128],
                                                    xT[:, k, c, lo:hi], start=(c == 0), stop=(c == KT - 1))
                            ins.then_inc(s["qk"], 1)

                    two_a_turn(pe, NB, body)

                @block.scalar
                def _(act):
                    act.sem_inc(s["y"], CREDIT)

                    def body(b, i, k, last):
                        act.wait_ge(s["max"], at(b, 1, -1))
                        for r in range(6):
                            act.wait_ge(s["qk"], at(b, 6, r + 1))
                            act.activation(y[:, k, r, :], pQ[:, r % 3, OFF:OFF + S], ACT.Identity,
                                           bias=K["bqi"][:, r:r + 1], scale=K["cqi"][:, r // 3:r // 3 + 1])\
                                .then_inc(s["y"], 1)

                    two_a_turn(act, NB, body)

                @block.vector
                def _(dve):
                    for n in ("max", "vb", "xb", "q"):
                        dve.sem_inc(s[n], CREDIT)
                    dve.wait_ge(s_m0, 1)

                    def body(b, i, k, last):
                        dve.wait_ge(s_x[k], i * 32 + 32)
                        dve.wait_ge(s["xb"], at(b, 1, -1))
                        v.tensor_scalar(xr[:, k, :], vb[:, k, :, :].rearrange("p t d -> p (t d)"),
                                        K["inv"][0:TP, 5:6], MAGIC, ALU.mult, ALU.add).then_inc(s["vb"], 1)
                        dve.wait_ge(s["vb"], at(b, 1, 1))
                        dve.wait_ge(s_o2[k], i * 16)
                        dve.sem_inc(s_go, 1)
                        v.tensor_scalar(vq[:, k, :, :, 0:HD].rearrange("p t h d -> p (t h) d"),
                                        xr[:, k, :].rearrange("p (t d) -> p t d", d=HD), -MAGIC, None,
                                        ALU.add).then_inc(s["xb"], 1)
                        dve.wait_ge(s["y"], at(b, 6, 6))
                        dve.wait_ge(s_o1[k], i * 16)
                        v.tensor_scalar(qk[:, k, :, :], y[:, k, :, :], MAGIC, -MAGIC, ALU.add, ALU.add)\
                            .then_inc(s["q"], 1)
                        dve.wait_ge(s["q"], at(b, 1, 1))
                        dve.sem_inc(s["max"], 1)

                    two_a_turn(dve, NB, body)


def attention(nc, h2, w_qkv, b_qkv, w_proj, b_proj, scratch, h3):
    with ExitStack() as keep:
        sb = lambda name, shape, dt=F32: keep.enter_context(nc.sbuf_tensor("k_" + name, shape, dt))
        K = {
            "ident": sb("ident", [128, 128], BF16), "pad": sb("pad", [128, 4, 3]), "padc": sb("padc", [128, 1]),
            "wT": sb("wT", [KC, KT, 2 * NHD * HP], BF16), "wvT": sb("wvT", [KC, KT, D], BF16),
            "wpT": sb("wpT", [128, HG, D], BF16), "bqk": sb("bqk", [128, 6]), "bqi": sb("bqi", [128, 6]),
            "bv": sb("bv", [TP, D]), "amax": sb("amax", [128, 8]), "gmax": sb("gmax", [128, 8]),
            "sc": sb("sc", [128, 8]), "inv": sb("inv", [128, 8]), "cq": sb("cq", [128, 1]),
            "cqi": sb("cqi", [128, 2]), "co": sb("co", [128, 3]), "cs": sb("cs", [128, 1]), "csi": sb("csi", [128, 1]),
            "s_b": keep.enter_context(nc.semaphore("k_s_b")),
        }
        attention_inputs(nc, h2, w_qkv, b_qkv, w_proj, scratch["xn"], scratch["xt"], scratch["v"],
                         scratch["qk"], scratch["vq"], K)
        attention_heads(nc, scratch, K, b_proj, h2, h3)


def attention_heads(nc, scratch, K, b_proj, h2, h3):
    v = nc.vector
    NQ = NHD * TT
    MAXR = bass.bass_isa.ReduceOp.max
    with ExitStack() as ctx:
        sb = lambda name, shape, dt=F32: ctx.enter_context(nc.sbuf_tensor("g_" + name, shape, dt))
        sem = semaphores(nc, ctx, "g_")
        RING = 4
        qk = sb("qk", [128, 2, 6, S], BF16)
        junk = sb("junk", [TP, 2, S], BF16)
        csn = sb("csn", [TP, 1])
        stt = sb("stt", [TP, 2, 2, NQ])
        low, m1 = sb("low", [TP, 1]), sb("m1", [TP, 1])
        pS = ctx.enter_context(nc.psum_tensor("g_pS", [TP, RING, 1024], F32))
        s_m0, s_all, s_v, s_go, s_i, s_c = (sem(n) for n in ("s_m0", "s_all", "s_v", "s_go", "s_i", "s_c"))
        s_q = [sem(f"s_q{k}") for k in range(2)]
        s_o = [sem(f"s_o{k}") for k in range(2)]
        s = {n: sem("q_" + n) for n in ("S", "mn", "exp", "min")}
        block = ctx.enter_context(nc.Block())

        @block.sync
        def _(sp):
            def load(b, i, k):
                sp.wait_ge(s["S"], at(b, NQ, -NQ))
                sp.sem_inc(s_go, 1)
                sp.dma_start(qk[:, k, :, :].rearrange("p g l -> p (g l)"), scratch["qk"][b]).then_inc(s_q[k], 16)

            def turn(b, i, k, last):
                if not last:
                    load(b + 2, i + 1, k)
                sp.wait_ge(s["exp"], at(b, NQ, NQ))
                sp.sem_inc(s_go, 1)
                sp.dma_start(scratch["st"][b], stt[:, k, :, :].rearrange("p a q -> p (a q)")).then_inc(s_o[k], 16)

            for k in range(2):
                load(k, 0, k)
            two_a_turn(sp, NB, turn)
            for k in range(2):
                sp.wait_ge(s_o[k], 16 * (NB // 2))

        @block.gpsimd
        def _(pool):
            pool.memset(low[:, :], 3.0e38).then_inc(s_i, 1)
            pool.memset(stt[:, :, :, :], 3.0e38).then_inc(s_i, 1)
            pool.wait_ge(s_m0, 1)
            pool.partition_all_reduce(K["gmax"][:, 6:7], K["amax"][:, 6:7], 128, MAXR).then_inc(s_all, 1)

        @block.tensor
        def _(pe):
            pe.sem_inc(s["S"], CREDIT)

            def body(b, i, k, last):
                pe.wait_ge(s_q[k], i * 16 + 16)
                for q in range(NQ):
                    pe.wait_ge(s["exp"], at(b, NQ, q + 1 - RING))
                    g, t, j = q // 20, q // 4 % 5, q % 4
                    at_ = slice(HP * j, HP * j + HD)
                    for lo, hi in CUT:
                        ins = pe.matmul(pS[:, q % RING, OFF + lo:OFF + hi], qk[at_, k, g, t * TP:(t + 1) * TP],
                                        qk[at_, k, 3 + g, lo:hi], start=True, stop=True)
                    ins.then_inc(s["S"], 1)

            two_a_turn(pe, NB, body)

        @block.scalar
        def _(act):
            act.sem_inc(s["exp"], CREDIT)
            act.wait_ge(s_i, 2)

            def body(b, i, k, last):
                act.wait_ge(s_o[k], i * 16)
                act.wait_ge(s["min"], at(b, 1, 0))
                for q in range(NQ):
                    act.wait_ge(s["mn"], at(b, NQ, q + 1))
                    x = pS[:, q % RING, OFF:OFF + S]
                    nc.scalar.activation(x, x, ACT.Exp, bias=stt[:, k, 0, q:q + 1], scale=K["cs"][0:TP, 0:1],
                                         accum_out=stt[:, k, 1, q:q + 1]).then_inc(s["exp"], 1)

            two_a_turn(act, NB, body)

        @block.vector
        def _(dve):
            for n in ("mn", "min"):
                dve.sem_inc(s[n], CREDIT)
            dve.wait_ge(s_i, 2)
            v.tensor_scalar(csn[:, :], K["cs"][0:TP, 0:1], -1.0, None, ALU.mult).then_inc(s_c, 1)
            dve.wait_ge(s_c, 1)

            def lowest(b, k):
                st = Steps(dve, s_v, 1, b + 1)
                dve.wait_ge(s["exp"], at(b, NQ, NQ))
                st.after(v.tensor_reduce(m1[:, :], stt[:, k, 1, :], AX, ALU.min))
                v.tensor_tensor(low[:, :], low[:, :], m1[:, :], ALU.min).then_inc(s["min"], 1)
                dve.wait_ge(s["min"], at(b, 1, 2))

            def body(b, i, k, last):
                dve.wait_ge(s_o[k], i * 16)
                for q in range(NQ):
                    dve.wait_ge(s["S"], at(b, NQ, q + 1))
                    dve.wait_ge(s["mn"], at(b, NQ, q - 1))
                    v.tensor_scalar(junk[:, q % 2, :], pS[:, q % RING, OFF:OFF + S], csn[:, 0:1], 3.0e38, ALU.mult, ALU.min,
                                    accum_out=stt[:, k, 0, q:q + 1]).then_inc(s["mn"], 1)
                    if q == 6:
                        lowest(b - 1, 1 - k)

            two_a_turn(dve, NB, body)
            lowest(NB - 1, 1)
            st = Steps(dve, s_go)
            v.reciprocal(K["amax"][0:TP, 6:7], low[:, :]).then_inc(s_m0, 1)
            dve.wait_ge(s_all, 1)
            st2 = Steps(dve, s_v, 1, NB + 1)
            quant_scale(nc, st2, K["sc"][:, 6:7], K["inv"][:, 6:7], K["gmax"][:, 6:7])

    with ExitStack() as ctx:
        sb = lambda name, shape, dt=F32: ctx.enter_context(nc.sbuf_tensor("h_" + name, shape, dt))
        sem = semaphores(nc, ctx, "h_")
        RING = 4
        qk = sb("qk", [128, 2, 6, S], BF16)
        vq = sb("vq", [TP, 2, TT, NHD, HP], BF16)
        stt = sb("stt", [TP, NB, 2, NQ])
        ln, r1 = sb("ln", [TP, NB, NQ]), sb("r1", [TP, NQ])
        A = sb("A", [TP, HG, TT, 4, HP], BF16)
        ex = sb("ex", [TP, RING, S])
        pr = sb("pr", [TP, RING, S], BF16)
        oT = sb("oT", [128, 2, HG, S])
        om = sb("om", [128, 1])
        pS = ctx.enter_context(nc.psum_tensor("h_pS", [128, 3, 1024], F32))
        pO = ctx.enter_context(nc.psum_tensor("h_pO", [128, 1024], F32))
        s_m0, s_all, s_v, s_go, s_i, s_om, s_st, s_ln, s_a = (sem(n) for n in (
            "s_m0", "s_all", "s_v", "s_go", "s_i", "s_om", "s_st", "s_ln", "s_a"))
        s_in = [sem(f"s_in{k}") for k in range(2)]
        s_o = [sem(f"s_o{k}") for k in range(2)]
        s = {n: sem("q_" + n) for n in ("A", "T", "qa", "S", "E", "P", "AV", "ev", "om")}
        block = ctx.enter_context(nc.Block())

        SEQ = []
        for u in range(NQ):
            SEQ.append(("tile", u))
            if u in (19, 34, 49):
                SEQ.append(("rows", (19, 34, 49).index(u)))
        L = len(SEQ)
        assert L % 3 == 0

        @block.sync
        def _(sp):
            def load(b, i, k):
                sp.wait_ge(s["AV"], at(b, NQ, -NQ))
                sp.sem_inc(s_go, 1)
                sp.dma_start(qk[:, k, :, :].rearrange("p g l -> p (g l)"), scratch["qk"][b]).then_inc(s_in[k], 16)
                sp.dma_start(vq[:, k, :, :, :].rearrange("p t h d -> p (t h d)"), scratch["vq"][b])\
                    .then_inc(s_in[k], 16)

            def turn(b, i, k, last):
                sp.wait_ge(s["ev"], at(b, 3, 3))
                sp.sem_inc(s_go, 1)
                sp.dma_start(scratch["o"][b], oT[:, k, :, :].rearrange("p g l -> p (g l)")).then_inc(s_o[k], 16)
                if not last:
                    load(b + 2, i + 1, k)

            sp.dma_start(stt[:, :, :, :].rearrange("p b a q -> p b (a q)"), scratch["st"].rearrange("b p q -> p b q"))\
                .then_inc(s_st, 16)
            for k in range(2):
                load(k, 0, k)
            two_a_turn(sp, NB, turn)
            for k in range(2):
                sp.wait_ge(s_o[k], 16 * (NB // 2))

        @block.gpsimd
        def _(pool):
            pool.memset(A[:, :, :, :, :], 0.0).then_inc(s_i, 1)
            pool.memset(oT[:, 1, HG - 1, :], 0.0).then_inc(s_i, 1)
            pool.wait_ge(s_m0, 1)
            pool.partition_all_reduce(K["gmax"][:, 7:8], K["amax"][:, 7:8], 128, MAXR).then_inc(s_all, 1)

        @block.tensor
        def _(pe):
            for n in ("T", "S", "AV"):
                pe.sem_inc(s[n], CREDIT)

            def transpose_rows(b, slot, g):
                pe.wait_ge(s["A"], at(b, 1, 1))
                out = pS[:, slot, :].bitcast(BF16)
                for t in range(TT):
                    ins = pe.transpose(out[:, t * (TP + 1):t * (TP + 1) + TP],
                                       A[:, g, t, :, :].rearrange("p j e -> p (j e)"), K["ident"][0:TP, 0:TP])
                ins.then_inc(s["T"], 1)

            def user(pos, last):
                p = pos - 3
                while p >= 0 and last and SEQ[p][0] == "rows":
                    p -= 3
                return (SEQ[p], False) if p >= 0 else (SEQ[p + L], True)

            def fill(b, i, k, pos, last):
                (kind, n), before = user(pos, last)
                assert not (before and kind == "rows")
                if kind == "tile":
                    pe.wait_ge(s["E"], at(b, NQ, n + 1 - (NQ if before else 0)))
                else:
                    pe.wait_ge(s["qa"], at(b, 3, 3 + n + 1))
                kind, n = SEQ[pos]
                if kind == "rows":
                    transpose_rows(b + 1, pos % 3, n)
                    return
                g, j, m = n // 20, n // 5 % 4, n % 5
                if n == 0:
                    pe.wait_ge(s_in[k], i * 32 + 32)
                    pe.wait_ge(s["qa"], at(b, 3, 3))
                at_ = slice(HP * j, HP * j + HD + 3)
                for lo, hi in CUT:
                    ins = pe.matmul(pS[0:TP, pos % 3, OFF + lo:OFF + hi], qk[at_, k, 3 + g, m * TP:(m + 1) * TP],
                                    qk[at_, k, g, lo:hi], start=True, stop=True)
                ins.then_inc(s["S"], 1)

            def combine(b, k, u):
                g, j, m = u // 20, u // 5 % 4, u % 5
                pe.wait_ge(s["P"], at(b, NQ, u + 1))
                if u % 20 == 0:
                    pe.wait_ge(s["ev"], at(b, 3, g))
                for lo, hi in CUT:
                    ins = pe.matmul(pO[HP * j:HP * j + HP, OFF + lo:OFF + hi], vq[:, k, m, 4 * g + j, :],
                                    pr[:, u % RING, lo:hi], start=(m == 0), stop=(m == TT - 1),
                                    skip_group_check=True)
                ins.then_inc(s["AV"], 1)

            pe.wait_ge(s_in[0], 32)
            for g in range(3):
                transpose_rows(0, g, g)
            pe.wait_ge(s["qa"], at(0, 3, 3))
            for pos in range(2):
                fill(0, 0, 0, pos, False)

            def body(b, i, k, last):
                for pos in range(L):
                    nxt = pos + 2
                    if nxt < L:
                        if not (last == 2 and SEQ[nxt][0] == "rows"):
                            fill(b, i, k, nxt, last == 2)
                    elif last < 2:
                        fill(b + 1, i + k, 1 - k, nxt - L, last == 1)
                    if pos > 0 and SEQ[pos - 1][0] == "tile":
                        combine(b, k, SEQ[pos - 1][1])
                combine(b, k, NQ - 1)

            two_a_turn(pe, NB, body)

        @block.scalar
        def _(act):
            act.sem_inc(s["E"], CREDIT)
            act.wait_ge(s_st, 16)
            nc.scalar.activation(ln[:, :, :], stt[:, :, 1, :], ACT.Ln, scale=K["sc"][0:TP, 6:7]).then_inc(s_ln, 1)

            def body(b, i, k, last):
                for u in range(NQ):
                    act.wait_ge(s["S"], at(b, NQ, u + 1))
                    act.wait_ge(s["P"], at(b, NQ, u + 1 - RING))
                    slot = SEQ.index(("tile", u)) % 3
                    nc.scalar.activation(ex[:, u % RING, :], pS[0:TP, slot, OFF:OFF + S], ACT.Exp,
                                         scale=K["cs"][0:TP, 0:1]).then_inc(s["E"], 1)

            two_a_turn(act, NB, body)

        @block.vector
        def _(dve):
            for n in ("A", "qa", "P", "ev", "om"):
                dve.sem_inc(s[n], CREDIT)
            dve.wait_ge(s_i, 2)

            def constants(b, i, k):
                st = Steps(dve, s_v, 3, b)
                flat = A[:, :, :, :, :].rearrange("p g t j e -> p (g t j) e")
                a1 = ln[:, bass.ds(b, 1), :].rearrange("p a q -> p (a q)")
                dve.wait_ge(s["T"], at(b, 3, 0))
                dve.sem_inc(s_go, 1)
                st.after(v.tensor_copy(flat[:, :, HD], a1))
                dve.sem_inc(s_go, 1)
                st.after(v.tensor_tensor(r1[:, :], a1, flat[:, :, HD], ALU.subtract))
                st.after(v.tensor_copy(flat[:, :, HD + 1], r1[:, :]))
                v.tensor_tensor(flat[:, :, HD + 2], r1[:, :], flat[:, :, HD + 1], ALU.subtract).then_inc(s["A"], 1)

            def largest(b, k, g):
                dve.wait_ge(s["ev"], at(b, 3, g + 1))
                x = oT[:, k, g, :] if g >= 0 else oT[:, 1 - k, HG - 1, :]
                v.tensor_reduce(om[:, :], x, AX, ALU.max, apply_absolute_value=True).then_inc(s_om, 1)
                dve.wait_ge(s_om, b * 3 + (g + 2))
                v.tensor_tensor(K["amax"][:, 7:8], K["amax"][:, 7:8], om[:, :], ALU.max).then_inc(s["om"], 1)
                dve.wait_ge(s["om"], at(b, 3, g + 2))

            def add_rows(b, i, k, g, slot):
                dve.wait_ge(s["T"], at(b, 3, g + 1))
                if g == 0:
                    dve.wait_ge(s_in[k], i * 32 + 32)
                x = qk[:, k, g, :].rearrange("p (t l) -> p t l", t=TT)
                rows = pS[:, slot, :].bitcast(BF16)[:, 0:TT * (TP + 1)].rearrange("p (t l) -> p t l", t=TT)[:, :, 0:TP]
                v.tensor_tensor(x, x, rows, ALU.add).then_inc(s["qa"], 1)

            dve.wait_ge(s_ln, 1)
            v.tensor_tensor(ln[:, :, :], stt[:, :, 0, :], ln[:, :, :], ALU.subtract).then_inc(s_a, 1)
            dve.wait_ge(s_a, 1)
            v.tensor_scalar(ln[:, :, :], ln[:, :, :], K["csi"][0:TP, 0:1], None, ALU.mult).then_inc(s_a, 1)
            dve.wait_ge(s_a, 2)
            constants(0, 0, 0)
            for g in range(3):
                add_rows(0, 0, 0, g, g)

            def body(b, i, k, last):
                for pos, (kind, n) in enumerate(SEQ):
                    if kind == "rows":
                        if last < 2:
                            add_rows(b + 1, i + k, 1 - k, n, pos % 3)
                        continue
                    u = n
                    dve.wait_ge(s["E"], at(b, NQ, u + 1))
                    dve.wait_ge(s["AV"], at(b, NQ, u + 1 - RING))
                    v.tensor_scalar(pr[:, u % RING, :], ex[:, u % RING, :], MAGIC, -MAGIC, ALU.add, ALU.add)\
                        .then_inc(s["P"], 1)
                    if u == 12 and last < 2:
                        constants(b + 1, i + k, 1 - k)
                    if u in (20, 40, NQ - 1):
                        g = (u - 1) // 20
                        dve.wait_ge(s["AV"], at(b, NQ, 20 * (g + 1)))
                        if g == 0:
                            dve.wait_ge(s_o[k], i * 16)
                        v.tensor_copy(oT[:, k, g, :], pO[:, OFF:OFF + S]).then_inc(s["ev"], 1)
                    if u in (5, 25, 45):
                        largest(b, k, u // 20 - 1)

            two_a_turn(dve, NB, body)
            largest(NB, 0, -1)
            dve.sem_inc(s_m0, 1)
            dve.wait_ge(s_all, 1)
            st = Steps(dve, s_v, 3, NB)
            st.after(v.tensor_tensor(K["co"][:, 0:1], K["sc"][:, 6:7], K["sc"][:, 5:6], ALU.mult))
            st.after(v.tensor_tensor(K["gmax"][:, 7:8], K["gmax"][:, 7:8], K["co"][:, 0:1], ALU.mult))
            quant_scale(nc, st, K["sc"][:, 7:8], K["inv"][:, 7:8], K["gmax"][:, 7:8])
            st.after(v.tensor_tensor(K["co"][:, 1:2], K["co"][:, 0:1], K["inv"][:, 7:8], ALU.mult))
            st.after(v.tensor_tensor(K["co"][:, 2:3], K["sc"][:, 7:8], K["sc"][:, 2:3], ALU.mult))

    with ExitStack() as ctx:
        sb = lambda name, shape, dt=F32: ctx.enter_context(nc.sbuf_tensor("i_" + name, shape, dt))
        sem = semaphores(nc, ctx, "i_")
        o, orr = sb("o", [128, 2, HG * S]), sb("orr", [128, 2, HG * S])
        oq = sb("oq", [128, 2, HG, S], BF16)
        h, hb, y = sb("h", [TP, 2, TT, D]), sb("hb", [TP, 2, TT, D]), sb("y", [TP, 2, TT, D])
        bp, mg = sb("bp", [TP, D]), sb("mg", [128, 1])
        pY = ctx.enter_context(nc.psum_tensor("i_pY", [TP, 2, 4, 512], F32))
        s_w, s_go, s_m = sem("s_w"), sem("s_go"), sem("s_m")
        s_in = [sem(f"s_in{k}") for k in range(2)]
        s_h = [sem(f"s_h{k}") for k in range(2)]
        s_o = [sem(f"s_o{k}") for k in range(2)]
        s = {n: sem("q_" + n) for n in ("hb", "rr", "oq", "Y", "y")}
        block = ctx.enter_context(nc.Block())
        rows = lambda x, b: x[bass.ds(b * S, S), :].rearrange("(t p) d -> p t d", p=TP)

        @block.sync
        def _(sp):
            sp.dma_start(bp[:, :], b_proj.rearrange("(a d) -> a d", a=1).broadcast_to([TP, D])).then_inc(s_w, 16)

            def load(b, i, k):
                sp.wait_ge(s["rr"], at(b, 1, -1))
                sp.wait_ge(s["hb"], at(b, 1, -1))
                sp.sem_inc(s_go, 1)
                sp.dma_start(o[:, k, :], scratch["o"][b]).then_inc(s_in[k], 16)
                sp.dma_start(h[:, k, :, :], rows(h2, b)).then_inc(s_h[k], 16)

            def turn(b, i, k, last):
                if not last:
                    load(b + 2, i + 1, k)
                sp.wait_ge(s["y"], at(b, 1, 1))
                sp.sem_inc(s_go, 1)
                sp.dma_start(rows(h3, b), y[:, k, :, :]).then_inc(s_o[k], 16)

            for k in range(2):
                load(k, 0, k)
            two_a_turn(sp, NB, turn)
            for k in range(2):
                sp.wait_ge(s_o[k], 16 * (NB // 2))

        @block.gpsimd
        def _(pool):
            pool.sem_inc(s["hb"], CREDIT)
            pool.memset(mg[:, :], MAGIC).then_inc(s_m, 1)
            pool.wait_ge(s_w, 16)

            def body(b, i, k, last):
                pool.wait_ge(s_h[k], i * 16 + 16)
                pool.wait_ge(s["y"], at(b, 1, -1))
                pool.tensor_tensor(hb[:, k, :, :], h[:, k, :, :],
                                   bp[:, :].rearrange("p (a d) -> p a d", a=1).broadcast_to([TP, TT, D]),
                                   ALU.add).then_inc(s["hb"], 1)

            two_a_turn(pool, NB, body)

        @block.scalar
        def _(act):
            act.sem_inc(s["rr"], CREDIT)
            act.wait_ge(s_m, 1)

            def body(b, i, k, last):
                act.wait_ge(s_in[k], i * 16 + 16)
                act.wait_ge(s["oq"], at(b, 1, -1))
                nc.scalar.activation(orr[:, k, :], o[:, k, :], ACT.Identity, bias=mg[:, 0:1],
                                     scale=K["co"][:, 1:2]).then_inc(s["rr"], 1)

            two_a_turn(act, NB, body)

        @block.tensor
        def _(pe):
            pe.sem_inc(s["Y"], CREDIT)

            def body(b, i, k, last):
                pe.wait_ge(s["oq"], at(b, 1, 1))
                pe.wait_ge(s["y"], at(b, 1, -1))
                for t in range(TT):
                    for g in range(HG):
                        ins = pe.matmul(pY[:, k, t // 2, t % 2 * D:(t % 2 + 1) * D], oq[:, k, g, t * TP:(t + 1) * TP],
                                        K["wpT"][:, g, :], start=(g == 0), stop=(g == HG - 1))
                ins.then_inc(s["Y"], 1)

            two_a_turn(pe, NB, body)

        @block.vector
        def _(dve):
            for n in ("oq", "y"):
                dve.sem_inc(s[n], CREDIT)

            def integers(b, i, k):
                dve.wait_ge(s["rr"], at(b, 1, 1))
                dve.wait_ge(s["Y"], at(b, 1, -1))
                v.tensor_scalar(oq[:, k, :, :].rearrange("p g l -> p (g l)"), orr[:, k, :], -MAGIC, None, ALU.add)\
                    .then_inc(s["oq"], 1)

            integers(0, 0, 0)

            def body(b, i, k, last):
                if last < 2:
                    integers(b + 1, i + k, 1 - k)
                dve.wait_ge(s["Y"], at(b, 1, 1))
                dve.wait_ge(s["hb"], at(b, 1, 1))
                dve.wait_ge(s_o[k], i * 16)
                for c in range(3):
                    n = 2 if c < 2 else 1
                    ins = v.scalar_tensor_tensor(y[:, k, 2 * c:2 * c + n, :],
                                                 pY[:, k, c, 0:n * D].rearrange("p (t d) -> p t d", t=n),
                                                 K["co"][0:TP, 2:3], hb[:, k, 2 * c:2 * c + n, :], ALU.mult, ALU.add)
                ins.then_inc(s["y"], 1)

            two_a_turn(dve, NB, body)


def switch_experts(nc, h3, ln_w, w_router, wi, wo, slot_x, slot_y, nrm_d, out):
    E, F, CAP = 16, 768, 64
    FT = F // 128
    NT = NB * TT
    SLOTS = E * NB * CAP
    EPS1, EPS2 = 1e-5, 1e-6
    v = nc.vector
    with ExitStack() as keep:
        sbk = lambda name, shape, dt=F32: keep.enter_context(nc.sbuf_tensor("m_" + name, shape, dt))
        ident = sbk("ident", [128, 128])
        base = sbk("base", [TP, NT, D])
        prob = sbk("prob", [TP, NT])
        dest = sbk("dest", [TP, NT], U32)

        with ExitStack() as ctx:
            sb = lambda name, shape, dt=F32: ctx.enter_context(nc.sbuf_tensor("n_" + name, shape, dt))
            ps = lambda name, shape: ctx.enter_context(nc.psum_tensor("n_" + name, shape, F32))
            sem = semaphores(nc, ctx, "n_")
            ZW = 3072
            zero = sb("zero", [128, ZW])
            lnw, wr = sb("lnw", [TP, D]), sb("wr", [KC, KT, E])
            tri, ones = sb("tri", [TP, TP], BF16), sb("ones", [TP, TP], BF16)
            desc = sb("desc", [TP, E])
            stats, mv = sb("stats", [TP, TT, 6]), sb("mv", [TP, TT, 2])
            R = 4
            ve, rs, nb_ = (sb(n, [TP, 2, 2, TT]) for n in ("ve", "rs", "nb"))
            hh = sb("hh", [TP, 2, TT])
            xs = sb("xs", [TP, TT, D])
            nx = sb("nx", [TP, R, TT, D])
            xT = sb("xT", [KC, 2 * TT, TP])
            eq, lg, ex, pr = (sb(n, [TP, TT, E]) for n in ("eq", "lg", "ex", "pr"))
            oh = sb("oh", [TP, TT, E], BF16)
            mx, first, sums, place, over, slot = (sb(n, [TP, TT]) for n in ("mx", "first", "sums", "place", "over", "slot"))
            sbase = sb("sbase", [TP, 1])
            to = sb("to", [TP, R, TT], U32)
            pT = ps("pT", [KC, 3, 512])
            pL, pC = ps("pL", [TP, TT, E]), ps("pC", [TP, TT, E])
            SLOT_OF = [(n // 4, (n % 4) * TP) for n in range(2 * TT)]

            s_z0, s_zero, s_w, s_i0, s_i, s_go, s_dv = (sem(n) for n in (
                "s_z0", "s_zero", "s_w", "s_i0", "s_i", "s_go", "s_dv"))
            s_sc = [sem(f"s_sc{k}") for k in range(R)]
            s_kn = [sem(f"s_kn{k}") for k in range(R)]
            s_ro = sem("s_ro")
            VS, VR = 4 + RSQRT_STEPS, 12
            s_h = [sem(f"s_h{k}") for k in range(R)]
            s = {n: sem("q_" + n) for n in ("stat", "xs", "nrm", "bas", "T", "xT", "L", "lg", "ex", "oh", "cum", "dest")}
            block = ctx.enter_context(nc.Block())

            @block.sync
            def _(sp):
                for k in range(R):
                    sp.dma_start(base[:, k * TT:(k + 1) * TT, :], h3[k * S:(k + 1) * S, :].rearrange(
                        "(t p) d -> p t d", p=TP)).then_inc(s_h[k], 16)
                sp.dma_start(lnw[:, :], ln_w.rearrange("(a d) -> a d", a=1).broadcast_to([TP, D])).then_inc(s_w, 16)
                sp.dma_start(wr[:, :, :], w_router.rearrange("(c p) e -> p c e", p=KC)).then_inc(s_w, 16)
                sp.wait_ge(s_z0, 1)
                for n in range(SLOTS * D // (128 * ZW)):
                    rows = 128 * ZW // D
                    sp.dma_start(slot_x[n * rows:(n + 1) * rows, :].rearrange("(p r) d -> p (r d)", p=128),
                                 zero[:, :]).then_inc(s_zero, 16)

                def body(c, i, k, left):
                    if left >= R:
                        sp.wait_ge(s["stat"], at(c, 1, 1))
                        sp.sem_inc(s_go, 1)
                        sp.dma_start(base[:, bass.ds(c * TT + R * TT, TT), :],
                                     h3[bass.ds(c * S + R * S, S), :].rearrange("(t p) d -> p t d", p=TP))\
                            .then_inc(s_h[k], 16)
                    sp.wait_ge(s["nrm"], at(c, 1, 1))
                    sp.sem_inc(s_go, 1)
                    sp.dma_start(nrm_d[c], nx[:, k, :, :].rearrange("p t d -> p (t d)")).then_inc(s_kn[k], 16)

                turns(sp, NB, R, body)
                for k in range(R):
                    sp.wait_ge(s_kn[k], 16 * (NB // R))

            @block.gpsimd
            def _(pool):
                pool.memset(zero[:, :], 0.0).then_inc(s_z0, 1)
                pool.memset(ident[:, :], 0.0).then_inc(s_i0, 1)
                pool.memset(tri[:, :], 1.0).then_inc(s_i0, 1)
                pool.memset(ones[:, :], 1.0).then_inc(s_i0, 1)
                for e in range(E):
                    pool.memset(desc[:, e:e + 1], float(E - e)).then_inc(s_i0, 1)
                pool.wait_ge(s_i0, 3 + E)
                pool.affine_select(out=ident[:, :], in_=ident[:, :], compare_op=ALU.not_equal, fill=1.0, base=0,
                                   pattern=[[-1, 128]], channel_multiplier=1).then_inc(s_i, 1)
                pool.wait_ge(s_i, 1)
                pool.affine_select(out=tri[:, :], in_=tri[:, :], compare_op=ALU.is_ge, fill=0.0, base=0,
                                   pattern=[[1, TP]], channel_multiplier=-1).then_inc(s_i, 1)
                last_slot = pool.to_reg(SLOTS - 1)
                pool.wait_ge(s_zero, 16 * (SLOTS * D // (128 * ZW)))

                def body(c, i, k, left):
                    pool.wait_ge(s["dest"], at(c, 1, 1))
                    pool.sem_inc(s_go, 1)
                    for t in range(TT):
                        pool.indirect_dma_start(slot_x, bass.IndirectOffsetOnAxis(ap=to[:, k, t:t + 1], axis=0),
                                                nx[:, k, t, :], None,
                                                bounds_check=last_slot, oob_is_err=False).then_inc(s_sc[k], 16)

                turns(pool, NB, R, body)
                for k in range(R):
                    pool.wait_ge(s_sc[k], 16 * TT * (NB // R))

            def transposes(pe, c, k):
                pe.wait_ge(s["nrm"], at(c, 1, 1))
                pe.wait_ge(s["xT"], at(c, 1, 0))
                for n in range(2 * TT):
                    b_, o = SLOT_OF[n]
                    ins = pe.transpose(pT[:, b_, o:o + TP], nx[:, k, n // 2, (n % 2) * KC:(n % 2 + 1) * KC],
                                       ident[0:TP, 0:TP])
                ins.then_inc(s["T"], 1)

            def logits(pe, c):
                pe.wait_ge(s["xT"], at(c, 1, 1))
                pe.wait_ge(s["oh"], at(c, 1, 0))
                for t in range(TT):
                    for cc in range(KT):
                        ins = pe.matmul(pL[:, t, :], xT[:, 2 * t + cc, :], wr[:, cc, :], start=(cc == 0),
                                        stop=(cc == KT - 1))
                ins.then_inc(s["L"], 1)

            @block.tensor
            def _(pe):
                for n in ("T", "L", "cum"):
                    pe.sem_inc(s[n], CREDIT)
                pe.wait_ge(s_w, 32)
                pe.wait_ge(s_i, 2)
                transposes(pe, 0, 0)
                logits(pe, 0)

                def body(c, i, k, left):
                    if left:
                        transposes(pe, c + 1, (k + 1) % R)
                    pe.wait_ge(s["oh"], at(c, 1, 1))
                    pe.wait_ge(s["dest"], at(c, 1, 0))
                    pe.matmul(pC[:, :, :], tri[:, :], oh[:, :, :], start=True, stop=False)
                    for d in range(1, TT):
                        ins = pe.matmul(pC[:, d:TT, :], ones[:, :], oh[:, 0:TT - d, :], start=False, stop=(d == TT - 1))
                    ins.then_inc(s["cum"], 1)
                    if left:
                        logits(pe, c + 1)

                turns(pe, NB, R, body)

            def rows_act(act, c, r):
                act.wait_ge(s["stat"], at(c, 1, 1))
                act.wait_ge(s["nrm"], at(c, 1, 0))
                act.sem_inc(s_go, 1)
                for t in range(TT):
                    ins = nc.scalar.activation(xs[:, t, :], base[:, bass.ds(c * TT + t, 1), :].rearrange("p a d -> p (a d)"),
                                               ACT.Identity, bias=nb_[:, r, 1, t:t + 1], scale=rs[:, r, 1, t:t + 1])
                ins.then_inc(s["xs"], 1)

            def base_act(act, c, r):
                act.wait_ge(s["xs"], at(c, 1, 1))
                act.sem_inc(s_go, 1)
                for t in range(TT):
                    rows = base[:, bass.ds(c * TT + t, 1), :].rearrange("p a d -> p (a d)")
                    ins = nc.scalar.activation(rows, rows, ACT.Identity, bias=nb_[:, r, 0, t:t + 1],
                                               scale=ve[:, r, 0, t:t + 1])
                ins.then_inc(s["bas"], 1)

            def copies_act(act, c):
                act.wait_ge(s["T"], at(c, 1, 1))
                act.wait_ge(s["L"], at(c, 1, 0))
                for lo in range(0, 2 * TT, 4):
                    w_ = min(4, 2 * TT - lo)
                    ins = nc.scalar.activation(xT[:, lo:lo + w_, :], pT[:, lo // 4, 0:w_ * TP].rearrange(
                        "p (n l) -> p n l", n=w_), ACT.Copy)
                ins.then_inc(s["xT"], 1)

            @block.scalar
            def _(act):
                for n in ("xs", "bas", "xT", "ex"):
                    act.sem_inc(s[n], CREDIT)
                for c in range(2):
                    rows_act(act, c, c)
                    base_act(act, c, c)
                copies_act(act, 0)

                def body(c, i, k, left):
                    if left:
                        copies_act(act, c + 1)
                    act.wait_ge(s["lg"], at(c, 1, 1))
                    nc.scalar.activation(ex[:, :, :], lg[:, :, :], ACT.Exp).then_inc(s["ex"], 1)
                    if left > 1:
                        rows_act(act, c + 2, k % 2)
                        base_act(act, c + 2, k % 2)

                turns(act, NB, R, body)

            def statistics(dve, c, i, k):
                st = Steps(dve, s_dv, VS, c)
                vr, rr, nr = (x[:, k % 2, :, :] for x in (ve, rs, nb_))
                dve.wait_ge(s_h[k], i * 16 + 16)
                dve.wait_ge(s["bas"], at(c, 1, -1))
                dve.sem_inc(s_go, 1)
                for t in range(TT):
                    ins = v.bn_stats(stats[:, t, :], base[:, bass.ds(c * TT + t, 1), :].rearrange("p a d -> p (a d)"))
                st.after(ins)
                dve.sem_inc(s_go, 1)
                for t in range(TT):
                    ins = v.bn_aggr(mv[:, t, :], stats[:, t, :])
                st.after(ins)
                v.tensor_scalar(vr[:, 0, :], mv[:, :, 1], EPS1, None, ALU.add)
                st.after(v.tensor_scalar(vr[:, 1, :], mv[:, :, 1], 1.0 + EPS2, EPS1 * EPS2, ALU.mult, ALU.add))
                rsqrt(nc, st, rr, vr, hh[:, :, :])
                for n in range(2):
                    ins = v.scalar_tensor_tensor(nr[:, n, :], mv[:, :, 0], -1.0, rr[:, n, :], ALU.mult, ALU.mult)
                st.after(ins)
                v.tensor_scalar(vr[:, 0, :], rr[:, 0, :], 1.0, None, ALU.add).then_inc(s["stat"], 1)
                st.end()

            def normed(dve, c, i, k):
                dve.wait_ge(s["xs"], at(c, 1, 1))
                dve.wait_ge(s["T"], at(c, 1, 1 - R))
                dve.wait_ge(s_kn[k], i * 16)
                dve.wait_ge(s_sc[k], i * (16 * TT))
                w3 = lnw[:, :].rearrange("p (a d) -> p a d", a=1).broadcast_to([TP, TT, D])
                v.tensor_tensor(nx[:, k, :, :], xs[:, :, :], w3, ALU.mult).then_inc(s["nrm"], 1)

            @block.vector
            def _(dve):
                for n in ("stat", "nrm", "lg", "oh", "dest"):
                    dve.sem_inc(s[n], CREDIT)
                dve.wait_ge(s_w, 32)
                dve.wait_ge(s_i, 2)
                v.memset(sbase[:, :], -1.0)
                for c in range(2):
                    statistics(dve, c, 0, c)
                    normed(dve, c, 0, c)
                wide = lambda x: x[:, :].rearrange("p (t a) -> p t a", a=1).broadcast_to([TP, TT, E])

                def body(c, i, k, left):
                    st = Steps(dve, s_ro, VR, c)
                    two_on = (i + (k + 2) // R, (k + 2) % R)
                    dve.wait_ge(s["L"], at(c, 1, 1))
                    st.after(v.tensor_reduce(mx[:, :], pL[:, :, :], AX, ALU.max))
                    v.tensor_tensor(eq[:, :, :], pL[:, :, :], wide(mx), ALU.is_equal)
                    v.tensor_tensor(lg[:, :, :], pL[:, :, :], wide(mx), ALU.subtract).then_inc(s["lg"], 1)
                    dve.wait_ge(s["lg"], at(c, 1, 1))
                    st.after(v.tensor_tensor(eq[:, :, :], eq[:, :, :], desc[:, :].rearrange("p (a e) -> p a e", a=1)
                                             .broadcast_to([TP, TT, E]), ALU.mult))
                    st.after(v.tensor_reduce(first[:, :], eq[:, :, :], AX, ALU.max))
                    v.tensor_tensor(oh[:, :, :], eq[:, :, :], wide(first), ALU.is_equal).then_inc(s["oh"], 1)
                    st.after(v.tensor_scalar(slot[:, :], first[:, :], -float(NB * CAP), float(E * NB * CAP),
                                             ALU.mult, ALU.add))
                    dve.wait_ge(s["oh"], at(c, 1, 1))
                    if left > 1:
                        statistics(dve, c + 2, *two_on)
                    dve.wait_ge(s["cum"], at(c, 1, 1))
                    st.after(v.tensor_tensor(pr[:, :, :], pC[:, :, :], oh[:, :, :], ALU.mult))
                    st.after(v.tensor_reduce(place[:, :], pr[:, :, :], AX, ALU.add))
                    st.after(v.tensor_scalar(over[:, :], place[:, :], float(CAP), 1.0e6, ALU.is_gt, ALU.mult))
                    st.after(v.tensor_tensor(slot[:, :], slot[:, :], place[:, :], ALU.add))
                    dve.wait_ge(s_sc[k], i * (16 * TT))
                    v.scalar_tensor_tensor(to[:, k, :], slot[:, :], sbase[:, 0:1], over[:, :],
                                           ALU.add, ALU.add).then_inc(s["dest"], 1)
                    dve.wait_ge(s["dest"], at(c, 1, 1))
                    dve.sem_inc(s_go, 1)
                    st.after(v.tensor_copy(dest[:, bass.ds(c * TT, TT)], to[:, k, :]))
                    st.after(v.tensor_scalar(sbase[:, :], sbase[:, :], float(CAP), None, ALU.add))
                    dve.wait_ge(s["ex"], at(c, 1, 1))
                    st.after(v.tensor_reduce(sums[:, :], ex[:, :, :], AX, ALU.add))
                    dve.sem_inc(s_go, 1)
                    st.after(v.reciprocal(prob[:, bass.ds(c * TT, TT)], sums[:, :]))
                    if left > 1:
                        normed(dve, c + 2, *two_on)
                    st.end()

                turns(dve, NB, R, body)

        with ExitStack() as ctx:
            sb = lambda name, shape, dt=F32: ctx.enter_context(nc.sbuf_tensor("o_" + name, shape, dt))
            ps = lambda name, shape: ctx.enter_context(nc.psum_tensor("o_" + name, shape, F32))
            sem = semaphores(nc, ctx, "o_")
            CT, CE = 2, 4
            CS = CT * 128
            CB, NTURN = 2 * CE, E // 2
            XR = 4
            assert CE * CS == NB * CAP
            HI, LO = 0, 1
            PARTS = ((HI, HI), (HI, LO), (LO, HI))
            wi_r, wo_r = sb("wi_r", [KC, KT, F]), sb("wo_r", [128, FT, D])
            wi_s = [sb(f"wi{p}", [KC, 2, KT, F], F32R) for p in range(2)]
            wo_s = [sb(f"wo{p}", [128, 2, FT, D], F32R) for p in range(2)]
            xr = sb("xr", [128, XR, CT, D])
            xT = [sb(f"xT{p}", [KC, 2, KT, CS], F32R) for p in range(2)]
            hT = [sb(f"hT{p}", [128, 2, FT, CS], F32R) for p in range(2)]
            yr = sb("yr", [128, 2, CT, D])
            pT, pH, pY = ps("pT", [KC, 2, KT, CS]), ps("pH", [128, 3, 512]), ps("pY", [128, 2, 512])
            s_w, s_wh, s_wl = sem("s_w"), sem("s_wh"), sem("s_wl")
            s_x = [sem(f"s_x{k}") for k in range(XR)]
            s_y = [sem(f"s_y{k}") for k in range(2)]
            s_go = sem("s_go")
            s = {n: sem("q_" + n) for n in ("T", "xh", "xl", "H", "hh", "hl", "Y", "y")}
            block = ctx.enter_context(nc.Block())

            def chunks(eng, body):
                with eng.Fori(0, NTURN - 1) as i:
                    for j in range(CB):
                        body(i * CB + j, i, j, False)
                for j in range(CB):
                    body((NTURN - 1) * CB + j, NTURN - 1, j, True)

            @block.sync
            def _(sp):
                def weights(e):
                    sp.wait_ge(s_wl, e)
                    sp.sem_inc(s_go, 1)
                    sp.dma_start(wi_r[:, :, :], wi[e].rearrange("(c p) f -> p c f", p=KC)).then_inc(s_w, 16)
                    sp.dma_start(wo_r[:, :, :], wo[e].rearrange("(c p) d -> p c d", p=128)).then_inc(s_w, 16)

                def rows(c, r):
                    sp.dma_start(xr[:, r, :, :], slot_x[bass.ds(c * CS, CS), :].rearrange("(p t) d -> p t d", p=128))\
                        .then_inc(s_x[r], 16)

                rows(0, 0)
                weights(0)
                for r in range(1, XR):
                    rows(r, r)
                weights(1)

                def body(c, i, j, last):
                    if not last or j + XR < CB:
                        sp.wait_ge(s["T"], at(c, 1, 1))
                        sp.sem_inc(s_go, 1)
                        rows(c + XR, j % XR)
                    sp.wait_ge(s["y"], at(c, 1, 1))
                    sp.sem_inc(s_go, 1)
                    sp.dma_start(slot_y[bass.ds(c * CS, CS), :].rearrange("(p t) d -> p t d", p=128),
                                 yr[:, j % 2, :, :]).then_inc(s_y[j % 2], 16)
                    if j % CE == CE - 1 and not last:
                        weights(i * 2 + (2 + j // CE))

                chunks(sp, body)
                for k in range(2):
                    sp.wait_ge(s_y[k], 16 * NTURN * CE)

            @block.tensor
            def _(pe):
                for n in ("T", "H", "Y"):
                    pe.sem_inc(s[n], CREDIT)

                def transposes(c, i, j):
                    pe.wait_ge(s_x[j % XR], i * (16 * CB // XR) + 16 * (j // XR + 1))
                    pe.wait_ge(s["xl"], at(c, 1, -1))
                    for t in range(CT):
                        for cc in range(KT):
                            ins = pe.transpose(pT[:, j % 2, cc, t * 128:(t + 1) * 128],
                                               xr[:, j % XR, t, cc * KC:(cc + 1) * KC], ident[:, :])
                    ins.then_inc(s["T"], 1)

                def hidden(c, i, j):
                    k = j // CE
                    if j % CE == 0:
                        pe.wait_ge(s_wl, i * 2 + (k + 1))
                    pe.wait_ge(s["xl"], at(c, 1, 1))
                    for q in range(3):
                        pe.wait_ge(s["hl"], at(c, 3, q - 2))
                        for f in (2 * q, 2 * q + 1):
                            for n, (cc, (a, b)) in enumerate((cc, ab) for cc in range(KT) for ab in PARTS):
                                ins = pe.matmul(pH[:, q, (f % 2) * CS:(f % 2 + 1) * CS],
                                                wi_s[a][:, k, cc, f * 128:(f + 1) * 128], xT[b][:, j % 2, cc, :],
                                                start=(n == 0), stop=(n == 3 * KT - 1))
                        ins.then_inc(s["H"], 1)

                def result(c, i, j):
                    pe.wait_ge(s["hl"], at(c, 3, 3))
                    pe.wait_ge(s["y"], at(c, 1, -1))
                    for t in range(CT):
                        for n, (f, (a, b)) in enumerate((f, ab) for f in range(FT) for ab in PARTS):
                            ins = pe.matmul(pY[:, j % 2, t * D:(t + 1) * D], hT[a][:, j % 2, f, t * 128:(t + 1) * 128],
                                            wo_s[b][:, j // CE, f, :], start=(n == 0), stop=(n == 3 * FT - 1))
                    ins.then_inc(s["Y"], 1)

                transposes(0, 0, 0)
                transposes(1, 0, 1)
                hidden(0, 0, 0)

                def body(c, i, j, last):
                    if not last or j + 2 < CB:
                        transposes(c + 2, i + (j + 2) // CB, (j + 2) % CB)
                    if not last or j + 1 < CB:
                        hidden(c + 1, i + (j + 1) // CB, (j + 1) % CB)
                    result(c, i, j)

                chunks(pe, body)

            @block.scalar
            def _(act):
                act.sem_inc(s["xh"], CREDIT)
                act.sem_inc(s["hh"], CREDIT)

                def split_weights(e, k):
                    act.wait_ge(s_w, e * 32 + 32)
                    act.sem_inc(s_go, 1)
                    nc.scalar.activation(wi_s[HI][:, k, :, :], wi_r[:, :, :], ACT.Copy)
                    nc.scalar.activation(wo_s[HI][:, k, :, :], wo_r[:, :, :], ACT.Copy).then_inc(s_wh, 1)

                def columns(c, i, j):
                    act.wait_ge(s["T"], at(c, 1, 1))
                    act.wait_ge(s["H"], at(c, 3, -3))
                    nc.scalar.activation(xT[HI][:, j % 2, :, :], pT[:, j % 2, :, :], ACT.Copy).then_inc(s["xh"], 1)

                def relu(c, i, j):
                    for q in range(3):
                        act.wait_ge(s["H"], at(c, 3, q + 1))
                        act.wait_ge(s["Y"], at(c, 1, -1))
                        nc.scalar.activation(hT[HI][:, j % 2, 2 * q:2 * q + 2, :], pH[:, q, :].rearrange(
                            "p (f n) -> p f n", f=2), ACT.Relu).then_inc(s["hh"], 1)

                split_weights(0, 0)
                columns(0, 0, 0)
                columns(1, 0, 1)
                relu(0, 0, 0)

                def body(c, i, j, last):
                    if not last or j + 2 < CB:
                        columns(c + 2, i + (j + 2) // CB, (j + 2) % CB)
                    if not last or j + 1 < CB:
                        relu(c + 1, i + (j + 1) // CB, (j + 1) % CB)
                    if j % CE == 1 and not (last and j > CE):
                        act.wait_ge(s["Y"], at(c, 1, -1))
                        split_weights(i * 2 + (j // CE + 1), 1 - j // CE)

                chunks(act, body)

            @block.gpsimd
            def _(pool):
                def split_weights(e, k):
                    pool.wait_ge(s_wh, e + 1)
                    nc.gpsimd.tensor_tensor(wi_s[LO][:, k, :, :], wi_r[:, :, :], wi_s[HI][:, k, :, :].bitcast(F32), ALU.subtract)
                    nc.gpsimd.tensor_tensor(wo_s[LO][:, k, :, :], wo_r[:, :, :], wo_s[HI][:, k, :, :].bitcast(F32), ALU.subtract)\
                        .then_inc(s_wl, 1)

                split_weights(0, 0)
                split_weights(1, 1)
                with pool.Fori(1, NTURN) as i:
                    for k in range(2):
                        split_weights(i * 2 + k, k)

            @block.vector
            def _(dve):
                for n in ("xl", "hl", "y"):
                    dve.sem_inc(s[n], CREDIT)

                def columns(c, i, j):
                    dve.wait_ge(s["xh"], at(c, 1, 1))
                    v.tensor_tensor(xT[LO][:, j % 2, :, :], pT[:, j % 2, :, :], xT[HI][:, j % 2, :, :].bitcast(F32),
                                    ALU.subtract).then_inc(s["xl"], 1)

                def relu(c, i, j):
                    for q in range(3):
                        dve.wait_ge(s["hh"], at(c, 3, q + 1))
                        part = slice(2 * q, 2 * q + 2)
                        v.scalar_tensor_tensor(hT[LO][:, j % 2, part, :], pH[:, q, :].rearrange("p (f n) -> p f n", f=2),
                                               0.0, hT[HI][:, j % 2, part, :].bitcast(F32), ALU.max, ALU.subtract)\
                            .then_inc(s["hl"], 1)

                columns(0, 0, 0)
                columns(1, 0, 1)
                relu(0, 0, 0)

                def body(c, i, j, last):
                    if not last or j + 2 < CB:
                        columns(c + 2, i + (j + 2) // CB, (j + 2) % CB)
                    if not last or j + 1 < CB:
                        relu(c + 1, i + (j + 1) // CB, (j + 1) % CB)
                    dve.wait_ge(s["Y"], at(c, 1, 1))
                    dve.wait_ge(s_y[j % 2], i * (16 * CE) + 16 * (j // 2))
                    v.tensor_copy(yr[:, j % 2, :, :], pY[:, j % 2, 0:CT * D].rearrange("p (t d) -> p t d", t=CT))\
                        .then_inc(s["y"], 1)

                chunks(dve, body)

        with ExitStack() as ctx:
            sem = semaphores(nc, ctx, "r_")
            GR = 4
            s_g = [sem(f"s_g{k}") for k in range(GR)]
            s_n = [sem(f"s_n{k}") for k in range(GR)]
            s_sum, s_out, s_go, s_at = sem("s_sum"), sem("s_out"), sem("s_go"), sem("s_at")
            at_ = ctx.enter_context(nc.sbuf_tensor("r_at", [TP, GR, TT], U32))
            got = ctx.enter_context(nc.sbuf_tensor("r_got", [TP, GR, TT, D], F32))
            block = ctx.enter_context(nc.Block())
            flat = lambda x, n: x[:, bass.ds(n, 1), :].rearrange("p a d -> p (a d)")

            @block.scalar
            def _(act):
                def body(c, i, k, left):
                    act.wait_ge(s_sum, at(c, 1, 1 - GR))
                    act.sem_inc(s_go, 1)
                    act.dma_start(got[:, k, :, :].rearrange("p t d -> p (t d)"), nrm_d[c]).then_inc(s_n[k], 16)

                turns(act, NB, GR, body)

            @block.gpsimd
            def _(pool):
                last_slot = pool.to_reg(SLOTS - 1)
                pool.sem_inc(s_go, 1)

                def body(c, i, k, left):
                    pool.wait_ge(s_n[k], i * 16 + 16)
                    pool.wait_ge(s_at, at(c, 1, 1))
                    pool.sem_inc(s_go, 1)
                    for t in range(TT):
                        pool.indirect_dma_start(got[:, k, t, :], None, slot_y,
                                                bass.IndirectOffsetOnAxis(ap=at_[:, k, t:t + 1], axis=0),
                                                bounds_check=last_slot, oob_is_err=False).then_inc(s_g[k], 16)

                turns(pool, NB, GR, body)

            @block.vector
            def _(dve):
                dve.sem_inc(s_sum, CREDIT)
                dve.sem_inc(s_at, CREDIT)
                dve.sem_inc(s_go, 1)
                def prepare(c, k):
                    v.tensor_copy(at_[:, k, :], dest[:, bass.ds(c * TT, TT)]).then_inc(s_at, 1)

                for k in range(GR):
                    prepare(k, k)

                def body(c, i, k, left):
                    dve.wait_ge(s_g[k], i * (16 * TT) + 16 * TT)
                    dve.sem_inc(s_go, 1)
                    for t in range(TT):
                        n = c * TT + t
                        ins = v.scalar_tensor_tensor(flat(base, n), got[:, k, t, :], prob[:, bass.ds(n, 1)], flat(base, n),
                                                     ALU.mult, ALU.add)
                    ins.then_inc(s_sum, 1)
                    if left >= GR:
                        dve.wait_ge(s_sum, at(c, 1, 1))
                        dve.sem_inc(s_go, 1)
                        prepare(c + GR, k)

                turns(dve, NB, GR, body)

            @block.sync
            def _(sp):
                def body(c, i, k, left):
                    sp.wait_ge(s_sum, at(c, 1, 1))
                    sp.sem_inc(s_go, 1)
                    sp.dma_start(out[c].rearrange("(t p) d -> p t d", p=TP), base[:, bass.ds(c * TT, TT), :])\
                        .then_inc(s_out, 16)

                turns(sp, NB, GR, body)
                sp.wait_ge(s_out, 16 * NB)


def trunk(nc, x, tok_gamma, tok_beta, tok_w, tok_b, ssm_lam, ssm_wd, ssm_bd, ssm_wb, ssm_wc, ssm_wout, ssm_bout,
          gate_w, gate_b, gate_bias, wu, bu, wg, bg, wd, bd, swu, sbu, swg, sbg, swd, sbd,
          w_qkv, b_qkv, w_proj, b_proj, ln_w, w_router, wi, wo, out):
    dram = lambda name, shape, dt=F32: nc.dram_tensor("dram_" + name, shape, dt, kind="Internal").ap()
    h0, h1, h2, h3 = (dram(f"h{n}", (T, D)) for n in range(4))
    token_selection(nc, x, tok_gamma, tok_beta, tok_w, tok_b, dram("score", (NB, N_IN)), h0)
    ssm(nc, h0, ssm_lam, ssm_wd, ssm_bd, ssm_wb, ssm_wc, ssm_wout, ssm_bout, dram("ct", (NB, 16, S)), h1)
    dense_experts(nc, h1, gate_w, gate_b, gate_bias, wu, bu, wg, bg, wd, bd, swu, sbu, swg, sbg, swd, sbd, h2)
    scratch = {
        "xn": dram("xn", (NB, TP, TT * D)), "xt": dram("xt", (NB, KC, KT * S), BF16),
        "v": dram("v", (NB, TP, TT * D)), "qk": dram("qk", (NB, 128, 6 * S), BF16),
        "vq": dram("vq", (NB, TP, TT * NHD * HP), BF16), "st": dram("st", (NB, TP, 2 * NHD * TT)),
        "o": dram("o", (NB, 128, 3 * S)),
    }
    attention(nc, h2, w_qkv, b_qkv, w_proj, b_proj, scratch, h3)
    slots = 16 * NB * 64
    switch_experts(nc, h3, ln_w, w_router, wi, wo, dram("slot_x", (slots, D)), dram("slot_y", (slots, D)),
                   dram("nrm", (NB, TP, TT * D)), out)


_INS = ['x', 'L0_tok_gamma', 'L0_tok_beta', 'L0_tok_w', 'L0_tok_b',
        'L0_attn_log_lambda', 'L0_attn_Wd', 'L0_attn_bd', 'L0_attn_WB', 'L0_attn_WC', 'L0_attn_Wout', 'L0_attn_bout',
        'L0_ffn_gate_w', 'L0_ffn_gate_b', 'L0_ffn_bias', 'L0_ffn_Wu', 'L0_ffn_bu', 'L0_ffn_Wg', 'L0_ffn_bg',
        'L0_ffn_Wd', 'L0_ffn_bd', 'L0_ffn_sWu', 'L0_ffn_sbu', 'L0_ffn_sWg', 'L0_ffn_sbg', 'L0_ffn_sWd', 'L0_ffn_sbd',
        'L1_attn_w_qkv', 'L1_attn_b_qkv', 'L1_attn_w_proj', 'L1_attn_b_proj',
        'L1_ffn_ln_w', 'L1_ffn_w_router', 'L1_ffn_wi', 'L1_ffn_wo']
_OUTS = [((NB, S, D), 'float32')]


def kernel(**inputs):
    import numpy as _np
    import concourse.bacc as _bacc
    from concourse import mybir as _mybir
    from concourse.bass_utils import run_bass_kernel_spmd as _run

    nc = _bacc.Bacc("TRN2", target_bir_lowering=False, num_devices=1)
    arrays, args = {}, []
    for name in _INS:
        a = _np.ascontiguousarray(inputs[name])
        arrays[f"in_{name}_dram"] = a
        args.append(nc.dram_tensor(f"in_{name}_dram", a.shape, _mybir.dt.from_np(a.dtype), kind="ExternalInput").ap())
    for i, (shape, dtype) in enumerate(_OUTS):
        dt = _mybir.dt.from_np(_np.dtype(dtype))
        args.append(nc.dram_tensor(f"out_{i}_dram", shape, dt, kind="ExternalOutput").ap())
    trunk(nc, *args)
    r = _run(nc, [arrays], core_ids=[0])
    return tuple(r.results[0][f"out_{i}_dram"] for i in range(len(_OUTS)))[0]
```
